# Optimizing a Trainium2 kernel written in Bass

```python
import numpy as np
import jax
import jax.numpy as jnp

def _softmax(x, axis=-1):
    return jax.nn.softmax(x, axis=axis)

def _gelu(x):
    return jax.nn.gelu(x, approximate=True)

def _silu(x):
    return jax.nn.silu(x)

def _sigmoid(x):
    return jax.nn.sigmoid(x)

def _layernorm(x, axis=-1, eps=1e-05):
    m = jnp.mean(x, axis=axis, keepdims=True)
    v = jnp.var(x, axis=axis, keepdims=True)
    return (x - m) / jnp.sqrt(v + eps)

def _scatter_add(tgt, idx, src, axis=0):
    return tgt.at[idx].add(src)

def _segment_sum(src, seg, n):
    return jax.ops.segment_sum(src, seg, n)
kernel_name = 'mk_decoder_preln_d1_seqx_r4_d37e57'

def setup_inputs(seed: int=0):
    np.random.seed(seed)
    _w = jnp.asarray

    def _rec_inputs():
        import jax
        import jax.numpy as jnp
        _rk = jax.random.key(seed)
        x = 7.22e-05 + 1 * jax.random.normal(jax.random.fold_in(_rk, 1), (4, 1024, 256), jnp.float32)
        _lenS = 1024 - jax.random.randint(jax.random.fold_in(_rk, 7), (4,), 0, max(1, 1024 // 4) + 1, jnp.int32)
        _lenS2 = 77 - jax.random.randint(jax.random.fold_in(_rk, 8), (4,), 0, max(1, 77 // 4) + 1, jnp.int32)
        _ctx_1024P = jax.random.normal(jax.random.fold_in(_rk, 11), (4, 16, 256), jnp.float32)
        _ctx_1024c = jax.random.dirichlet(jax.random.fold_in(_rk, 511), 0.3 * jnp.ones((16,), jnp.float32), (4, 77))
        _ctx_1024t = jnp.einsum('bsk,bkd->bsd', _ctx_1024c, _ctx_1024P)
        _ctx_1024t = _ctx_1024t * jax.lax.rsqrt(jnp.mean(jnp.square(_ctx_1024t)) + 1e-12) * 0.953939
        ctx_1024 = 4.13588e-05 + 0.999923 * (_ctx_1024t + 0.3 * jax.random.normal(jax.random.fold_in(_rk, 611), (4, 77, 256), jnp.float32))
        return (x, ctx_1024)
    x, ctx_1024 = _rec_inputs()

    def _L0_attn_setup():
        import jax, jax.numpy as jnp
        import numpy as np
        EPS = 1e-05

        def _forward(x, time_decay, time_first, W_key, W_value, W_output, W_shift, shift_gate, ln_w, ln_b):
            B, T, D = x.shape
            S = time_decay.shape[0]
            shift_len = max(1, int(T * 0.5))
            x_cat = jnp.concatenate([x[:, shift_len:], x[:, :-shift_len]], axis=1)
            gate = jax.nn.sigmoid(shift_gate)
            x_shift = jnp.einsum('btd,ed->bte', x_cat, W_shift) * gate + x * (1.0 - gate)
            mu = jnp.mean(x_shift, axis=-1, keepdims=True)
            var = jnp.mean(jnp.square(x_shift - mu), axis=-1, keepdims=True)
            xn = (x_shift - mu) * jax.lax.rsqrt(var + EPS) * ln_w + ln_b
            k = jnp.einsum('btd,sd->bts', xn, W_key)
            v = jnp.einsum('btd,sd->bts', xn, W_value)
            wkv = jnp.exp(-jnp.exp(time_first) * jax.nn.sigmoid(k)) * v
            w = jnp.exp(time_decay)

            def step(state, wkv_t):
                state = state * w + wkv_t
                return (state, state)
            init = jnp.zeros((B, S), dtype=x.dtype)
            last_state, states = jax.lax.scan(step, init, jnp.swapaxes(wkv, 0, 1))
            states = jnp.swapaxes(states, 0, 1)
            output = jnp.einsum('bts,ds->btd', states, W_output)
            return (output, last_state)

        def _reference_tuple_inner(x, time_decay, time_first, W_key, W_value, W_output, W_shift, shift_gate, ln_w, ln_b):
            out, last_state = _forward(x, time_decay, time_first, W_key, W_value, W_output, W_shift, shift_gate, ln_w, ln_b)
            return (out, jax.lax.stop_gradient(last_state))
        key = jax.random.key(seed)
        ks = jax.random.split(key, 8)
        B, T, D, S = (8, 1024, 256, 64)
        return {'x': jax.random.normal(ks[0], (B, T, D), dtype=jnp.float32), 'time_decay': jax.random.normal(ks[1], (S,), dtype=jnp.float32) * 0.1 - 0.5, 'time_first': jax.random.normal(ks[2], (S,), dtype=jnp.float32) * 0.1, 'W_key': jax.random.normal(ks[3], (S, D), dtype=jnp.float32) * 0.02, 'W_value': jax.random.normal(ks[4], (S, D), dtype=jnp.float32) * 0.02, 'W_output': jax.random.normal(ks[5], (D, S), dtype=jnp.float32) * 0.02, 'W_shift': jax.random.normal(ks[6], (D, D), dtype=jnp.float32) * 0.02, 'shift_gate': jnp.ones((D,), dtype=jnp.float32), 'ln_w': jnp.ones((D,), dtype=jnp.float32), 'ln_b': jnp.zeros((D,), dtype=jnp.float32)}
    _L0_attn_all = _L0_attn_setup()
    _L0_attn_in = {k: v for k, v in _L0_attn_all.items() if k in ('time_decay', 'time_first', 'W_key', 'W_value', 'W_output', 'W_shift', 'shift_gate', 'ln_w', 'ln_b')}
    del _L0_attn_all

    def _L0_xattn_setup():
        import jax, jax.numpy as jnp
        import numpy as np
        DIM = 256
        NUM_HEADS = 16
        HEAD_DIM = DIM // NUM_HEADS
        SCALE = HEAD_DIM ** (-0.5)
        key = jax.random.key(seed)
        ks = jax.random.split(key, 11)
        B, N = (4, 512)
        init = 1.0 / np.sqrt(DIM)
        return {'q': jax.random.normal(ks[0], (B, N, DIM), jnp.float32), 'k': jax.random.normal(ks[1], (B, N, DIM), jnp.float32), 'v': jax.random.normal(ks[2], (B, N, DIM), jnp.float32), 'wq': jax.random.normal(ks[3], (DIM, DIM), jnp.float32) * init, 'bq': jax.random.normal(ks[4], (DIM,), jnp.float32) * init, 'wk': jax.random.normal(ks[5], (DIM, DIM), jnp.float32) * init, 'bk': jax.random.normal(ks[6], (DIM,), jnp.float32) * init, 'wv': jax.random.normal(ks[7], (DIM, DIM), jnp.float32) * init, 'bv': jax.random.normal(ks[8], (DIM,), jnp.float32) * init, 'wo': jax.random.normal(ks[9], (DIM, DIM), jnp.float32) * init, 'bo': jax.random.normal(ks[10], (DIM,), jnp.float32) * init}
    _L0_xattn_all = _L0_xattn_setup()
    _L0_xattn_in = {k: v for k, v in _L0_xattn_all.items() if k in ('wq', 'bq', 'wk', 'bk', 'wv', 'bv', 'wo', 'bo')}
    del _L0_xattn_all

    def _L0_ffn_setup():
        import jax, jax.numpy as jnp
        import numpy as np
        B, S, H = (1, 256, 256)
        E = 256
        NEXP = 16
        TOPK = 2
        ALPHA = 1.702
        LIMIT = 7.0

        def _moe_forward(x, Wg, bg, Wgu, bgu, Wd, bd):
            b, s, h = x.shape
            xt = x.reshape(-1, h)
            logits = xt @ Wg.T + bg
            top_vals, top_idx = jax.lax.top_k(logits, TOPK)
            rw = jax.nn.softmax(top_vals.astype(jnp.float32), axis=-1).astype(xt.dtype)
            onehot = jax.nn.one_hot(top_idx, NEXP, dtype=xt.dtype)
            cw = jnp.einsum('tk,tke->te', rw, onehot)
            gu = jnp.einsum('th,ehf->tef', xt, Wgu) + bgu[None]
            gate = gu[..., ::2]
            up = gu[..., 1::2]
            gate = jnp.minimum(gate, LIMIT)
            up = jnp.clip(up, -LIMIT, LIMIT)
            glu = gate * jax.nn.sigmoid(gate * ALPHA)
            gated = (up + 1.0) * glu
            out_e = jnp.einsum('tef,efh->teh', gated, Wd) + bd[None]
            out = jnp.einsum('teh,te->th', out_e, cw)
            return out.reshape(b, s, h)
        key = jax.random.key(seed)
        ks = jax.random.split(key, 8)
        hidden_states = jax.random.normal(ks[0], (B, S, H), dtype=jnp.float32)
        Wg = jax.random.normal(ks[1], (NEXP, H), dtype=jnp.float32) / np.sqrt(H)
        bg = jax.random.normal(ks[2], (NEXP,), dtype=jnp.float32) * 0.01
        Wgu = jax.random.normal(ks[3], (NEXP, H, 2 * E), dtype=jnp.float32) / np.sqrt(H)
        bgu = jax.random.normal(ks[4], (NEXP, 2 * E), dtype=jnp.float32) * 0.01
        Wd = jax.random.normal(ks[5], (NEXP, E, H), dtype=jnp.float32) / np.sqrt(E)
        bd = jax.random.normal(ks[6], (NEXP, H), dtype=jnp.float32) * 0.01
        return {'hidden_states': hidden_states, 'Wg': Wg, 'bg': bg, 'Wgu': Wgu, 'bgu': bgu, 'Wd': Wd, 'bd': bd}
    _L0_ffn_all = _L0_ffn_setup()
    _L0_ffn_in = {k: v for k, v in _L0_ffn_all.items() if k in ('Wg', 'bg', 'Wgu', 'bgu', 'Wd', 'bd')}
    del _L0_ffn_all
    return {'x': x, 'ctx_1024': ctx_1024, 'L0_attn_time_decay': _L0_attn_in['time_decay'], 'L0_attn_time_first': _L0_attn_in['time_first'], 'L0_attn_W_key': _L0_attn_in['W_key'], 'L0_attn_W_value': _L0_attn_in['W_value'], 'L0_attn_W_output': _L0_attn_in['W_output'], 'L0_attn_W_shift': _L0_attn_in['W_shift'], 'L0_attn_shift_gate': _L0_attn_in['shift_gate'], 'L0_attn_ln_w': _L0_attn_in['ln_w'], 'L0_attn_ln_b': _L0_attn_in['ln_b'], 'L0_xattn_wq': _L0_xattn_in['wq'], 'L0_xattn_bq': _L0_xattn_in['bq'], 'L0_xattn_wk': _L0_xattn_in['wk'], 'L0_xattn_bk': _L0_xattn_in['bk'], 'L0_xattn_wv': _L0_xattn_in['wv'], 'L0_xattn_bv': _L0_xattn_in['bv'], 'L0_xattn_wo': _L0_xattn_in['wo'], 'L0_xattn_bo': _L0_xattn_in['bo'], 'L0_ffn_Wg': _L0_ffn_in['Wg'], 'L0_ffn_bg': _L0_ffn_in['bg'], 'L0_ffn_Wgu': _L0_ffn_in['Wgu'], 'L0_ffn_bgu': _L0_ffn_in['bgu'], 'L0_ffn_Wd': _L0_ffn_in['Wd'], 'L0_ffn_bd': _L0_ffn_in['bd']}

def reference(x, ctx_1024, L0_attn_time_decay, L0_attn_time_first, L0_attn_W_key, L0_attn_W_value, L0_attn_W_output, L0_attn_W_shift, L0_attn_shift_gate, L0_attn_ln_w, L0_attn_ln_b, L0_xattn_wq, L0_xattn_bq, L0_xattn_wk, L0_xattn_bk, L0_xattn_wv, L0_xattn_bv, L0_xattn_wo, L0_xattn_bo, L0_ffn_Wg, L0_ffn_bg, L0_ffn_Wgu, L0_ffn_bgu, L0_ffn_Wd, L0_ffn_bd):
    import jax
    import jax.numpy as jnp

    def _L0_attn_ref(x, time_decay, time_first, W_key, W_value, W_output, W_shift, shift_gate, ln_w, ln_b):
        import jax, jax.numpy as jnp
        import numpy as np
        EPS = 1e-05

        def _forward(x, time_decay, time_first, W_key, W_value, W_output, W_shift, shift_gate, ln_w, ln_b):
            B, T, D = x.shape
            S = time_decay.shape[0]
            shift_len = max(1, int(T * 0.5))
            x_cat = jnp.concatenate([x[:, shift_len:], x[:, :-shift_len]], axis=1)
            gate = jax.nn.sigmoid(shift_gate)
            x_shift = jnp.einsum('btd,ed->bte', x_cat, W_shift) * gate + x * (1.0 - gate)
            mu = jnp.mean(x_shift, axis=-1, keepdims=True)
            var = jnp.mean(jnp.square(x_shift - mu), axis=-1, keepdims=True)
            xn = (x_shift - mu) * jax.lax.rsqrt(var + EPS) * ln_w + ln_b
            k = jnp.einsum('btd,sd->bts', xn, W_key)
            v = jnp.einsum('btd,sd->bts', xn, W_value)
            wkv = jnp.exp(-jnp.exp(time_first) * jax.nn.sigmoid(k)) * v
            w = jnp.exp(time_decay)

            def step(state, wkv_t):
                state = state * w + wkv_t
                return (state, state)
            init = jnp.zeros((B, S), dtype=x.dtype)
            last_state, states = jax.lax.scan(step, init, jnp.swapaxes(wkv, 0, 1))
            states = jnp.swapaxes(states, 0, 1)
            output = jnp.einsum('bts,ds->btd', states, W_output)
            return (output, last_state)

        def _reference_tuple_inner(x, time_decay, time_first, W_key, W_value, W_output, W_shift, shift_gate, ln_w, ln_b):
            out, last_state = _forward(x, time_decay, time_first, W_key, W_value, W_output, W_shift, shift_gate, ln_w, ln_b)
            return (out, jax.lax.stop_gradient(last_state))
        return _reference_tuple_inner(x, time_decay, time_first, W_key, W_value, W_output, W_shift, shift_gate, ln_w, ln_b)[0]

    def _L0_xattn_ref(q, k, v, wq, bq, wk, bk, wv, bv, wo, bo):
        import jax, jax.numpy as jnp
        import numpy as np
        DIM = 256
        NUM_HEADS = 16
        HEAD_DIM = DIM // NUM_HEADS
        SCALE = HEAD_DIM ** (-0.5)
        B, Nq, C = q.shape
        Nk = k.shape[1]
        qh = (q @ wq.T + bq).reshape(B, Nq, NUM_HEADS, HEAD_DIM).transpose(0, 2, 1, 3)
        kh = (k @ wk.T + bk).reshape(B, Nk, NUM_HEADS, HEAD_DIM).transpose(0, 2, 1, 3)
        vh = (v @ wv.T + bv).reshape(B, Nk, NUM_HEADS, HEAD_DIM).transpose(0, 2, 1, 3)
        attn = jnp.einsum('bhqd,bhkd->bhqk', qh * SCALE, kh)
        attn = jax.nn.softmax(attn, axis=-1)
        out = jnp.einsum('bhqk,bhkd->bhqd', attn, vh)
        out = out.transpose(0, 2, 1, 3).reshape(B, Nq, C)
        return out @ wo.T + bo

    def _L0_ffn_ref(hidden_states, Wg, bg, Wgu, bgu, Wd, bd):
        import jax, jax.numpy as jnp
        import numpy as np
        B, S, H = (1, 256, 256)
        E = 256
        NEXP = 16
        TOPK = 2
        ALPHA = 1.702
        LIMIT = 7.0

        def _moe_forward(x, Wg, bg, Wgu, bgu, Wd, bd):
            b, s, h = x.shape
            xt = x.reshape(-1, h)
            logits = xt @ Wg.T + bg
            top_vals, top_idx = jax.lax.top_k(logits, TOPK)
            rw = jax.nn.softmax(top_vals.astype(jnp.float32), axis=-1).astype(xt.dtype)
            onehot = jax.nn.one_hot(top_idx, NEXP, dtype=xt.dtype)
            cw = jnp.einsum('tk,tke->te', rw, onehot)
            gu = jnp.einsum('th,ehf->tef', xt, Wgu) + bgu[None]
            gate = gu[..., ::2]
            up = gu[..., 1::2]
            gate = jnp.minimum(gate, LIMIT)
            up = jnp.clip(up, -LIMIT, LIMIT)
            glu = gate * jax.nn.sigmoid(gate * ALPHA)
            gated = (up + 1.0) * glu
            out_e = jnp.einsum('tef,efh->teh', gated, Wd) + bd[None]
            out = jnp.einsum('teh,te->th', out_e, cw)
            return out.reshape(b, s, h)
        return _moe_forward(hidden_states, Wg, bg, Wgu, bgu, Wd, bd)
    x = x + _L0_attn_ref(_layernorm(x, axis=-1), L0_attn_time_decay, L0_attn_time_first, L0_attn_W_key, L0_attn_W_value, L0_attn_W_output, L0_attn_W_shift, L0_attn_shift_gate, L0_attn_ln_w, L0_attn_ln_b)
    x = x + _L0_xattn_ref(_layernorm(x, axis=-1), ctx_1024, ctx_1024, L0_xattn_wq, L0_xattn_bq, L0_xattn_wk, L0_xattn_bk, L0_xattn_wv, L0_xattn_bv, L0_xattn_wo, L0_xattn_bo)
    x = x + _L0_ffn_ref(_layernorm(x, axis=-1), L0_ffn_Wg, L0_ffn_bg, L0_ffn_Wgu, L0_ffn_bgu, L0_ffn_Wd, L0_ffn_bd)
    return x

_drawn_inputs = setup_inputs


def setup_inputs(seed=0):
    import zlib

    import numpy as np

    out = dict(_drawn_inputs(seed))
    spreads = {'L0_attn_shift_gate': (1.0, 0.544), 'L0_attn_ln_w': (1.0, 0.2), 'L0_attn_ln_b': (0.0, 0.1)}
    factors = {'L0_attn_time_first': 3.561,
     'L0_xattn_bk': 64.0,
     'L0_ffn_bgu': 8.0,
     'L0_ffn_bd': 8.0,
     'L0_attn_W_key': 2.898}
    for name, (base, spread) in spreads.items():
        noise = np.random.default_rng([zlib.crc32(name.encode()), seed]).standard_normal(out[name].shape)
        drawn = base * np.exp(spread * noise) if base else spread * noise
        out[name] = jnp.asarray(drawn.astype(out[name].dtype))
    for name, factor in factors.items():
        out[name] = (out[name] * factor).astype(out[name].dtype)
    return out
```

```python
from contextlib import ExitStack

import concourse.bass as bass
from concourse import mybir

ALU = mybir.AluOpType
ACT = mybir.ActivationFunctionType
AX = mybir.AxisListType
F32 = mybir.dt.float32
F16 = mybir.dt.float16
I32 = mybir.dt.int32
U32 = mybir.dt.uint32
ds = bass.ds

P = 128
D = 256
DC = D // P
B, T, KEYS = 4, 1024, 77
NTOK = B * T
TILES = NTOK // P
TPB = T // P
SHIFT_TILES = TPB // 2
S = 64
HEADS, HD = 16, 16
HG = 8
GK = HG * KEYS
NCH = -(-GK // P)
LAST = GK - (NCH - 1) * P
GT = 4
GTOK = GT * P
GROUPS = TILES // GT
NEXP, TOPK, E = 16, 2, 256
F = 2 * E
CAP = NTOK + P
NSLOT = (TOPK * NTOK + NEXP * (P - 1)) // P
XS_ROWS = NEXP * CAP + P
ROW = D + 1
FAR = 1 << 20
EPS = 1e-5
XSC = 16.0
WSC = 16.0
GUS = XSC * WSC
ONE = 16.0
GDS = 2 * GUS
YS = GDS * WSC
ALPHA, LIMIT = 1.702, 7.0

_at = 0


def _cols(n):
    global _at
    _at += n
    return _at - n


C_WSH = _cols(DC * D)
C_GATE = _cols(D)
C_WKV = _cols(DC * 2 * S)
C_LNW, C_LNB = _cols(DC), _cols(DC)
C_TD, C_TF = _cols(1), _cols(1)
C_WOUT = _cols(D)
C_WQ = _cols(DC * D)
C_WO = _cols(DC * D)
C_BQ, C_BK = _cols(DC), _cols(DC)
C_BO = _cols(D)
C_WG = _cols(DC * NEXP)
C_BG = _cols(NEXP)
C_ALL = _at
Q_WK, Q_WV, Q_BV, Q_CTX = 0, DC * D, 2 * DC * D, 2 * DC * D + D
Q_ALL = Q_CTX + DC * B * KEYS
WEX = 2 * DC * F + 2 * DC * E
W_GUH, W_GUL, W_DH, W_DL = 0, DC * F, 2 * DC * F, 2 * DC * F + DC * E
WRAW = DC * F + DC * E


def build_decoder(nc, x, cst, kvc, wexp, bexp, out):
    xs_rows = nc.dram_tensor("xs_rows", (XS_ROWS, ROW), F32, kind="Internal").ap()
    y_rows = nc.dram_tensor("y_rows", (TOPK * NTOK, D), F32, kind="Internal").ap()
    v_flat = nc.dram_tensor("v_flat", (B, HEADS // HG, GK, HD), F32, kind="Internal").ap()

    ctx = ExitStack()
    with ctx:
        def sb(name, shape, dt):
            return ctx.enter_context(nc.sbuf_tensor(name, shape, dt))

        def sem(name):
            return ctx.enter_context(nc.semaphore(name))

        X = sb("X", [P, TILES, D], F32)
        W16 = sb("W16", [P, NEXP, WEX], F16)
        CST = sb("CST", [P, C_ALL], F32)
        KRAW = sb("KRAW", [P, 2, DC, B, KEYS], F16)
        KCUR = sb("KCUR", [P, DC, 2, HG, KEYS], F16)
        VFLAT = sb("VFLAT", [P, B, DC, NCH, HD], F32)
        VCUR = sb("VCUR", [P, DC, NCH, 2, 2, HD], F32)
        MV = sb("MV", [P, NCH, 2, 2, HD], F32)
        MK = sb("MK", [P, HG], F16)
        IND = sb("IND", [2 * HEADS, HEADS * KEYS], F16)
        ID32 = sb("ID32", [P, P], F32)
        ID16 = sb("ID16", [P, P], F16)
        UP16 = sb("UP16", [P, P], F16)
        ON16 = sb("ON16", [P, P], F16)
        BEX = sb("BEX", [2 * NEXP, F + E], F16)
        TOK = sb("TOK", [P, TILES], I32)
        IOTA = sb("IOTA", [P, NEXP], F32)
        RUN = sb("RUN", [P, GT + 1, NEXP], F32)
        ECAP = sb("ECAP", [P, NEXP], F32)
        RW = sb("RW", [P, TOPK, TILES], F32)
        HALF = sb("HALF", [P, TPB], F32)
        SMALL = sb("SMALL", [P, 16], F32)
        STG = sb("STG", [P, WRAW], F32)

        AR = sb("AR", [P, 9856], F32)

        def ar(at, n, dt=F32):
            v = AR[:, at:at + n]
            return v if dt == F32 else v.bitcast(dt)

        XN = ar(0, 16 * D).rearrange("p (k d) -> p k d", k=16)
        XNT = ar(4096, 16 * D).rearrange("p (c t) -> p c t", c=DC)
        XST = ar(4096, 16 * D).rearrange("p (h c t) -> p h c t", h=2, c=DC)
        TW = ar(8192, GTOK)
        ST = ar(8704, 2 * GTOK).rearrange("p (h t) -> p h t", h=2)
        PB = ar(0, NCH * GTOK).rearrange("p (n t) -> p n t", n=NCH)
        XQ = ar(2560, GT * D).rearrange("p (k d) -> p k d", k=GT)
        XQT = ar(3584, DC * GTOK).rearrange("p (c t) -> p c t", c=DC)
        QH = ar(4608, DC * GTOK // 2, F16).rearrange("p (c t) -> p c t", c=DC)
        QL = ar(5120, DC * GTOK // 2, F16).rearrange("p (c t) -> p c t", c=DC)
        AT = ar(5632, DC * GTOK).rearrange("p (c t) -> p c t", c=DC)
        X3 = ar(6656, GT * D).rearrange("p (k d) -> p k d", k=GT)
        X3T = ar(7680, DC * GTOK).rearrange("p (c t) -> p c t", c=DC)
        RB = ar(8704, 4 * ROW).rearrange("p (b k w) -> p b k w", b=2, k=2)
        RIN = ar(0, 2 * ROW).rearrange("p (b w) -> p b w", b=2)
        XTS = ar(514, 2 * D, F16).rearrange("p (b v t) -> p b v t", b=2, v=4)
        CG = ar(1026, 2 * E).rearrange("p (b e) -> p b e", b=2)
        CT = ar(1538, 2 * E).rearrange("p (b e) -> p b e", b=2)
        CU = ar(2050, 2 * E).rearrange("p (b e) -> p b e", b=2)
        CGD = ar(2562, 2 * E).rearrange("p (b e) -> p b e", b=2)
        GH = ar(3074, E, F16).rearrange("p (b c t) -> p b c t", b=2, c=DC)
        GL = ar(3330, E, F16).rearrange("p (b c t) -> p b c t", b=2, c=DC)
        CY = ar(3586, 2 * D).rearrange("p (b e) -> p b e", b=2)
        OHB = ar(4098, 2 * P, F16).rearrange("p (b k t) -> p b k t", b=2, k=2)
        PAD = ar(4354, ROW)
        OHT = ar(4611, P, F16)[:, 0:P]
        TAB = ar(4739, 2 * P, I32)
        RUNI = ar(4995, NEXP, I32)
        CW = ar(5014, 10 * NEXP).rearrange("p (a e) -> p a e", e=NEXP)
        CWI = ar(5014 + 10 * NEXP, NEXP, I32)
        NIX = ar(5014 + 11 * NEXP + NSLOT, 2, I32)
        CIX = ar(5014 + 11 * NEXP, NSLOT, I32)
        Y01 = W16[:, :, :].rearrange("p a b -> p (a b)").bitcast(F32)[:, 0:TOPK * TILES * D]\
            .rearrange("p (k i d) -> p k i d", k=TOPK, i=TILES)
        KVC = W16[:, NEXP - 2:NEXP, :].rearrange("p a b -> p (a b)").bitcast(F32)
        VSB = W16[:, NEXP - 3, :].bitcast(F32)[0:KEYS, 0:B * D].rearrange("p (b e) -> p b e", b=B)
        KTMP = W16[:, NEXP - 4, :].bitcast(F32)[:, 0:B * KEYS]
        BRAW = W16[:, NEXP - 5, :].bitcast(F32)

        STAT = sb("STAT", [P, 16, 6], F32)
        MVA = sb("MVA", [P, 16, 2], F32)
        RS = sb("RS", [P, 16], F32)
        STAT3 = sb("STAT3", [P, GT, 6], F32)
        MVA3 = sb("MVA3", [P, GT, 2], F32)
        RS3 = sb("RS3", [P, GT], F32)
        MX = sb("MX", [P, GT, HEADS], F32)
        MH = sb("MH", [P, GT, 2 * HEADS], F16)
        MT = sb("MT", [2 * HEADS, GTOK], F16)
        LG = sb("LG", [P, GT, NEXP], F32)
        M8 = sb("M8", [P, GT, 8], F32)
        I8 = sb("I8", [P, GT, 8], U32)
        IF = sb("IF", [P, GT, TOPK], F32)
        MS = sb("MS", [P, TOPK, GT, NEXP], F32)
        MS16 = sb("MS16", [P, GT, NEXP], F16)
        SL = sb("SL", [P, TOPK, GT, NEXP], F32)
        SLF = sb("SLF", [P, TOPK, GT], F32)
        SLOT = sb("SLOT", [P, TOPK, GT], I32)
        RD = sb("RD", [P, 3, GT], F32)

        def bank(i, n=1):
            return ctx.enter_context(nc.psum_tensor(f"bank{i}", [P, n * 512], F32))

        SC = [bank(0), bank(1)]
        MXP = bank(2, 2)
        NUM, DEN = bank(4), bank(5)
        WA, WB = bank(6), bank(7)
        WK = [WA, WB]
        MXB = MXP[:, :].rearrange("p (b n) -> p b n", b=2)
        TRA, SHA, KVA, OUA = [SC[0], SC[1]], [MXB[:, 0], MXB[:, 1]], [NUM, DEN], [WA, WB]
        XTP = [SC[0][:, 0:D].bitcast(F16), SC[1][:, 0:D].bitcast(F16)]
        GUP, GTP, YP = [MXB[:, 0], MXB[:, 1]], [NUM, DEN], [WA, WB]

        def cst_w(c0, n, c):
            return CST[:, c0 + c * n:c0 + (c + 1) * n]

        names = """sct0 sct1 rin0 rin1 ysc0 ysc1 cst_in x_in kvc_in bex_in v_sb v_out v_in w_split stg_in row_r
            dup_r consts_ready c_tab pad_r pads_in c_cp ct_mm cix_r f_r out_done consts1 w_hi w_scaled
            a_aggr a_eps a_rs wsh_done a_t1 a_xg a_aggr2 a_eps2 a_rs2 va2 ep2 rs2_r xq_r xb_r va3 ep3 rs3_r
            slot_r cy_r gate_tanh etf_exp k_mm small_ready k_hi a_kv a_xnt a_t2 a_sh a_xst kv_bias_ready
            a_scan a_tanh a_exp t_mm xqT_r q_mm qh_r mt_mm mT_r sc_mm pv_mm exp_r t3_mm x3T_r hi_r rd_s
            rd_e xn3_r a_x1 bex_ready cg_r ctanh_r ctg_mm cgh_r cd_mm v_mm kv_bias_mm wkv_ready k_ready
            a_xn a_xs a_xn2 a_wkv a_out lg_r kcur_r mx_r mx_mm mh_r ql_r vcur_r at_r run_s out_mm x2_r
            lg_mm ms_r px_mm c_tabe c_mm cxt_r cob_r cu_r cgu_mm cgd_r cgl_r cod_r wsh_ready k_tmp bex_s
            a_stat a_stat2 st2 mh_s rec_s st3 top_r ix_r if_r ms_s rd_r pos_s sl_s slf_s ct1_r f_s y_in0
            y_in1 y_in2 y_in3 nix_r sp_past pool_past dve_past""".split()
        s = {n: sem(n) for n in names}
        SCT = [s["sct0"], s["sct1"]]
        RINS = [s["rin0"], s["rin1"]]
        YSC = [s["ysc0"], s["ysc1"]]
        YIN = [s[f"y_in{i}"] for i in range(4)]

        block = ctx.enter_context(nc.Block())
        HALF_TILES = [[bb * TPB + SHIFT_TILES * h + j for bb in range(2) for j in range(SHIFT_TILES)]
                      for h in range(2)]
        ORDER = HALF_TILES[0] + HALF_TILES[1]
        x_t = x.rearrange("(i p) d -> p i d", p=P)
        out_t = out.rearrange("(i p) d -> p i d", p=P)

        @block.sync
        def _(sp):
            sp.dma_start(CST[:, :], cst).then_inc(s["cst_in"], 16)
            for p in range(2):
                if p:
                    sp.wait_ge(s["x_in"], 32)
                for q in range(2):
                    i = 16 * p + 8 * q
                    sp.dma_start(X[:, i:i + 8, :], x_t[:, i:i + 8, :]).then_inc(s["x_in"], 16)
                if p == 0:
                    sp.dma_start(KVC[:, 0:Q_ALL], kvc).then_inc(s["kvc_in"], 16)
                    sp.dma_start(BRAW[0:2 * NEXP, 0:F + E], bexp).then_inc(s["bex_in"], 16)
            sp.wait_ge(s["v_sb"], B)
            for b in range(B):
                for m in range(DC):
                    sp.dma_start(v_flat[b, m].rearrange("(h k) e -> k h e", k=KEYS),
                                 VSB[:, b, m * P:(m + 1) * P].rearrange("p (h e) -> p h e", h=HG))\
                        .then_inc(s["v_out"], 16)
            sp.wait_ge(s["v_out"], 16 * B * DC)
            for b in range(B):
                for m in range(DC):
                    sp.dma_start(VFLAT[:, b, m, 0:NCH - 1, :],
                                 v_flat[b, m, 0:(NCH - 1) * P, :].rearrange("(n p) e -> p n e", p=P))\
                        .then_inc(s["v_in"], 16)
                    sp.dma_start(VFLAT[0:LAST, b, m, NCH - 1, :], v_flat[b, m, (NCH - 1) * P:GK, :])\
                        .then_inc(s["v_in"], 16)

            def wload(e, first=False):
                if not first:
                    sp.wait_ge(s["w_split"], e)
                sp.dma_start(STG[:, :], wexp[ds(e, 1)].rearrange("a p n -> (a p) n")).then_inc(s["stg_in"], 16)

            def dup(g, j, first=False):
                sp.wait_ge(s["row_r"], g * GT + j + 1).then_inc(s["sp_past"], 1)
                if not first:
                    sp.wait_ge(s["dup_r"], g * (16 * GT) + 16 * j)
                sp.dma_start(RB[:, j % 2, 1, 0:D], RB[:, j % 2, 0, 0:D]).then_inc(s["dup_r"], 16)

            def group(g, first=False):
                wload(g * 2 + 2)
                dup(g, 0, first)
                dup(g, 1)
                wload(g * 2 + 3)
                dup(g, 2)
                dup(g, 3)

            sp.wait_ge(s["consts_ready"], 1)
            wload(0, True)
            wload(1)
            group(0, True)
            with sp.Fori(1, GROUPS - 1) as g:
                group(g)
            for j in range(GT):
                dup(GROUPS - 1, j)

            sp.wait_ge(s["c_tab"], 1)
            sp.wait_ge(s["pad_r"], 2)
            with sp.Fori(0, NEXP) as e:
                r = sp.value_load(RUNI[0:1, ds(e, 1)], min_val=0, max_val=XS_ROWS - P)
                sp.dma_start(xs_rows[ds(r, P), :], PAD).then_inc(s["pads_in"], 16)
            sp.dma_start(xs_rows[NEXP * CAP:XS_ROWS, :], PAD).then_inc(s["pads_in"], 16)
            sp.wait_ge(s["pads_in"], 16 * (NEXP + 1))
            for q in range(2):
                sp.wait_ge(SCT[q], 32 * TILES // 2)
            sp.wait_ge(s["c_cp"], 2)

            def load(n, q, first=False):
                r = sp.value_load(TAB[0:1, ds(P + n, 1)], min_val=0, max_val=XS_ROWS - P)
                if not first:
                    sp.wait_ge(s["ct_mm"], n - 1)
                    sp.wait_ge(s["cix_r"], n - 1)
                sp.dma_start(RIN[:, q, :], xs_rows[ds(r, P), :]).then_inc(RINS[q], 16)

            load(0, 0, True)
            load(1, 1, True)
            load(2, 0)
            with sp.Fori(0, (NSLOT - 3) // 2) as t:
                load(t * 2 + 3, 1)
                load(t * 2 + 4, 0)

            for q in range(2):
                sp.wait_ge(YSC[q], 16 * ((NSLOT + 1 - q) // 2))
            y_t = y_rows.rearrange("(k i p) d -> p k i d", k=TOPK, p=P)
            for c in range(4):
                for k in range(TOPK):
                    sp.dma_start(Y01[:, k, 8 * c:8 * c + 8, :], y_t[:, k, 8 * c:8 * c + 8, :])\
                        .then_inc(YIN[c], 16)
            for c in range(4):
                sp.wait_ge(s["f_r"], 8 * (c + 1))
                sp.dma_start(out_t[:, 8 * c:8 * c + 8, :], X[:, 8 * c:8 * c + 8, :]).then_inc(s["out_done"], 16)
            sp.wait_ge(s["out_done"], 64)

        @block.gpsimd
        def _(pool):
            n1 = [0]

            def c1(ins):
                n1[0] += 1
                ins.then_inc(s["consts1"], 1)

            def sel(v, op, base, pattern, cm, fill=0.0):
                pool.wait_ge(s["consts1"], n1[0])
                c1(pool.affine_select(out=v, in_=v, compare_op=op, fill=fill, base=base, pattern=pattern,
                                      channel_multiplier=cm))

            c1(pool.memset(HALF[:, :], -0.5))
            for m in (ID32, ID16):
                c1(pool.memset(m[:, :], 0.0))
                sel(m[:, :], ALU.not_equal, 0, [[-1, P]], 1, 1.0)
            c1(pool.memset(MK[:, :], 1.0))
            sel(MK[:, :], ALU.is_ge, 0, [[-HD, HG]], 1)
            sel(MK[:, :], ALU.is_ge, HD - 1, [[HD, HG]], -1)
            c1(pool.memset(MV[:, :, :, :, :].rearrange("p a b c d -> p (a b c d)"), 1.0))
            for v in range(2):
                pat = [[P - 2 * KEYS, NCH], [-KEYS, 2], [0, HD]]
                sel(MV[:, :, v], ALU.is_ge, 2 * KEYS * v, pat, 1)
                sel(MV[:, :, v], ALU.is_ge, (KEYS - 1) - 2 * KEYS * v, [[-a, n] for a, n in pat], -1)
            ind2 = STG[0:2 * HEADS, 0:HEADS * KEYS // 2].bitcast(F16)
            for v, base in ((IND[:, :], 0), (ind2, KEYS * HEADS)):
                c1(pool.memset(v, 1.0))
                sel(v, ALU.is_ge, base, [[1, HEADS * KEYS]], -KEYS)
                sel(v, ALU.is_ge, (KEYS - 1) - base, [[-1, HEADS * KEYS]], KEYS)
            pool.wait_ge(s["consts1"], n1[0])
            c1(pool.tensor_tensor(IND[:, :], IND[:, :], ind2, ALU.add))
            c1(pool.memset(ON16[:, :], 1.0))
            c1(pool.memset(UP16[:, :], 1.0))
            sel(UP16[:, :], ALU.is_gt, 0, [[1, P]], -1)
            c1(pool.iota(TOK[:, :], [[P, TILES]], base=0, channel_multiplier=1))
            c1(pool.iota(STG[:, 0:NEXP].bitcast(I32), [[1, NEXP]], base=0, channel_multiplier=0))
            pool.wait_ge(s["consts1"], n1[0])
            c1(pool.tensor_copy(IOTA[:, :], STG[:, 0:NEXP].bitcast(I32)))
            pool.wait_ge(s["consts1"], n1[0])
            c1(pool.tensor_scalar(ECAP[:, :], IOTA[:, :], float(CAP), 0.0, ALU.mult, ALU.add))
            pool.wait_ge(s["consts1"], n1[0])
            pool.tensor_copy(RUN[:, 0, :], ECAP[:, :]).then_inc(s["consts_ready"], 1)

            def root(var, eps_sem, rs_sem, rs, n, k, scale):
                pool.tensor_scalar(rs, var, EPS, 1.0 / (scale * scale), ALU.add, ALU.mult).then_inc(eps_sem, 1)
                pool.wait_ge(eps_sem, k)
                pool.tensor_tensor(rs, rs, HALF[:, 0:n], ALU.pow).then_inc(rs_sem, 1)

            def split(e):
                pool.wait_ge(s["stg_in"], 16 * (e + 1)).then_inc(s["pool_past"], 1)
                pool.wait_ge(s["w_hi"], e + 1).then_inc(s["pool_past"], 1)
                pool.tensor_scalar(STG[:, :], STG[:, :], WSC, 0.0, ALU.mult, ALU.add).then_inc(s["w_scaled"], 1)
                pool.wait_ge(s["w_scaled"], e + 1)
                pool.tensor_tensor(W16[:, e, W_GUL:W_DH], STG[:, 0:DC * F], W16[:, e, W_GUH:W_GUL], ALU.subtract)
                pool.tensor_tensor(W16[:, e, W_DL:WEX], STG[:, DC * F:WRAW], W16[:, e, W_DH:W_DL], ALU.subtract)\
                    .then_inc(s["w_split"], 1)

            for p in range(2):
                for q in range(2):
                    pool.wait_ge(s["a_aggr"], 2 * p + q + 1)
                    root(MVA[:, 8 * q:8 * q + 8, 1], s["a_eps"], s["a_rs"], RS[:, 8 * q:8 * q + 8], 8, 2 * p + q + 1, 1.0)
                pool.wait_ge(s["wsh_done"], 1)
                for k in ORDER:
                    pool.wait_ge(s["a_t1"], 16 * p + k + 1)
                    pool.tensor_tensor(XN[:, k, :], XN[:, k, :], CST[:, C_GATE:C_GATE + D], ALU.mult)\
                        .then_inc(s["a_xg"], 1)
                for q in range(2):
                    pool.wait_ge(s["a_aggr2"], 2 * p + q + 1)
                    root(MVA[:, 8 * q:8 * q + 8, 1], s["a_eps2"], s["a_rs2"], RS[:, 8 * q:8 * q + 8], 8, 2 * p + q + 1, 1.0)

            def root2(g):
                pool.wait_ge(s["va2"], g + 1).then_inc(s["pool_past"], 1)
                root(MVA[:, 0:GT, 1], s["ep2"], s["rs2_r"], RS[:, 0:GT], GT, g + 1, 1.0)

            def add_bo(g):
                pool.wait_ge(s["xq_r"], 2 * g + 2)
                for j in range(GT):
                    xt = X[:, ds(g * GT + j, 1), :].rearrange("p a d -> p (a d)")
                    ins = pool.tensor_tensor(xt, xt, CST[:, C_BO:C_BO + D], ALU.add)
                ins.then_inc(s["xb_r"], 1)

            def root3(g):
                pool.wait_ge(s["va3"], g + 1).then_inc(s["pool_past"], 1)
                root(MVA3[:, :, 1], s["ep3"], s["rs3_r"], RS3[:, :], GT, g + 1, XSC)

            def scatter(g):
                pool.wait_ge(s["slot_r"], g + 1)
                for j in range(GT):
                    for k in range(TOPK):
                        if k == 0:
                            pool.wait_ge(s["row_r"], g * GT + j + 1).then_inc(s["pool_past"], 1)
                        else:
                            pool.wait_ge(s["dup_r"], 16 * (g * GT + j + 1)).then_inc(s["pool_past"], 1)
                        pool.indirect_dma_start(
                            xs_rows, bass.IndirectOffsetOnAxis(ap=SLOT[:, k, j:j + 1], axis=0),
                            RB[:, j % 2, k, :], None, bounds_check=XS_ROWS - 1, oob_is_err=True)\
                            .then_inc(SCT[j % 2], 16)

            root2(0)
            add_bo(0)
            split(0)
            root2(1)
            add_bo(1)
            split(1)
            with pool.Fori(1, GROUPS - 1) as g:
                root3(g - 1)
                root2(g + 1)
                add_bo(g + 1)
                split(g * 2)
                scatter(g - 1)
                split(g * 2 + 1)
            root3(GROUPS - 2)
            split(2 * GROUPS - 2)
            scatter(GROUPS - 2)
            root3(GROUPS - 1)
            split(2 * GROUPS - 1)
            scatter(GROUPS - 1)

            pool.memset(PAD, 0.0).then_inc(s["pad_r"], 1)
            pool.wait_ge(s["pad_r"], 1)
            pool.memset(PAD[:, D:ROW].bitcast(I32), FAR).then_inc(s["pad_r"], 1)

            def y_index(n, q, t):
                pool.wait_ge(RINS[q], 16 * (t + 1)).then_inc(s["pool_past"], 1)
                pool.tensor_copy(CIX[:, ds(n, 1)], RIN[:, q, D:ROW].bitcast(I32)).then_inc(s["cix_r"], 1)

            def y_scatter(n, q, t, first=False):
                if not first:
                    pool.wait_ge(YSC[q], 16 * t).then_inc(s["pool_past"], 1)
                pool.wait_ge(s["cix_r"], n + 1).then_inc(s["pool_past"], 1)
                pool.tensor_copy(NIX[:, q:q + 1], CIX[:, ds(n, 1)]).then_inc(s["nix_r"], 1)
                pool.wait_ge(s["cy_r"], n + 1).then_inc(s["pool_past"], 1)
                pool.wait_ge(s["nix_r"], n + 1).then_inc(s["pool_past"], 1)
                pool.indirect_dma_start(
                    y_rows, bass.IndirectOffsetOnAxis(ap=NIX[:, q:q + 1], axis=0), CY[:, q, :], None,
                    bounds_check=TOPK * NTOK - 1, oob_is_err=False).then_inc(YSC[q], 16)

            y_index(0, 0, 0)
            y_index(1, 1, 0)
            y_index(2, 0, 1)
            y_index(3, 1, 1)
            y_scatter(0, 0, 0, True)
            y_index(4, 0, 2)
            y_scatter(1, 1, 0, True)
            with pool.Fori(1, (NSLOT - 3) // 2) as t:
                y_index(t * 2 + 3, 1, t + 1)
                y_scatter(t * 2, 0, t)
                y_index(t * 2 + 4, 0, t + 2)
                y_scatter(t * 2 + 1, 1, t)
            for n in range(NSLOT - 3, NSLOT):
                y_scatter(n, n % 2, n // 2)

        @block.scalar
        def _(act):
            act.wait_ge(s["cst_in"], 16)
            act.activation(CST[:, C_GATE:C_GATE + D], CST[:, C_GATE:C_GATE + D], ACT.Tanh, scale=0.5)\
                .then_inc(s["gate_tanh"], 1)
            act.activation(SMALL[:, 0:1], CST[:, C_TD:C_TD + 1], ACT.Exp).then_inc(s["etf_exp"], 1)
            act.activation(SMALL[:, 1:2], CST[:, C_TF:C_TF + 1], ACT.Exp).then_inc(s["etf_exp"], 1)
            for m in range(DC):
                act.wait_ge(s["k_mm"], m + 1)
                act.wait_ge(s["small_ready"], 1)
                act.activation(KRAW[:, 0, m].rearrange("p b k -> p (b k)"), WK[m][:, 0:B * KEYS], ACT.Identity,
                               scale=0.25, bias=SMALL[:, 2 + m:3 + m]).then_inc(s["k_hi"], 1)

            for p in range(2):
                for k in range(16):
                    act.wait_ge(s["a_t1"], 16 * p + k + 1)
                    if p:
                        act.wait_ge(s["a_kv"], 2 * p)
                    act.activation(XNT[:, :, k * P:(k + 1) * P],
                                   TRA[k % 2][:, 0:D].rearrange("p (c t) -> p c t", c=DC), ACT.Copy)\
                        .then_inc(s["a_xnt"], 1)
                for h in range(2):
                    for k in range(8):
                        act.wait_ge(s["a_t2"], 16 * p + 8 * h + k + 1)
                        act.wait_ge(s["a_sh"], 16 * (p + 1))
                        act.activation(XST[:, h, :, k * P:(k + 1) * P],
                                       TRA[k % 2][:, 0:D].rearrange("p (c t) -> p c t", c=DC), ACT.Copy)\
                            .then_inc(s["a_xst"], 1)
                    act.wait_ge(s["a_kv"], 2 * p + h + 1)
                    act.wait_ge(s["kv_bias_ready"], 1)
                    if p or h:
                        act.wait_ge(s["a_scan"], 2 * p + h)
                    act.activation(TW, KVA[0][:, :], ACT.Tanh, scale=0.5, bias=SMALL[:, 5:6])\
                        .then_inc(s["a_tanh"], 1)
                    act.wait_ge(s["a_tanh"], 2 * p + h + 1)
                    act.activation(TW, TW, ACT.Exp, scale=SMALL[:, 4:5], bias=SMALL[:, 4:5])\
                        .then_inc(s["a_exp"], 1)

            def whi(e):
                act.wait_ge(s["stg_in"], 16 * (e + 1))
                act.activation(W16[:, e, W_GUH:W_GUL], STG[:, 0:DC * F], ACT.Copy, scale=WSC)
                act.activation(W16[:, e, W_DH:W_DL], STG[:, DC * F:WRAW], ACT.Copy, scale=WSC)\
                    .then_inc(s["w_hi"], 1)

            def evac_t(g):
                for r in range(2):
                    act.wait_ge(s["t_mm"], 2 * g + r + 1)
                    act.activation(XQT[:, :, 2 * r * P:2 * (r + 1) * P],
                                   WK[1 - r][:, :].rearrange("p (j c t) -> p c j t", j=2, c=DC),
                                   ACT.Copy).then_inc(s["xqT_r"], 1)

            def evac_q(g):
                for m in range(DC):
                    act.wait_ge(s["q_mm"], 2 * g + m + 1)
                    act.activation(QH[:, m], WK[1 - m][:, :], ACT.Identity, bias=CST[:, C_BQ + m:C_BQ + m + 1])\
                        .then_inc(s["qh_r"], 1)

            def evac_m(g):
                act.wait_ge(s["mt_mm"], g + 1)
                act.activation(MT[:, :], WA[0:2 * HEADS, 0:GTOK // 2].bitcast(F16), ACT.Copy)\
                    .then_inc(s["mT_r"], 1)

            def exps(g, m, first=False):
                for c in range(NCH):
                    rows = P if c < NCH - 1 else LAST
                    act.wait_ge(s["sc_mm"], g * (2 * NCH) + m * NCH + c + 1)
                    if not first:
                        act.wait_ge(s["pv_mm"], 2 * g + m)
                    act.activation(PB[0:rows, c, :], SC[(m * NCH + c) % 2][0:rows, :], ACT.Exp)\
                        .then_inc(s["exp_r"], 1)

            def evac_t3(g):
                for r in range(2):
                    act.wait_ge(s["t3_mm"], 2 * g + r + 1)
                    act.activation(X3T[:, :, 2 * r * P:2 * (r + 1) * P],
                                   WK[r][:, :].rearrange("p (j c t) -> p c j t", j=2, c=DC),
                                   ACT.Copy).then_inc(s["x3T_r"], 1)

            def row_hi(g, j, early=False):
                if not early:
                    act.wait_ge(SCT[j % 2], g * 64 + 32 * (j // 2))
                act.activation(RB[:, j % 2, 0, 0:D // 2].bitcast(F16), X3[:, j, :], ACT.Copy)\
                    .then_inc(s["hi_r"], 1)

            def pair_exp(g):
                act.wait_ge(s["rd_s"], g + 1)
                act.activation(RD[:, 1, :], RD[:, 0, :], ACT.Exp).then_inc(s["rd_e"], 1)

            def s3_act(g, first=False):
                act.wait_ge(s["xn3_r"], 4 * g + 4)
                for j in range(GT):
                    row_hi(g, j, first and j < 2)

            def body(g, part3, part1, first=False):
                exps(g, 0, first)
                if part3:
                    evac_t3(g - 1)
                exps(g, 1)
                if part3:
                    pair_exp(g - 1)
                if part1:
                    evac_t(g + 1)
                    evac_q(g + 1)
                    evac_m(g + 1)
                if part3:
                    s3_act(g - 1, part3 == 2)

            act.wait_ge(s["a_x1"], 16)
            evac_t(0)
            evac_q(0)
            evac_m(0)
            act.wait_ge(s["v_in"], 32 * B * DC)
            act.wait_ge(s["bex_ready"], 1)
            whi(0)
            body(0, 0, True, True)
            whi(1)
            whi(2)
            body(1, 2, True)
            whi(3)
            with act.Fori(2, GROUPS - 1) as g:
                whi(g * 2)
                body(g, 1, True)
                whi(g * 2 + 1)
            whi(2 * GROUPS - 2)
            body(GROUPS - 1, 1, False)
            whi(2 * GROUPS - 1)
            evac_t3(GROUPS - 1)
            pair_exp(GROUPS - 1)
            s3_act(GROUPS - 1)

            def c_tanh(n, q):
                act.wait_ge(s["cg_r"], n + 1)
                act.activation(CT[:, q], CG[:, q], ACT.Tanh, scale=ALPHA / 2).then_inc(s["ctanh_r"], 1)

            def c_gh(n, q):
                act.wait_ge(s["ctg_mm"], n + 1)
                act.activation(GH[:, q].rearrange("p c t -> p (c t)"), GTP[q][:, 0:E], ACT.Copy)\
                    .then_inc(s["cgh_r"], 1)

            def c_y(n, q, t, first=False):
                act.wait_ge(s["cd_mm"], n + 1)
                if not first:
                    act.wait_ge(YSC[q], 16 * t)
                act.activation(CY[:, q], YP[q][:, 0:D], ACT.Copy, scale=1.0 / YS).then_inc(s["cy_r"], 1)

            act.wait_ge(s["pad_r"], 2)
            c_tanh(0, 0)
            c_tanh(1, 1)
            c_gh(0, 0)
            c_tanh(2, 0)
            c_gh(1, 1)
            c_y(0, 0, 0, True)
            c_tanh(3, 1)
            c_gh(2, 0)
            c_y(1, 1, 0, True)
            with act.Fori(0, (NSLOT - 5) // 2) as t:
                c_tanh(t * 2 + 4, 0)
                c_gh(t * 2 + 3, 1)
                c_y(t * 2 + 2, 0, t + 1)
                c_tanh(t * 2 + 5, 1)
                c_gh(t * 2 + 4, 0)
                c_y(t * 2 + 3, 1, t + 1)
            c_tanh(NSLOT - 1, 0)
            c_gh(NSLOT - 2, 1)
            c_y(NSLOT - 3, 0, (NSLOT - 3) // 2)
            c_gh(NSLOT - 1, 0)
            c_y(NSLOT - 2, 1, (NSLOT - 3) // 2)
            c_y(NSLOT - 1, 0, (NSLOT - 1) // 2)

        @block.tensor
        def _(pe):
            pe.wait_ge(s["consts_ready"], 1)
            pe.wait_ge(s["cst_in"], 16)
            pe.wait_ge(s["kvc_in"], 16)
            for m in range(DC):
                for c in range(DC):
                    mm = pe.matmul(WK[m][:, 0:B * KEYS], KVC[:, Q_WK + c * D + m * P:Q_WK + c * D + (m + 1) * P],
                                   KVC[:, Q_CTX + c * B * KEYS:Q_CTX + (c + 1) * B * KEYS],
                                   start=(c == 0), stop=(c == DC - 1))
                mm.then_inc(s["k_mm"], 1)
            for kv in range(2):
                for hh in range(2):
                    for c in range(DC):
                        mm = pe.matmul(MXB[S * hh:S * hh + S, 0, kv:kv + 1],
                                       CST[:, C_WKV + c * 2 * S + kv * S:C_WKV + c * 2 * S + kv * S + S],
                                       CST[:, C_LNB + c:C_LNB + c + 1], start=(c == 0), stop=(c == DC - 1))
            mm.then_inc(s["kv_bias_mm"], 1)
            for b in range(B):
                v = [NUM, DEN][b % 2]
                if b >= 2:
                    pe.wait_ge(s["v_sb"], b - 1)
                for c in range(DC):
                    at = Q_CTX + c * B * KEYS + b * KEYS
                    mm = pe.matmul(v[0:KEYS, 0:D], KVC[:, at:at + KEYS], KVC[:, Q_WV + c * D:Q_WV + (c + 1) * D],
                                   start=(c == 0), stop=(c == DC - 1))
                mm.then_inc(s["v_mm"], 1)

            pe.wait_ge(s["kv_bias_ready"], 1)
            pe.wait_ge(s["v_sb"], B)
            pe.wait_ge(s["wkv_ready"], 1)
            pe.wait_ge(s["k_ready"], DC)
            pe.wait_ge(s["wsh_done"], 1)
            for p in range(2):
                for k in range(16):
                    pe.wait_ge(s["a_xn"], 16 * p + k + 1)
                    if k >= 2:
                        pe.wait_ge(s["a_xnt"], 16 * p + k - 1)
                    elif p:
                        pe.wait_ge(s["a_xst"], 16 * p)
                    for c in range(DC):
                        mm = pe.transpose(TRA[k % 2][:, c * P:(c + 1) * P], XN[:, k, c * P:(c + 1) * P], ID32[:, :])
                    mm.then_inc(s["a_t1"], 1)
                pe.wait_ge(s["a_xnt"], 16 * (p + 1))
                for n, k in enumerate(ORDER):
                    o = k // TPB * TPB + (k + SHIFT_TILES) % TPB
                    if n >= 2 or p:
                        pe.wait_ge(s["a_xs"], 16 * p + n - 1)
                    for c in range(DC):
                        mm = pe.matmul(SHA[n % 2][:, 0:D], XNT[:, c, o * P:(o + 1) * P], cst_w(C_WSH, D, c),
                                       start=(c == 0), stop=(c == DC - 1))
                    mm.then_inc(s["a_sh"], 1)
                for h in range(2):
                    for n, k in enumerate(HALF_TILES[h]):
                        pe.wait_ge(s["a_xn2"], 16 * p + 8 * h + n + 1)
                        if 8 * h + n >= 2:
                            pe.wait_ge(s["a_xst"], 16 * p + 8 * h + n - 1)
                        for c in range(DC):
                            mm = pe.transpose(TRA[n % 2][:, c * P:(c + 1) * P], XN[:, k, c * P:(c + 1) * P],
                                              ID32[:, :])
                        mm.then_inc(s["a_t2"], 1)
                    pe.wait_ge(s["a_xst"], 16 * p + 8 * (h + 1))
                    if p or h:
                        pe.wait_ge(s["a_wkv"], 2 * p + h)
                        pe.wait_ge(s["a_tanh"], 2 * p + h)
                    for kv in range(2):
                        for c in range(DC):
                            for bb in range(2):
                                mm = pe.matmul(KVA[kv][S * bb:S * bb + S, :],
                                               CST[:, C_WKV + c * 2 * S + kv * S:C_WKV + c * 2 * S + kv * S + S],
                                               XST[:, h, c, bb * GTOK:(bb + 1) * GTOK],
                                               start=(c == 0), stop=(c == DC - 1))
                    mm.then_inc(s["a_kv"], 1)
                for h in range(2):
                    pe.wait_ge(s["a_scan"], 2 * p + h + 1)
                    for r in range(4):
                        u = 8 * p + 4 * h + r
                        bb = r // 2
                        if u >= 2:
                            pe.wait_ge(s["a_x1"], u - 1)
                        for q in range(2):
                            t0 = (2 * (r % 2) + q) * P
                            mm = pe.matmul(OUA[r % 2][:, q * D:(q + 1) * D], ST[S * bb:S * bb + S, h, t0:t0 + P],
                                           CST[S * bb:S * bb + S, C_WOUT:C_WOUT + D], start=True, stop=True)
                        mm.then_inc(s["a_out"], 1)

            def turn(src, ready, per_bank, g, banks, mm_sem):
                for r in range(2):
                    pe.wait_ge(ready, g * (2 * per_bank) + per_bank * (r + 1))
                    for j in range(2):
                        for c in range(DC):
                            at = (j * DC + c) * P
                            mm = pe.transpose(banks[r][:, at:at + P], src[:, 2 * r + j, c * P:(c + 1) * P], ID32[:, :])
                    mm.then_inc(mm_sem, 1)

            def s1_turn(g, after3):
                if after3:
                    pe.wait_ge(s["x3T_r"], 2 * (g - 1))
                    pe.wait_ge(s["lg_r"], g - 1)
                turn(XQ, s["xq_r"], 1, g, [WB, WA], s["t_mm"])

            def s1_q(g):
                pe.wait_ge(s["xqT_r"], 2 * g + 2)
                for m in range(DC):
                    for c in range(DC):
                        mm = pe.matmul(WK[1 - m][:, :], CST[:, C_WQ + c * D + m * P:C_WQ + c * D + (m + 1) * P],
                                       XQT[:, c, :], start=(c == 0), stop=(c == DC - 1))
                    mm.then_inc(s["q_mm"], 1)

            def s1_max(g, b, j, first=False):
                if j == 0:
                    pe.wait_ge(s["qh_r"], 2 * g + 2)
                    pe.wait_ge(s["kcur_r"], b + 1)
                for m in range(DC):
                    if not (first and j == 0 and m == 0):
                        pe.wait_ge(s["mx_r"], 8 * g + 2 * j + m)
                    for half in range(2):
                        mm = pe.matmul(MXB[:, half, 0:GK // 2], QH[:, m, j * P:(j + 1) * P],
                                       KCUR[:, m, 0, 4 * half:4 * half + 4].rearrange("p h k -> p (h k)"),
                                       start=True, stop=True)
                    mm.then_inc(s["mx_mm"], 1)

            def s1_mt(g):
                pe.wait_ge(s["mh_r"], g + 1)
                for j in range(GT):
                    mm = pe.transpose(WA[0:2 * HEADS, j * P // 2:(j + 1) * P // 2].bitcast(F16), MH[:, j, :],
                                      ID16[:, :])
                mm.then_inc(s["mt_mm"], 1)

            def s2_scores(g, m, first=False):
                if m == 0:
                    pe.wait_ge(s["mT_r"], g + 1)
                    pe.wait_ge(s["ql_r"], 2 * g + 2)
                for c in range(NCH):
                    rows = P if c < NCH - 1 else LAST
                    if not (first and m == 0 and c < 2):
                        pe.wait_ge(s["exp_r"], g * (2 * NCH) + m * NCH + c - 1)
                    o = SC[(m * NCH + c) % 2][0:rows, :]
                    kh = KCUR[:, m, 0].rearrange("p h k -> p (h k)")[:, c * P:c * P + rows]
                    kl = KCUR[:, m, 1].rearrange("p h k -> p (h k)")[:, c * P:c * P + rows]
                    ind = IND[:, m * GK + c * P:m * GK + c * P + rows]
                    pe.matmul(o, ind, MT[:, :], start=True, stop=False)
                    pe.matmul(o, kh, QL[:, m], start=False, stop=False)
                    pe.matmul(o, kl, QH[:, m], start=False, stop=False)
                    pe.matmul(o, kh, QH[:, m], start=False, stop=True).then_inc(s["sc_mm"], 1)

            def s2_pv(g, b, m, first=False):
                pe.wait_ge(s["exp_r"], g * (2 * NCH) + (m + 1) * NCH)
                if m == 0:
                    pe.wait_ge(s["vcur_r"], b + 1)
                if not (first and m == 0):
                    pe.wait_ge(s["at_r"], 2 * g + m)
                for o, w in ((NUM, VCUR[:, m]), (DEN, MV)):
                    for v in range(2):
                        for j in range(4):
                            rows = P if j + v < NCH - 1 else LAST
                            mm = pe.matmul(o[32 * j:32 * j + 32, :],
                                           w[0:rows, j + v, v].rearrange("p a e -> p (a e)"),
                                           PB[0:rows, j + v, :], start=(v == 0), stop=(v == 1))
                mm.then_inc(s["pv_mm"], 1)

            def s2_out(g, j, after3):
                if j == 0:
                    pe.wait_ge(s["at_r"], 2 * g + 2)
                if j == 2 and after3:
                    pe.wait_ge(s["run_s"], 5 * g)
                for c in range(DC):
                    mm = pe.matmul(WK[j // 2][:, (j % 2) * D:(j % 2 + 1) * D], AT[:, c, j * P:(j + 1) * P],
                                   cst_w(C_WO, D, c), start=(c == 0), stop=(c == DC - 1))
                mm.then_inc(s["out_mm"], 1)

            def s3_turn(g):
                pe.wait_ge(s["x2_r"], 2 * (g + 1))
                turn(X3, s["xn3_r"], 2, g, [WA, WB], s["t3_mm"])

            def s3_logits(g):
                pe.wait_ge(s["x3T_r"], 2 * g + 2)
                for j in range(GT):
                    for c in range(DC):
                        mm = pe.matmul(WA[:, j * NEXP:(j + 1) * NEXP], X3T[:, c, j * P:(j + 1) * P],
                                       cst_w(C_WG, NEXP, c), start=(c == 0), stop=(c == DC - 1))
                mm.then_inc(s["lg_mm"], 1)

            def s3_prefix(g):
                pe.wait_ge(s["ms_r"], g + 1)
                ms = MS16[:, :, :].rearrange("p j e -> p (j e)")
                pe.matmul(WB[:, 0:GT * NEXP], UP16[:, :], ms, start=True, stop=True)
                pe.matmul(WB[:, GT * NEXP:2 * GT * NEXP], ON16[:, :], ms, start=True, stop=True)\
                    .then_inc(s["px_mm"], 1)

            def body(g, b, b1, part3, part1, first=False):
                s2_scores(g, 0, first)
                if part3:
                    s3_turn(g - 1)
                s2_pv(g, b, 0, first)
                s2_scores(g, 1)
                if part3:
                    s3_logits(g - 1)
                if part1:
                    s1_turn(g + 1, part3)
                s2_pv(g, b, 1)
                if part1:
                    s1_q(g + 1)
                if part3:
                    if part1:
                        pe.wait_ge(s["ql_r"], 2 * (g + 1) + 1)
                    s3_prefix(g - 1)
                for j in range(GT):
                    if part1:
                        s1_max(g + 1, b1, j)
                        if j == 0:
                            pe.wait_ge(s["ql_r"], 2 * (g + 1) + 2)
                    elif j == 0:
                        pe.wait_ge(s["lg_r"], g)
                    s2_out(g, j, part3)
                if part1:
                    pe.wait_ge(s["x2_r"], 2 * g + 1)
                    s1_mt(g + 1)

            pe.wait_ge(s["a_x1"], 16)
            s1_turn(0, False)
            s1_q(0)
            for j in range(GT):
                s1_max(0, 0, j, True)
            pe.wait_ge(s["ql_r"], 2)
            s1_mt(0)
            body(0, 0, 0, False, True, True)
            with pe.Fori(0, (GROUPS - 2) // 2) as t:
                body(t * 2 + 1, t, t + 1, True, True)
                body(t * 2 + 2, t + 1, t + 1, True, True)
            body(GROUPS - 1, B - 1, None, True, False)
            s3_turn(GROUPS - 1)
            s3_logits(GROUPS - 1)
            s3_prefix(GROUPS - 1)

            pe.wait_ge(s["c_tabe"], 18)
            pe.wait_ge(s["run_s"], 5 * GROUPS)
            pe.transpose(WA[0:1, 0:P], CW[:, 0, 0:1], ID32[:, :])
            pe.transpose(WA[0:1, P:2 * P], CW[:, 0, 1:2], ID32[:, :]).then_inc(s["c_mm"], 1)
            pe.transpose(WB[0:2 * NEXP, 0:P], CW[:, 8:10].rearrange("p a e -> p (a e)"), ID32[:, :])\
                .then_inc(s["c_mm"], 1)
            pe.wait_ge(s["c_cp"], 2)
            pe.wait_ge(s["w_split"], NEXP)
            pe.wait_ge(s["bex_ready"], 1)

            def c_turn(n, q, t):
                pe.wait_ge(RINS[q], 16 * (t + 1))
                if not isinstance(n, int) or n >= 2:
                    pe.wait_ge(s["cxt_r"], n - 1)
                rows = RIN[:, q, 0:D].bitcast(F16)
                for v in range(4):
                    mm = pe.transpose(XTP[q][:, v * P:(v + 1) * P], rows[:, v * P:(v + 1) * P], ID16[:, :])
                mm.then_inc(s["ct_mm"], 1)

            w_flat = W16[:, :, :].rearrange("p e w -> p (e w)")

            def w_at(e, at, n):
                return w_flat[:, ds(e * WEX + at, n)]

            def expert(n):
                return pe.value_load(TAB[0:1, ds(n, 1)], min_val=0, max_val=NEXP - 1)

            def c_gu(n, q):
                e = expert(n)
                pe.wait_ge(s["cob_r"], n + 1)
                if not isinstance(n, int) or n >= 2:
                    pe.wait_ge(s["cu_r"], n - 1)
                    pe.wait_ge(s["cg_r"], n - 1)
                pe.matmul(GUP[q], OHB[0:2 * NEXP, q, 0], BEX[:, 0:F], start=True, stop=False)
                pe.wait_ge(s["cxt_r"], n + 1)
                for c in range(DC):
                    pe.matmul(GUP[q], XTS[:, q, c], w_at(e, W_GUL + c * F, F), start=False, stop=False)
                    pe.matmul(GUP[q], XTS[:, q, c], w_at(e, W_GUH + c * F, F), start=False, stop=False)
                for c in range(DC):
                    mm = pe.matmul(GUP[q], XTS[:, q, 2 + c], w_at(e, W_GUH + c * F, F), start=False,
                                   stop=(c == DC - 1))
                mm.then_inc(s["cgu_mm"], 1)

            def c_tg(n, q):
                pe.wait_ge(s["cgd_r"], n + 1)
                if not isinstance(n, int) or n >= 2:
                    pe.wait_ge(s["cgl_r"], n - 1)
                for c in range(DC):
                    mm = pe.transpose(GTP[q][:, c * P:(c + 1) * P], CGD[:, q, c * P:(c + 1) * P], ID32[:, :])
                mm.then_inc(s["ctg_mm"], 1)

            def c_down(n, q):
                e = expert(n)
                pe.wait_ge(s["cod_r"], n + 1)
                if not isinstance(n, int) or n >= 2:
                    pe.wait_ge(s["cy_r"], n - 1)
                pe.matmul(YP[q][:, 0:D], OHB[0:2 * NEXP, q, 1], BEX[:, F:F + E], start=True, stop=False)
                pe.wait_ge(s["cgl_r"], n + 1)
                for c in range(DC):
                    pe.matmul(YP[q][:, 0:D], GH[:, q, c], w_at(e, W_DL + c * E, E), start=False, stop=False)
                    pe.matmul(YP[q][:, 0:D], GH[:, q, c], w_at(e, W_DH + c * E, E), start=False, stop=False)
                for c in range(DC):
                    mm = pe.matmul(YP[q][:, 0:D], GL[:, q, c], w_at(e, W_DH + c * E, E), start=False,
                                   stop=(c == DC - 1))
                mm.then_inc(s["cd_mm"], 1)

            c_turn(0, 0, 0)
            c_turn(1, 1, 0)
            c_gu(0, 0)
            c_turn(2, 0, 1)
            c_gu(1, 1)
            c_tg(0, 0)

            def steps(t):
                c_turn(t * 2 + 3, 1, t + 1)
                c_gu(t * 2 + 2, 0)
                c_tg(t * 2 + 1, 1)
                c_down(t * 2, 0)
                c_turn(t * 2 + 4, 0, t + 2)
                c_gu(t * 2 + 3, 1)
                c_tg(t * 2 + 2, 0)
                c_down(t * 2 + 1, 1)

            steps(0)
            with pe.Fori(1, (NSLOT - 3) // 2) as t:
                steps(t)
            c_gu(NSLOT - 1, 0)
            c_tg(NSLOT - 2, 1)
            c_down(NSLOT - 3, 0)
            c_tg(NSLOT - 1, 0)
            c_down(NSLOT - 2, 1)
            c_down(NSLOT - 1, 0)

        @block.vector
        def _(dve):
            dve.wait_ge(s["gate_tanh"], 1)
            gate = CST[:, C_GATE:C_GATE + D]
            for c in range(DC):
                w = cst_w(C_WSH, D, c)
                dve.scalar_tensor_tensor(out=w, in0=gate, scalar=1.0, in1=w, op0=ALU.add, op1=ALU.mult)\
                    .then_inc(s["wsh_ready"], 1)
            dve.wait_ge(s["wsh_ready"], 2)
            for c in range(DC):
                w = cst_w(C_WSH, D, c)
                dve.tensor_scalar(w, w, 0.5, None, ALU.mult)
            dve.tensor_scalar(gate, gate, -0.5, 0.5, ALU.mult, ALU.add).then_inc(s["wsh_done"], 1)
            dve.wait_ge(s["etf_exp"], 2)
            dve.tensor_scalar(SMALL[:, 2:4], CST[:, C_BK:C_BK + DC], 0.25, None, ALU.mult)
            dve.tensor_scalar(SMALL[:, 4:5], SMALL[:, 1:2], -0.5, None, ALU.mult).then_inc(s["small_ready"], 1)
            dve.wait_ge(s["small_ready"], 1)
            dve.wait_ge(s["kv_bias_mm"], 1)
            dve.tensor_scalar(SMALL[:, 5:6], MXB[:, 0, 0:1], 0.5, None, ALU.mult)
            dve.tensor_copy(SMALL[:, 6:7], MXB[:, 0, 1:2]).then_inc(s["kv_bias_ready"], 1)
            for c in range(DC):
                w = cst_w(C_WKV, 2 * S, c)
                ins = dve.tensor_scalar(w, w, CST[:, C_LNW + c:C_LNW + c + 1], None, ALU.mult)
            ins.then_inc(s["wkv_ready"], 1)
            for b in range(B):
                dve.wait_ge(s["v_mm"], b + 1)
                v = [NUM, DEN][b % 2]
                dve.tensor_tensor(VSB[:, b], v[0:KEYS, 0:D], KVC[0:KEYS, Q_BV:Q_BV + D], ALU.add)\
                    .then_inc(s["v_sb"], 1)
            for m in range(DC):
                dve.wait_ge(s["k_hi"], m + 1)
                if m:
                    dve.wait_ge(s["k_ready"], m)
                dve.tensor_scalar(KTMP, WK[m][:, 0:B * KEYS], 0.25, SMALL[:, 2 + m:3 + m], ALU.mult, ALU.add)\
                    .then_inc(s["k_tmp"], 1)
                dve.wait_ge(s["k_tmp"], m + 1)
                dve.tensor_tensor(KRAW[:, 1, m].rearrange("p b k -> p (b k)"), KTMP,
                                  KRAW[:, 0, m].rearrange("p b k -> p (b k)"), ALU.subtract).then_inc(s["k_ready"], 1)
            dve.wait_ge(s["bex_in"], 16)
            br = BRAW[0:2 * NEXP, 0:F + E]
            dve.tensor_scalar(br[:, 0:F], br[:, 0:F], GUS / ONE, None, ALU.mult)
            dve.tensor_scalar(br[:, F:F + E], br[:, F:F + E], YS / ONE, None, ALU.mult).then_inc(s["bex_s"], 1)
            dve.wait_ge(s["bex_s"], 1)
            dve.tensor_copy(BEX[:, :], br).then_inc(s["bex_s"], 1)
            dve.wait_ge(s["bex_s"], 2)
            dve.tensor_tensor(br, br, BEX[:, :], ALU.subtract).then_inc(s["bex_s"], 1)
            dve.wait_ge(s["bex_s"], 3)
            dve.wait_ge(s["consts_ready"], 1)
            mhi, mlo = SMALL[0:2 * NEXP, 8:9], SMALL[0:2 * NEXP, 9:10]
            dve.tensor_copy(mhi, MK[0:2 * NEXP, 0:1])
            dve.tensor_copy(mlo, MK[0:2 * NEXP, 1:2]).then_inc(s["bex_s"], 1)
            dve.wait_ge(s["bex_s"], 4)
            dve.tensor_scalar(br, br, mlo, None, ALU.mult).then_inc(s["bex_s"], 1)
            dve.wait_ge(s["bex_s"], 5)
            dve.scalar_tensor_tensor(out=BEX[:, :], in0=BEX[:, :], scalar=mhi, in1=br, op0=ALU.mult, op1=ALU.add)\
                .then_inc(s["bex_ready"], 1)
            dve.wait_ge(s["k_ready"], DC)

            def kcur(b):
                for m in range(DC):
                    for v in range(2):
                        k = KRAW[:, v, m, ds(b, 1), :].broadcast_to([P, HG, KEYS])
                        ins = dve.tensor_tensor(KCUR[:, m, v], k,
                                                MK[:, :].unsqueeze(2).broadcast_to([P, HG, KEYS]), ALU.mult)
                ins.then_inc(s["kcur_r"], 1)

            def vcur(b):
                for m in range(DC):
                    for n in range(2):
                        rows, c0, c1 = (P, 0, NCH - 1) if n == 0 else (LAST, NCH - 1, NCH)
                        vf = VFLAT[0:rows, ds(b, 1), m, c0:c1, :].rearrange("p a n e -> p (a n) e")
                        nn = c1 - c0
                        ins = dve.tensor_tensor(
                            VCUR[0:rows, m, c0:c1].rearrange("p n v a e -> p n (v a) e"),
                            vf.unsqueeze(2).broadcast_to([rows, nn, 4, HD]),
                            MV[0:rows, c0:c1].rearrange("p n v a e -> p n (v a) e"), ALU.mult)
                ins.then_inc(s["vcur_r"], 1)

            for p in range(2):
                dve.wait_ge(s["x_in"], 32 * (p + 1))
                if p:
                    dve.wait_ge(s["a_rs2"], 2 * p)
                for q in range(2):
                    for k in range(8 * q, 8 * q + 8):
                        ins = dve.bn_stats(STAT[:, k, :], X[:, 16 * p + k, :])
                    ins.then_inc(s["a_stat"], 1)
                for q in range(2):
                    dve.wait_ge(s["a_stat"], 2 * p + q + 1)
                    for k in range(8 * q, 8 * q + 8):
                        ins = dve.bn_aggr(MVA[:, k, :], STAT[:, k, :])
                    ins.then_inc(s["a_aggr"], 1)
                if p:
                    dve.wait_ge(s["a_t2"], 16 * p)
                for q in range(2):
                    dve.wait_ge(s["a_rs"], 2 * p + q + 1)
                    for k in range(8 * q, 8 * q + 8):
                        dve.tensor_scalar(XN[:, k, :], X[:, 16 * p + k, :], MVA[:, k, 0:1], RS[:, k:k + 1],
                                          ALU.subtract, ALU.mult).then_inc(s["a_xn"], 1)
                for h in range(2):
                    for n, k in enumerate(HALF_TILES[h]):
                        u = 16 * p + 8 * h + n
                        dve.wait_ge(s["a_sh"], u + 1)
                        dve.wait_ge(s["a_xg"], u + 1)
                        dve.tensor_tensor(XN[:, k, :], XN[:, k, :], SHA[n % 2][:, 0:D], ALU.add)\
                            .then_inc(s["a_xs"], 1)
                        if n:
                            dve.wait_ge(s["a_xs"], u)
                            dve.bn_stats(STAT[:, 8 * h + n - 1, :], XN[:, HALF_TILES[h][n - 1], :])
                    dve.wait_ge(s["a_xs"], 16 * p + 8 * h + 8)
                    dve.bn_stats(STAT[:, 8 * h + 7, :], XN[:, HALF_TILES[h][7], :]).then_inc(s["a_stat2"], 1)
                    dve.wait_ge(s["a_stat2"], 2 * p + h + 1)
                    for n in range(8 * h, 8 * h + 8):
                        ins = dve.bn_aggr(MVA[:, n, :], STAT[:, n, :])
                    ins.then_inc(s["a_aggr2"], 1)
                for h in range(2):
                    dve.wait_ge(s["a_rs2"], 2 * p + h + 1)
                    for n, k in enumerate(HALF_TILES[h]):
                        dve.tensor_scalar(XN[:, k, :], XN[:, k, :], MVA[:, 8 * h + n, 0:1],
                                          RS[:, 8 * h + n:8 * h + n + 1], ALU.subtract, ALU.mult)\
                            .then_inc(s["a_xn2"], 1)
                for h in range(2):
                    dve.wait_ge(s["a_exp"], 2 * p + h + 1)
                    dve.scalar_tensor_tensor(out=TW, in0=KVA[1][:, :], scalar=SMALL[:, 6:7], in1=TW,
                                             op0=ALU.add, op1=ALU.mult).then_inc(s["a_wkv"], 1)
                    dve.wait_ge(s["a_wkv"], 2 * p + h + 1)
                    if p:
                        dve.wait_ge(s["a_out"], 4 * (2 * p + h - 1))
                    if h:
                        dve.wait_ge(s["a_scan"], 2 * p + 1)
                    dve.tensor_tensor_scan(ST[:, h, :], SMALL[:, 0:1].broadcast_to([P, GTOK]), TW,
                                           ST[:, 0, GTOK - 1:GTOK] if h else 0.0, ALU.mult, ALU.add)\
                        .then_inc(s["a_scan"], 1)
                for h in range(2):
                    for r in range(4):
                        u = 8 * p + 4 * h + r
                        i = 16 * p + (r // 2) * TPB + 4 * h + 2 * (r % 2)
                        dve.wait_ge(s["a_out"], u + 1)
                        xt = X[:, i:i + 2, :].rearrange("p a d -> p (a d)")
                        ins = dve.tensor_tensor(xt, xt, OUA[r % 2][:, :], ALU.add).then_inc(s["a_x1"], 1)
            dve.wait_ge(s["a_x1"], 16)
            dve.wait_ge(s["v_in"], 32 * B * DC)

            def s1_stats(g):
                for j in range(GT):
                    ins = dve.bn_stats(STAT[:, j, :], X[:, ds(g * GT + j, 1), :].rearrange("p a d -> p (a d)"))
                ins.then_inc(s["st2"], 1)
                dve.wait_ge(s["st2"], g + 1).then_inc(s["dve_past"], 1)
                for j in range(GT):
                    ins = dve.bn_aggr(MVA[:, j, :], STAT[:, j, :])
                ins.then_inc(s["va2"], 1)

            def s1_norm(g, first=False):
                dve.wait_ge(s["rs2_r"], g + 1)
                if not first:
                    dve.wait_ge(s["t_mm"], 2 * g)
                for j in range(GT):
                    ins = dve.tensor_scalar(XQ[:, j, :], X[:, ds(g * GT + j, 1), :].rearrange("p a d -> p (a d)"),
                                            MVA[:, j, 0:1], RS[:, j:j + 1], ALU.subtract, ALU.mult)
                    if j % 2:
                        ins.then_inc(s["xq_r"], 1)

            def s1_ql(g):
                for m in range(DC):
                    dve.wait_ge(s["qh_r"], 2 * g + m + 1)
                    dve.scalar_tensor_tensor(out=QL[:, m], in0=WK[1 - m][:, :], scalar=CST[:, C_BQ + m:C_BQ + m + 1],
                                             in1=QH[:, m], op0=ALU.add, op1=ALU.subtract).then_inc(s["ql_r"], 1)

            def s1_max(g, j):
                for m in range(DC):
                    dve.wait_ge(s["mx_mm"], 8 * g + 2 * j + m + 1)
                    dve.tensor_reduce(MX[:, j, m * HG:(m + 1) * HG].rearrange("p (a h) -> p a h", a=2),
                                      MXB[:, :, 0:GK // 2].rearrange("p a (h k) -> p a h k", k=KEYS),
                                      AX.X, ALU.max).then_inc(s["mx_r"], 1)

            def s1_mh(g):
                dve.wait_ge(s["mx_r"], 8 * g + 8)
                dve.tensor_scalar(MH[:, :, 0:HEADS], MX[:, :, :], -1.0, None, ALU.mult).then_inc(s["mh_s"], 1)
                dve.wait_ge(s["mh_s"], g + 1)
                dve.scalar_tensor_tensor(out=MH[:, :, HEADS:2 * HEADS], in0=MX[:, :, :], scalar=-1.0,
                                         in1=MH[:, :, 0:HEADS], op0=ALU.mult, op1=ALU.subtract)\
                    .then_inc(s["mh_r"], 1)

            def s2_attn(g, m):
                dve.wait_ge(s["pv_mm"], 2 * g + m + 1)
                dve.reciprocal(AT[:, m], DEN[:, :]).then_inc(s["rec_s"], 1)
                dve.wait_ge(s["rec_s"], 2 * g + m + 1)
                dve.tensor_tensor(AT[:, m], AT[:, m], NUM[:, :], ALU.mult).then_inc(s["at_r"], 1)

            def s2_x2(g, r):
                dve.wait_ge(s["out_mm"], 4 * g + 2 * r + 2)
                if r == 0:
                    dve.wait_ge(s["xb_r"], g + 1)
                xt = X[:, ds(g * GT + 2 * r, 2), :].rearrange("p a d -> p (a d)")
                dve.tensor_tensor(xt, xt, WK[r][:, :], ALU.add).then_inc(s["x2_r"], 1)

            def s3_stats(g):
                dve.wait_ge(s["x2_r"], 2 * g + 2).then_inc(s["dve_past"], 1)
                for j in range(GT):
                    ins = dve.bn_stats(STAT3[:, j, :], X[:, ds(g * GT + j, 1), :].rearrange("p a d -> p (a d)"))
                ins.then_inc(s["st3"], 1)
                dve.wait_ge(s["st3"], g + 1).then_inc(s["dve_past"], 1)
                for j in range(GT):
                    ins = dve.bn_aggr(MVA3[:, j, :], STAT3[:, j, :])
                ins.then_inc(s["va3"], 1)

            def s3_norm(g, first=False):
                dve.wait_ge(s["rs3_r"], g + 1)
                if not first:
                    dve.wait_ge(s["t3_mm"], 2 * g)
                    dve.wait_ge(s["hi_r"], 4 * g)
                for j in range(GT):
                    dve.tensor_scalar(X3[:, j, :], X[:, ds(g * GT + j, 1), :].rearrange("p a d -> p (a d)"),
                                      MVA3[:, j, 0:1], RS3[:, j:j + 1], ALU.subtract, ALU.mult)\
                        .then_inc(s["xn3_r"], 1)

            def s3_logits(g, first=False):
                dve.wait_ge(s["lg_mm"], g + 1)
                dve.scalar_tensor_tensor(
                    out=LG[:, :, :], in0=WA[:, 0:GT * NEXP].rearrange("p (j e) -> p j e", j=GT), scalar=1.0 / XSC,
                    in1=CST[:, C_BG:C_BG + NEXP].unsqueeze(1).broadcast_to([P, GT, NEXP]),
                    op0=ALU.mult, op1=ALU.add).then_inc(s["lg_r"], 1)
                dve.wait_ge(s["lg_r"], g + 1).then_inc(s["dve_past"], 1)
                if not first:
                    dve.wait_ge(s["rd_e"], g).then_inc(s["dve_past"], 1)
                for j in range(GT):
                    ins = dve.max(M8[:, j, :], LG[:, j, :])
                ins.then_inc(s["top_r"], 1)
                dve.wait_ge(s["top_r"], g + 1)
                dve.tensor_tensor(RD[:, 0, :], M8[:, :, 1], M8[:, :, 0], ALU.subtract).then_inc(s["rd_s"], 1)
                for j in range(GT):
                    ins = dve.max_index(I8[:, j, :], M8[:, j, :], LG[:, j, :])
                ins.then_inc(s["ix_r"], 1)
                dve.wait_ge(s["ix_r"], g + 1)
                dve.tensor_copy(IF[:, :, :], I8[:, :, 0:TOPK]).then_inc(s["if_r"], 1)
                dve.wait_ge(s["if_r"], g + 1)
                for k in range(TOPK):
                    ins = dve.tensor_tensor(MS[:, k], IOTA[:, :].unsqueeze(1).broadcast_to([P, GT, NEXP]),
                                            IF[:, :, k:k + 1].broadcast_to([P, GT, NEXP]), ALU.is_equal)
                ins.then_inc(s["ms_s"], 1)
                dve.wait_ge(s["ms_s"], g + 1)
                dve.tensor_tensor(MS16[:, :, :], MS[:, 0], MS[:, 1], ALU.add).then_inc(s["ms_r"], 1)
                dve.wait_ge(s["rd_e"], g + 1)
                dve.tensor_scalar(RD[:, 2, :], RD[:, 1, :], 1.0, None, ALU.add).then_inc(s["rd_r"], 1)
                dve.wait_ge(s["rd_r"], 2 * g + 1)
                dve.reciprocal(RW[:, 0, ds(g * GT, GT)], RD[:, 2, :]).then_inc(s["rd_r"], 1)
                dve.wait_ge(s["rd_r"], 2 * g + 2)
                dve.tensor_tensor(RW[:, 1, ds(g * GT, GT)], RD[:, 1, :], RW[:, 0, ds(g * GT, GT)], ALU.mult)

            def s3_slots(g, first=False):
                dve.wait_ge(s["px_mm"], g + 1)
                for j in range(GT):
                    at = GT * NEXP + j * NEXP
                    dve.tensor_tensor(RUN[:, j + 1, :], RUN[:, j, :], WB[:, at:at + NEXP], ALU.add)\
                        .then_inc(s["run_s"], 1)
                    dve.wait_ge(s["run_s"], 5 * g + j + 1)
                dve.tensor_tensor(LG[:, :, :], RUN[:, 0:GT, :], WB[:, 0:GT * NEXP].rearrange("p (j e) -> p j e", j=GT),
                                  ALU.add).then_inc(s["run_s"], 1)
                dve.wait_ge(s["run_s"], 5 * g + 5)
                dve.tensor_copy(RUN[:, 0, :], RUN[:, GT, :]).then_inc(s["pos_s"], 1)
                for k in range(TOPK):
                    ins = dve.tensor_tensor(SL[:, k], MS[:, k], LG[:, :, :], ALU.mult)
                ins.then_inc(s["sl_s"], 1)
                dve.wait_ge(s["sl_s"], g + 1)
                dve.tensor_reduce(SLF[:, :, :], SL[:, :, :, :], AX.X, ALU.add).then_inc(s["slf_s"], 1)
                dve.wait_ge(s["slf_s"], g + 1)
                if not first:
                    for q in range(2):
                        dve.wait_ge(SCT[q], 64 * g)
                dve.tensor_copy(SLOT[:, :, :], SLF[:, :, :]).then_inc(s["slot_r"], 1)

            def s3_rows(g):
                for j in range(GT):
                    dve.wait_ge(s["hi_r"], 4 * g + j + 1)
                    r0 = RB[:, j % 2, 0]
                    tok = TOK[:, ds(g * GT + j, 1)]
                    dve.tensor_copy(r0[:, D:ROW].bitcast(I32), tok)
                    dve.tensor_scalar(RB[:, j % 2, 1, D:ROW].bitcast(I32), tok, float(NTOK), None, ALU.add)
                    dve.tensor_tensor(r0[:, D // 2:D].bitcast(F16), X3[:, j, :], r0[:, 0:D // 2].bitcast(F16),
                                      ALU.subtract).then_inc(s["row_r"], 1)

            def body(g, b1, new_batch, part3, part1, first=False):
                if part3:
                    s3_stats(g - 1)
                if part1:
                    s1_stats(g + 1)
                if part3:
                    s3_norm(g - 1, part3 == 2)
                if part1:
                    s1_norm(g + 1)
                s2_attn(g, 0)
                if part3:
                    s3_logits(g - 1, part3 == 2)
                if new_batch:
                    dve.wait_ge(s["sc_mm"], g * (2 * NCH) + 2 * NCH)
                    kcur(b1)
                if part1:
                    s1_ql(g + 1)
                s2_attn(g, 1)
                if new_batch:
                    vcur(b1)
                if part3:
                    s3_slots(g - 1, part3 == 2)
                for j in range(GT):
                    if part1:
                        s1_max(g + 1, j)
                    if j == 2:
                        s2_x2(g, 0)
                if part1:
                    s1_mh(g + 1)
                s2_x2(g, 1)
                if part3:
                    s3_rows(g - 1)

            s1_stats(0)
            kcur(0)
            vcur(0)
            s1_norm(0, True)
            s1_ql(0)
            for j in range(GT):
                s1_max(0, j)
            s1_mh(0)
            body(0, 0, False, 0, True, True)
            body(1, 1, True, 2, True)
            with dve.Fori(0, (GROUPS - 4) // 2) as t:
                body(t * 2 + 2, t + 1, False, 1, True)
                body(t * 2 + 3, t + 2, True, 1, True)
            body(GROUPS - 2, B - 1, False, 1, True)
            body(GROUPS - 1, None, False, 1, False)
            s3_stats(GROUPS - 1)
            s3_norm(GROUPS - 1)
            s3_logits(GROUPS - 1)
            s3_slots(GROUPS - 1)
            s3_rows(GROUPS - 1)

            for q in range(2):
                dve.wait_ge(SCT[q], 32 * TILES // 2)
            dve.wait_ge(s["pos_s"], GROUPS)
            dve.tensor_copy(RUNI, RUN[:, 0, :]).then_inc(s["c_tab"], 1)
            steps = [0]

            def link(ins):
                steps[0] += 1
                ins.then_inc(s["c_tabe"], 1)
                dve.wait_ge(s["c_tabe"], steps[0])

            cnt, nt, end, le, tmp = (CW[:, 1 + a] for a in range(5))
            link(dve.tensor_tensor(cnt, RUN[:, 0, :], ECAP[:, :], ALU.subtract))
            link(dve.tensor_scalar(CWI, cnt, float(P - 1), None, ALU.add))
            link(dve.tensor_scalar(CWI, CWI, 7, None, ALU.arith_shift_right))
            link(dve.tensor_copy(nt, CWI))
            link(dve.tensor_scalar(tmp, nt, 0.0, 1.0, ALU.mult, ALU.add))
            link(dve.tensor_tensor_scan(end, tmp, nt, 0.0, ALU.mult, ALU.add))
            pidx = CW[:, 7, 0:1]
            link(dve.tensor_copy(pidx, TOK[:, 0:1]))
            link(dve.tensor_scalar(le, end, pidx, None, ALU.is_le))
            link(dve.tensor_tensor(tmp, le, nt, ALU.mult))
            ei, done = CW[:, 6, 0:1], CW[:, 6, 1:2]
            link(dve.tensor_reduce(ei, le, AX.X, ALU.add))
            link(dve.tensor_reduce(done, tmp, AX.X, ALU.add))
            j_in = CW[:, 6, 2:3]
            link(dve.tensor_tensor(j_in, pidx, done, ALU.subtract))
            link(dve.tensor_scalar(j_in, j_in, float(P), None, ALU.mult))
            row = CW[:, 0, 1:2]
            link(dve.scalar_tensor_tensor(out=row, in0=ei, scalar=float(CAP), in1=j_in, op0=ALU.mult, op1=ALU.add))
            link(dve.tensor_scalar(row, row, float(NEXP * CAP), None, ALU.min))
            link(dve.tensor_scalar(CW[:, 0, 0:1], ei, float(NEXP - 1), None, ALU.min))
            for v in range(2):
                link(dve.tensor_scalar(CW[:, 8 + v], IOTA[:, :], CW[:, 0, 0:1], ONE, ALU.is_equal, ALU.mult))
            dve.wait_ge(s["c_mm"], 2)
            dve.tensor_copy(TAB[0:1, :], WA[0:1, 0:2 * P]).then_inc(s["c_cp"], 1)
            dve.tensor_copy(OHT[0:2 * NEXP], WB[0:2 * NEXP, 0:P]).then_inc(s["c_cp"], 1)
            dve.wait_ge(s["c_cp"], 2)

            def c_xt(n, q):
                dve.wait_ge(s["ct_mm"], n + 1)
                dve.tensor_copy(OHB[0:2 * NEXP, q, 0], OHT[0:2 * NEXP, ds(n, 1)].broadcast_to([2 * NEXP, P]))\
                    .then_inc(s["cob_r"], 1)
                dve.tensor_copy(XTS[:, q].rearrange("p v t -> p (v t)"), XTP[q]).then_inc(s["cxt_r"], 1)

            def c_gate(n, q):
                dve.wait_ge(s["cgu_mm"], n + 1)
                dve.tensor_scalar(CG[:, q], GUP[q][:, 0:E], 1.0 / GUS, LIMIT, ALU.mult, ALU.min)\
                    .then_inc(s["cg_r"], 1)
                dve.tensor_scalar(CU[:, q], GUP[q][:, E:F], LIMIT * GUS, -LIMIT * GUS, ALU.min, ALU.max)\
                    .then_inc(s["cu_r"], 1)

            def c_glu(n, q):
                dve.wait_ge(s["ctanh_r"], n + 1)
                dve.scalar_tensor_tensor(out=CT[:, q], in0=CT[:, q], scalar=1.0, in1=CG[:, q],
                                         op0=ALU.add, op1=ALU.mult).then_inc(s["ct1_r"], 1)
                dve.wait_ge(s["ct1_r"], n + 1)
                dve.wait_ge(s["cu_r"], n + 1)
                dve.scalar_tensor_tensor(out=CGD[:, q], in0=CU[:, q], scalar=GUS, in1=CT[:, q],
                                         op0=ALU.add, op1=ALU.mult).then_inc(s["cgd_r"], 1)

            def c_gl(n, q):
                dve.wait_ge(s["cgh_r"], n + 1)
                dve.tensor_copy(OHB[0:2 * NEXP, q, 1], OHT[0:2 * NEXP, ds(n, 1)].broadcast_to([2 * NEXP, P]))\
                    .then_inc(s["cod_r"], 1)
                dve.tensor_tensor(GL[:, q].rearrange("p c t -> p (c t)"), GTP[q][:, 0:E],
                                  GH[:, q].rearrange("p c t -> p (c t)"), ALU.subtract).then_inc(s["cgl_r"], 1)

            c_xt(0, 0)
            c_xt(1, 1)
            c_gate(0, 0)
            c_glu(0, 0)
            c_xt(2, 0)
            c_gate(1, 1)
            c_gl(0, 0)
            c_glu(1, 1)
            with dve.Fori(0, (NSLOT - 3) // 2) as t:
                c_xt(t * 2 + 3, 1)
                c_gate(t * 2 + 2, 0)
                c_gl(t * 2 + 1, 1)
                c_glu(t * 2 + 2, 0)
                c_xt(t * 2 + 4, 0)
                c_gate(t * 2 + 3, 1)
                c_gl(t * 2 + 2, 0)
                c_glu(t * 2 + 3, 1)
            c_gate(NSLOT - 1, 0)
            c_gl(NSLOT - 2, 1)
            c_glu(NSLOT - 1, 0)
            c_gl(NSLOT - 1, 0)

            for c in range(4):
                dve.wait_ge(YIN[c], 32)
                for i in range(8 * c, 8 * c + 8):
                    dve.scalar_tensor_tensor(out=X[:, i, :], in0=Y01[:, 0, i, :], scalar=RW[:, 0, i:i + 1],
                                             in1=X[:, i, :], op0=ALU.mult, op1=ALU.add).then_inc(s["f_s"], 1)
                for i in range(8 * c, 8 * c + 8):
                    dve.wait_ge(s["f_s"], i + 1)
                    dve.scalar_tensor_tensor(out=X[:, i, :], in0=Y01[:, 1, i, :], scalar=RW[:, 1, i:i + 1],
                                             in1=X[:, i, :], op0=ALU.mult, op1=ALU.add).then_inc(s["f_r"], 1)


def kernel(**inputs):
    import numpy as np
    import concourse.bacc as bacc
    from concourse.bass_utils import run_bass_kernel_spmd

    a = {k: np.asarray(v) for k, v in inputs.items()}

    def chunks(w):
        return w.reshape(DC, P, -1).transpose(1, 0, 2).reshape(P, -1)

    def rows(v):
        return np.broadcast_to(v[None, :], (P, v.shape[0]))

    def cols(v):
        return v.reshape(DC, P).T

    def both(v):
        return np.concatenate([v, v], 0)

    cst = np.concatenate([
        chunks(a["L0_attn_W_shift"].T), rows(a["L0_attn_shift_gate"]),
        chunks(np.concatenate([a["L0_attn_W_key"].T, a["L0_attn_W_value"].T], 1)),
        cols(a["L0_attn_ln_w"]), cols(a["L0_attn_ln_b"]),
        both(a["L0_attn_time_decay"][:, None]), both(a["L0_attn_time_first"][:, None]),
        both(a["L0_attn_W_output"].T),
        chunks(a["L0_xattn_wq"].T), chunks(a["L0_xattn_wo"].T),
        cols(a["L0_xattn_bq"]), cols(a["L0_xattn_bk"]), rows(a["L0_xattn_bo"]),
        chunks(a["L0_ffn_Wg"].T), rows(a["L0_ffn_bg"])], 1)
    ctx_t = a["ctx_1024"].reshape(B * KEYS, D).T
    kvc = np.concatenate([chunks(a["L0_xattn_wk"].T), chunks(a["L0_xattn_wv"].T), rows(a["L0_xattn_bv"]),
                          chunks(ctx_t)], 1)

    def apart(w):
        return np.concatenate([w[..., 0::2], w[..., 1::2]], -1)

    def by_part(w):
        return w.reshape(NEXP, DC, P, -1).transpose(0, 2, 1, 3).reshape(NEXP, P, -1)

    wexp = np.concatenate([by_part(apart(a["L0_ffn_Wgu"])), by_part(a["L0_ffn_Wd"])], 2)
    bexp = np.concatenate([apart(a["L0_ffn_bgu"]), a["L0_ffn_bd"]], 1)
    bexp = np.concatenate([bexp, bexp], 0)
    arrays = {"x": a["x"].reshape(NTOK, D), "cst": cst, "kvc": kvc, "wexp": wexp, "bexp": bexp}
    arrays = {f"in_{n}": np.ascontiguousarray(v) for n, v in arrays.items()}
    nc = bacc.Bacc("TRN2", target_bir_lowering=False, num_devices=1)
    args = [nc.dram_tensor(n, v.shape, mybir.dt.from_np(v.dtype), kind="ExternalInput").ap()
            for n, v in arrays.items()]
    args.append(nc.dram_tensor("out_0", (NTOK, D), F32, kind="ExternalOutput").ap())
    build_decoder(nc, *args)
    r = run_bass_kernel_spmd(nc, [arrays], core_ids=[0])
    return np.asarray(r.results[0]["out_0"]).reshape(B, T, D)
```

```python
from contextlib import ExitStack

import concourse.bass as bass
from concourse import mybir

ALU = mybir.AluOpType
ACT = mybir.ActivationFunctionType
AX = mybir.AxisListType
F32 = mybir.dt.float32
F16 = mybir.dt.float16
I32 = mybir.dt.int32
U32 = mybir.dt.uint32
ds = bass.ds

P = 128
D = 256
DC = D // P
B, T, KEYS = 4, 1024, 77
NTOK = B * T
TILES = NTOK // P
TPB = T // P
SHIFT_TILES = TPB // 2
S = 64
HEADS, HD = 16, 16
HG = 8
GK = HG * KEYS
NCH = -(-GK // P)
LAST = GK - (NCH - 1) * P
GT = 4
GTOK = GT * P
GROUPS = TILES // GT
NEXP, TOPK, E = 16, 2, 256
F = 2 * E
CAP = NTOK + P
NSLOT = (TOPK * NTOK + NEXP * (P - 1)) // P
XS_ROWS = NEXP * CAP + P
ROW = D + 2
FAR = 1 << 20
EPS = 1e-5
XSC = 16.0
WSC = 16.0
GUS = XSC * WSC
ONE = 16.0
GDS = 2 * GUS
YS = GDS * WSC
ALPHA, LIMIT = 1.702, 7.0

_at = 0


def _cols(n):
    global _at
    _at += n
    return _at - n


C_WSH = _cols(DC * D)
C_GATE = _cols(D)
C_WKV = _cols(DC * 2 * S)
C_LNW, C_LNB = _cols(DC), _cols(DC)
C_TD, C_TF = _cols(1), _cols(1)
C_WOUT = _cols(D)
C_WQ = _cols(DC * D)
C_WO = _cols(DC * D)
C_BQ, C_BK = _cols(DC), _cols(DC)
C_BO = _cols(D)
C_WG = _cols(DC * NEXP)
C_BG = _cols(NEXP)
C_ALL = _at
Q_WK, Q_WV, Q_BV, Q_CTX = 0, DC * D, 2 * DC * D, 2 * DC * D + D
Q_ALL = Q_CTX + DC * B * KEYS
PW = 512
PIECES = 3
NPIECE = NEXP * PIECES
A_PIECES = NPIECE // 2
assert DC * F == 2 * PW and DC * E == PW
W_DOWN, LOW = 2 * 2 * PW, PW
WEX = 2 * PIECES * PW

def build_decoder(nc, x, cst, kvc, wexp, bexp, out):
    xs_rows = nc.dram_tensor("xs_rows", (XS_ROWS, ROW), F32, kind="Internal").ap()
    y_rows = nc.dram_tensor("y_rows", (TOPK * NTOK, D), F32, kind="Internal").ap()
    v_flat = nc.dram_tensor("v_flat", (B, HEADS // HG, GK, HD), F32, kind="Internal").ap()

    ctx = ExitStack()
    with ctx:
        def sb(name, shape, dt):
            return ctx.enter_context(nc.sbuf_tensor(name, shape, dt))

        def sem(name):
            return ctx.enter_context(nc.semaphore(name))

        X = sb("X", [P, TILES, D], F32)
        W16 = sb("W16", [P, NPIECE, 2, PW], F16)
        CST = sb("CST", [P, C_ALL], F32)
        KRAW = sb("KRAW", [P, 2, DC, B, KEYS], F16)
        KCUR = sb("KCUR", [P, 2, DC, 2, HG, KEYS], F16)
        VFLAT = sb("VFLAT", [P, DC, NCH, HD], F32)
        VCUR = sb("VCUR", [P, DC, NCH, 2, 2, HD], F32)
        MV = sb("MV", [P, NCH, 2, 2, HD], F32)
        MK = sb("MK", [P, HG], F16)
        IND = sb("IND", [2 * HEADS, HEADS * KEYS], F16)
        ID32 = sb("ID32", [P, P], F32)
        ID16 = sb("ID16", [P, P], F16)
        UP16 = sb("UP16", [P, P], F16)
        ON16 = sb("ON16", [P, P], F16)
        BEX = sb("BEX", [2 * NEXP, F + E], F16)
        TOK = sb("TOK", [P, TILES], I32)
        IOTA = sb("IOTA", [P, NEXP], F32)
        RUN = sb("RUN", [P, GT + 1, NEXP], F32)
        ECAP = sb("ECAP", [P, NEXP], F32)
        RW = sb("RW", [P, TOPK, TILES], F32)
        HALF = sb("HALF", [P, TPB], F32)
        SMALL = sb("SMALL", [P, 16], F32)
        STG = sb("STG", [P, 2, PW], F32)

        AR = sb("AR", [P, 9744], F32)

        def ar(at, n, dt=F32):
            v = AR[:, at:at + n]
            return v if dt == F32 else v.bitcast(dt)

        XN = ar(0, 16 * D).rearrange("p (k d) -> p k d", k=16)
        XNT = ar(4096, 16 * D).rearrange("p (c t) -> p c t", c=DC)
        XST = ar(4096, 16 * D).rearrange("p (h c t) -> p h c t", h=2, c=DC)
        TW = ar(8192, GTOK)
        ST = ar(8704, 2 * GTOK).rearrange("p (h t) -> p h t", h=2)
        PB = ar(0, NCH * GTOK).rearrange("p (n t) -> p n t", n=NCH)
        XQ = ar(2560, GT * D).rearrange("p (k d) -> p k d", k=GT)
        XQT = ar(3584, DC * GTOK).rearrange("p (c t) -> p c t", c=DC)
        X3, X3T = XQ, XQT
        QH = ar(4608, DC * GTOK, F16).rearrange("p (b c t) -> p b c t", b=2, c=DC)
        QL = ar(5632, DC * GTOK, F16).rearrange("p (b c t) -> p b c t", b=2, c=DC)
        AT = ar(6656, DC * GTOK).rearrange("p (c t) -> p c t", c=DC)
        RB = ar(7680, 2 * GT * ROW).rearrange("p (b k w) -> p b k w", b=2, k=GT)
        RIN = ar(0, 2 * ROW).rearrange("p (b w) -> p b w", b=2)
        XTS = ar(516, 2 * D, F16).rearrange("p (b v t) -> p b v t", b=2, v=4)
        CG = ar(1028, 2 * E).rearrange("p (b e) -> p b e", b=2)
        CT = ar(1540, 2 * E).rearrange("p (b e) -> p b e", b=2)
        CU = ar(2052, 2 * E).rearrange("p (b e) -> p b e", b=2)
        CGD = ar(2564, 2 * E).rearrange("p (b e) -> p b e", b=2)
        GH = ar(3076, E, F16).rearrange("p (b c t) -> p b c t", b=2, c=DC)
        GL = ar(3332, E, F16).rearrange("p (b c t) -> p b c t", b=2, c=DC)
        CY = ar(3588, 2 * D).rearrange("p (b e) -> p b e", b=2)
        OHB = ar(4100, 2 * P, F16).rearrange("p (b k t) -> p b k t", b=2, k=2)
        PAD = ar(4356, ROW)
        OHT = ar(4614, P, F16)[:, 0:P]
        TAB = ar(4742, 2 * P, I32)
        RUNI = ar(4998, NEXP, I32)
        CW = ar(5014, 10 * NEXP).rearrange("p (a e) -> p a e", e=NEXP)
        CWI = ar(5014 + 10 * NEXP, NEXP, I32)
        NIX = ar(5190, 2, I32)
        IXF = ar(5192, 2)
        CIX = ar(5194, NSLOT)
        DIAG = ar(5273, P // 2, F16)
        EXB = ar(5337, P)
        w_flat = W16[:, :, :, :].rearrange("p n v w -> p (n v w)")
        w_words = w_flat.bitcast(F32)
        Y01 = w_words[:, 0:TOPK * TILES * D].rearrange("p (k i d) -> p k i d", k=TOPK, i=TILES)

        def spare(e, n):
            return w_words[:, e * WEX // 2:(e + n) * WEX // 2]

        KVC = spare(NEXP - 2, 2)
        VSB = spare(NEXP - 3, 1)[0:KEYS, 0:B * D].rearrange("p (b e) -> p b e", b=B)
        KTMP = spare(NEXP - 4, 1)[:, 0:B * KEYS]
        BRAW = spare(NEXP - 5, 1)
        SCR = spare(NEXP - 6, 1)

        STAT = sb("STAT", [P, 16, 6], F32)
        MVA = sb("MVA", [P, 16, 2], F32)
        RS = sb("RS", [P, 16], F32)
        MVQ = sb("MVQ", [P, TILES, 2], F32)
        RSQ = sb("RSQ", [P, 2, TILES], F32)
        STAT3 = sb("STAT3", [P, GT, 6], F32)
        MVA3 = sb("MVA3", [P, GT, 2], F32)
        RS3 = sb("RS3", [P, 2, GT], F32)
        MX = sb("MX", [P, GT, HEADS], F32)
        MH = sb("MH", [P, GT, 2 * HEADS], F16)
        MT = sb("MT", [2 * HEADS, GTOK], F16)
        LG = sb("LG", [P, GT, NEXP], F32)
        M8 = sb("M8", [P, GT, 8], F32)
        I8 = sb("I8", [P, GT, 8], U32)
        IF = sb("IF", [P, GT, TOPK], F32)
        MS = sb("MS", [P, TOPK, GT, NEXP], F32)
        MS16 = sb("MS16", [P, GT, NEXP], F16)
        SL = sb("SL", [P, TOPK, GT, NEXP], F32)
        TOKF = sb("TOKF", [P, TILES], F32)
        SLF = sb("SLF", [P, TOPK, GT], F32)
        SLOT = sb("SLOT", [P, 2, TOPK, GT], I32)
        RD = sb("RD", [P, 3, GT], F32)

        def bank(i, n=1):
            return ctx.enter_context(nc.psum_tensor(f"bank{i}", [P, n * 512], F32))

        SC = [bank(0), bank(1)]
        MXP = bank(2, 2)
        NUM, DEN = bank(4), bank(5)
        WA, WB = bank(6), bank(7)
        WK = [WA, WB]
        MXB = MXP[:, :].rearrange("p (b n) -> p b n", b=2)
        TRA, SHA, KVA, OUA = [SC[0], SC[1]], [MXB[:, 0], MXB[:, 1]], [NUM, DEN], [WA, WB]
        LGP, UPP, ONP = MXB[:, 0, 320:384], MXB[:, 0, 384:448], MXB[:, 1, 384:448]
        MTP = [MXB[0:2 * HEADS, h, 320:448].bitcast(F16) for h in range(2)]
        XTP = [SC[0][:, 0:D].bitcast(F16), SC[1][:, 0:D].bitcast(F16)]
        GUP, GTP, YP = [MXB[:, 0], MXB[:, 1]], [NUM, DEN], [WA, WB]

        def cst_w(c0, n, c):
            return CST[:, c0 + c * n:c0 + (c + 1) * n]

        names = """sct0 sct1 rin0 rin1 ysc0 ysc1 cst_in x_in kvc_in bex_in v_sb v_out v_in w_split stg_in row_r
            dup_r consts_ready c_tab pad_r pads_in c_cp ct_mm cix_r f_r out_done consts1 w_hi w_scaled
            a_aggr a_eps a_rs wsh_done a_t1 a_xg a_aggr2 a_eps2 a_rs2 va2 ep2 rs2_r xq_r xb_r va3 ep3 rs3_r
            slot_r cy_r gate_tanh etf_exp k_mm small_ready k_hi a_kv a_xnt a_t2 a_sh a_xst kv_bias_ready
            a_scan a_tanh a_exp t_mm xqT_r q_mm qh_r mt_mm mT_r sc_mm pv_mm exp_r t3_mm x3T_r hi_r rd_s
            rd_e xn3_r a_x1 bex_ready cg_r ctanh_r ctg_mm cgh_r cd_mm v_mm kv_bias_mm wkv_ready k_ready
            a_xn a_xs a_xn2 a_wkv a_out lg_r kcur_r mx_r mx_mm mh_r ql_r vcur_r at_r run_s out_mm x2_r
            lg_mm ms_r px_mm c_tabe c_mm cxt_r cob_r cu_r cgu_mm cgd_r cgl_r cod_r wsh_ready k_tmp bex_s
            a_stat a_stat2 st2 mh_s rec_s st3 top_r ix_r if_r ms_s rd_r pos_s sl_s slf_s ct1_r f_s y_in0
            y_in1 y_in2 y_in3 stg0 stg1 act_past lo_r rsq_s rsq_r rs3_s stq vaq ep4 eb_r pe_past ixa ixb nix_r sp_past pool_past dve_past""".split()
        s = {n: sem(n) for n in names}
        SCT = [s["sct0"], s["sct1"]]
        RINS = [s["rin0"], s["rin1"]]
        YSC = [s["ysc0"], s["ysc1"]]
        STGI = [s["stg0"], s["stg1"]]
        YIN = [s[f"y_in{i}"] for i in range(4)]

        block = ctx.enter_context(nc.Block())
        HALF_TILES = [[bb * TPB + SHIFT_TILES * h + j for bb in range(2) for j in range(SHIFT_TILES)]
                      for h in range(2)]
        ORDER = HALF_TILES[0] + HALF_TILES[1]
        x_t = x.rearrange("(i p) d -> p i d", p=P)
        out_t = out.rearrange("(i p) d -> p i d", p=P)

        @block.sync
        def _(sp):
            sp.dma_start(CST[:, :], cst).then_inc(s["cst_in"], 16)
            for p in range(2):
                if p:
                    sp.wait_ge(s["x_in"], 32)
                for q in range(2):
                    i = 16 * p + 8 * q
                    sp.dma_start(X[:, i:i + 8, :], x_t[:, i:i + 8, :]).then_inc(s["x_in"], 16)
                if p == 0:
                    sp.dma_start(KVC[:, 0:Q_ALL], kvc).then_inc(s["kvc_in"], 16)
                    sp.dma_start(BRAW[0:2 * NEXP, 0:F + E], bexp).then_inc(s["bex_in"], 16)
            sp.wait_ge(s["v_sb"], B)
            for b in range(B):
                for m in range(DC):
                    sp.dma_start(v_flat[b, m].rearrange("(h k) e -> k h e", k=KEYS),
                                 VSB[:, b, m * P:(m + 1) * P].rearrange("p (h e) -> p h e", h=HG))\
                        .then_inc(s["v_out"], 16)
            sp.wait_ge(s["v_out"], 16 * B * DC)

            def vload(b, first=False):
                if not first:
                    sp.wait_ge(s["vcur_r"], b)
                for m in range(DC):
                    v = v_flat[ds(b, 1), m].rearrange("a n e -> (a n) e")
                    sp.dma_start(VFLAT[:, m, 0:NCH - 1, :],
                                 v[0:(NCH - 1) * P, :].rearrange("(n p) e -> p n e", p=P)).then_inc(s["v_in"], 16)
                    sp.dma_start(VFLAT[0:LAST, m, NCH - 1, :], v[(NCH - 1) * P:GK, :]).then_inc(s["v_in"], 16)

            def wload(n, q, first=False):
                if not first:
                    sp.wait_ge(s["w_split"], n - 1)
                sp.dma_start(STG[:, q, :], wexp[ds(n, 1)].rearrange("a p n -> (a p) n")).then_inc(STGI[q], 16)

            vload(0, True)
            wload(0, 0, True)
            wload(1, 1, True)
            with sp.Fori(1, A_PIECES // 2) as t:
                wload(t * 2, 0)
                wload(t * 2 + 1, 1)
            for k in range(6):
                wload(A_PIECES + k, k % 2)
            vload(1)
            with sp.Fori(1, B - 1) as b:
                for k in range(6):
                    wload(b * 6 + (A_PIECES + k), k % 2)
                vload(b + 1)
            for k in range(6):
                wload(A_PIECES + 6 * (B - 1) + k, k % 2)

            sp.wait_ge(s["c_tab"], 1)
            sp.wait_ge(s["pad_r"], 2)
            with sp.Fori(0, NEXP) as e:
                r = sp.value_load(RUNI[0:1, ds(e, 1)], min_val=0, max_val=XS_ROWS - P)
                sp.dma_start(xs_rows[ds(r, P), :], PAD).then_inc(s["pads_in"], 16)
            sp.dma_start(xs_rows[NEXP * CAP:XS_ROWS, :], PAD).then_inc(s["pads_in"], 16)
            sp.wait_ge(s["pads_in"], 16 * (NEXP + 1))
            for q in range(2):
                sp.wait_ge(SCT[q], 16 * TOPK * TILES // 2)
            sp.wait_ge(s["c_cp"], 2)

            def load(n, q, first=False):
                r = sp.value_load(TAB[0:1, ds(P + n, 1)], min_val=0, max_val=XS_ROWS - P)
                if not first:
                    sp.wait_ge(s["ct_mm"], n - 1)
                    sp.wait_ge(s["cix_r"], n - 1)
                sp.dma_start(RIN[:, q, :], xs_rows[ds(r, P), :]).then_inc(RINS[q], 16)

            load(0, 0, True)
            load(1, 1, True)
            load(2, 0)
            with sp.Fori(0, (NSLOT - 3) // 2) as t:
                load(t * 2 + 3, 1)
                load(t * 2 + 4, 0)

            for q in range(2):
                sp.wait_ge(YSC[q], 16 * ((NSLOT + 1 - q) // 2))
            y_t = y_rows.rearrange("(k i p) d -> p k i d", k=TOPK, p=P)
            for c in range(4):
                for k in range(TOPK):
                    sp.dma_start(Y01[:, k, 8 * c:8 * c + 8, :], y_t[:, k, 8 * c:8 * c + 8, :])\
                        .then_inc(YIN[c], 16)
            for c in range(4):
                sp.wait_ge(s["f_r"], 8 * (c + 1))
                sp.dma_start(out_t[:, 8 * c:8 * c + 8, :], X[:, 8 * c:8 * c + 8, :]).then_inc(s["out_done"], 16)
            sp.wait_ge(s["out_done"], 64)

        @block.gpsimd
        def _(pool):
            n1 = [0]

            def c1(ins):
                n1[0] += 1
                ins.then_inc(s["consts1"], 1)

            def sel(v, op, base, pattern, cm, fill=0.0):
                pool.wait_ge(s["consts1"], n1[0])
                c1(pool.affine_select(out=v, in_=v, compare_op=op, fill=fill, base=base, pattern=pattern,
                                      channel_multiplier=cm))

            c1(pool.memset(HALF[:, :], -0.5))
            for m in (ID32, ID16):
                c1(pool.memset(m[:, :], 0.0))
                sel(m[:, :], ALU.not_equal, 0, [[-1, P]], 1, 1.0)
            c1(pool.memset(MK[:, :], 1.0))
            sel(MK[:, :], ALU.is_ge, 0, [[-HD, HG]], 1)
            sel(MK[:, :], ALU.is_ge, HD - 1, [[HD, HG]], -1)
            c1(pool.memset(MV[:, :, :, :, :].rearrange("p a b c d -> p (a b c d)"), 1.0))
            for v in range(2):
                pat = [[P - 2 * KEYS, NCH], [-KEYS, 2], [0, HD]]
                sel(MV[:, :, v], ALU.is_ge, 2 * KEYS * v, pat, 1)
                sel(MV[:, :, v], ALU.is_ge, (KEYS - 1) - 2 * KEYS * v, [[-a, n] for a, n in pat], -1)
            ind2 = SCR[0:2 * HEADS, 0:HEADS * KEYS // 2].bitcast(F16)
            for v, base in ((IND[:, :], 0), (ind2, KEYS * HEADS)):
                c1(pool.memset(v, 1.0))
                sel(v, ALU.is_ge, base, [[1, HEADS * KEYS]], -KEYS)
                sel(v, ALU.is_ge, (KEYS - 1) - base, [[-1, HEADS * KEYS]], KEYS)
            pool.wait_ge(s["consts1"], n1[0])
            c1(pool.tensor_tensor(IND[:, :], IND[:, :], ind2, ALU.add))
            c1(pool.memset(ON16[:, :], 1.0))
            c1(pool.memset(UP16[:, :], 1.0))
            sel(UP16[:, :], ALU.is_gt, 0, [[1, P]], -1)
            c1(pool.iota(TOK[:, :], [[P, TILES]], base=0, channel_multiplier=1))
            pool.wait_ge(s["consts1"], n1[0])
            c1(pool.tensor_scalar(TOKF[:, :], TOK[:, :], 1.0, float(NTOK), ALU.mult, ALU.add))
            c1(pool.iota(SCR[:, 700:700 + NEXP].bitcast(I32), [[1, NEXP]], base=0, channel_multiplier=0))
            pool.wait_ge(s["consts1"], n1[0])
            c1(pool.tensor_copy(IOTA[:, :], SCR[:, 700:700 + NEXP].bitcast(I32)))
            pool.wait_ge(s["consts1"], n1[0])
            c1(pool.tensor_scalar(ECAP[:, :], IOTA[:, :], float(CAP), 0.0, ALU.mult, ALU.add))
            pool.wait_ge(s["consts1"], n1[0])
            pool.tensor_copy(RUN[:, 0, :], ECAP[:, :]).then_inc(s["consts_ready"], 1)

            def root(var, eps_sem, rs_sem, rs, n, k, scale):
                pool.tensor_scalar(rs, var, EPS, 1.0 / (scale * scale), ALU.add, ALU.mult).then_inc(eps_sem, 1)
                pool.wait_ge(eps_sem, k)
                pool.tensor_tensor(rs, rs, HALF[:, 0:n], ALU.pow).then_inc(rs_sem, 1)

            def split(n, q, h):
                pool.wait_ge(STGI[q], 16 * (h + 1)).then_inc(s["pool_past"], 1)
                pool.wait_ge(s["w_hi"], n + 1).then_inc(s["pool_past"], 1)
                w = W16[:, ds(n, 1), :, :].rearrange("p a v w -> p (a v) w")
                pool.tensor_tensor(w[:, 1], STG[:, q], w[:, 0], ALU.subtract).then_inc(s["w_split"], 1)

            def splits(first):
                with pool.Fori(first, first + A_PIECES // 4) as h:
                    split(h * 2, 0, h)
                    split(h * 2 + 1, 1, h)

            for p in range(2):
                if p == 0:
                    splits(0)
                for q in range(2):
                    pool.wait_ge(s["a_aggr"], 2 * p + q + 1)
                    root(MVA[:, 8 * q:8 * q + 8, 1], s["a_eps"], s["a_rs"], RS[:, 8 * q:8 * q + 8], 8, 2 * p + q + 1, 1.0)
                pool.wait_ge(s["wsh_done"], 1)
                for n, k in enumerate(ORDER):
                    pool.wait_ge(s["a_t1"], 16 * p + k + 1)
                    pool.tensor_tensor(XN[:, k, :], XN[:, k, :], CST[:, C_GATE:C_GATE + D], ALU.mult)\
                        .then_inc(s["a_xg"], 1)
                for q in range(2):
                    pool.wait_ge(s["a_aggr2"], 2 * p + q + 1)
                    root(MVA[:, 8 * q:8 * q + 8, 1], s["a_eps2"], s["a_rs2"], RS[:, 8 * q:8 * q + 8], 8, 2 * p + q + 1, 1.0)

                if p == 0:
                    splits(A_PIECES // 4)
                pool.wait_ge(s["vaq"], p + 1)
                mv = MVQ[:, 16 * p:16 * p + 16]
                rq, nq = RSQ[:, 0, 16 * p:16 * p + 16], RSQ[:, 1, 16 * p:16 * p + 16]
                for q in range(2):
                    pool.tensor_scalar(rq[:, 8 * q:8 * q + 8], mv[:, 8 * q:8 * q + 8, 1], EPS, 1.0, ALU.add, ALU.mult)\
                        .then_inc(s["rsq_s"], 1)
                    pool.wait_ge(s["rsq_s"], 6 * p + 3 * q + 1)
                    pool.tensor_tensor(rq[:, 8 * q:8 * q + 8], rq[:, 8 * q:8 * q + 8], HALF[:, 0:8], ALU.pow)\
                        .then_inc(s["rsq_s"], 1)
                    pool.wait_ge(s["rsq_s"], 6 * p + 3 * q + 2)
                    pool.tensor_tensor(nq[:, 8 * q:8 * q + 8], rq[:, 8 * q:8 * q + 8], mv[:, 8 * q:8 * q + 8, 0],
                                       ALU.mult).then_inc(s["rsq_s"], 1)
                    pool.wait_ge(s["rsq_s"], 6 * p + 3 * q + 3)
                    pool.tensor_scalar(nq[:, 8 * q:8 * q + 8], nq[:, 8 * q:8 * q + 8], -1.0, 0.0, ALU.mult, ALU.add)\
                        .then_inc(s["rsq_r"], 1)

            def add_bo(g):
                pool.wait_ge(s["xq_r"], 4 * g + 4)
                for j in range(GT):
                    xt = X[:, ds(g * GT + j, 1), :].rearrange("p a d -> p (a d)")
                    ins = pool.tensor_tensor(xt, xt, CST[:, C_BO:C_BO + D], ALU.add)
                ins.then_inc(s["xb_r"], 1)

            def root3(g):
                pool.wait_ge(s["va3"], g + 1).then_inc(s["pool_past"], 1)
                root(MVA3[:, :, 1], s["ep3"], s["rs3_s"], RS3[:, 0], GT, g + 1, XSC)
                pool.wait_ge(s["rs3_s"], g + 1).then_inc(s["pool_past"], 1)
                pool.tensor_tensor(RS3[:, 1], RS3[:, 0], MVA3[:, :, 0], ALU.mult).then_inc(s["ep4"], 1)
                pool.wait_ge(s["ep4"], g + 1).then_inc(s["pool_past"], 1)
                pool.tensor_scalar(RS3[:, 1], RS3[:, 1], -1.0, 0.0, ALU.mult, ALU.add).then_inc(s["rs3_r"], 1)

            def low_rows(g, par):
                pool.wait_ge(s["hi_r"], g + 1)
                for j in range(GT):
                    hl = RB[:, par, j, 0:D].bitcast(F16).rearrange("p (v d) -> p v d", v=2)
                    ins = pool.tensor_tensor(hl[:, 1], X3[:, j, :], hl[:, 0], ALU.subtract)
                ins.then_inc(s["lo_r"], 1)

            def scatter(g, par):
                pool.wait_ge(s["lo_r"], g + 1).then_inc(s["pool_past"], 1)
                pool.wait_ge(s["slot_r"], g + 1).then_inc(s["pool_past"], 1)
                for j in range(GT):
                    for k in range(TOPK):
                        pool.indirect_dma_start(
                            xs_rows, bass.IndirectOffsetOnAxis(ap=SLOT[:, par, k, j:j + 1], axis=0),
                            RB[:, par, j, :], None, bounds_check=XS_ROWS - 1, oob_is_err=True)\
                            .then_inc(SCT[par], 16)

            def kcur(b, bp):
                if not (isinstance(b, int) and b < 2):
                    pool.wait_ge(s["sc_mm"], (b - 1) * (4 * NCH))
                for m in range(DC):
                    for v in range(2):
                        ins = pool.tensor_tensor(
                            KCUR[:, ds(bp, 1), m, v].rearrange("p a h k -> p (a h) k"),
                            KRAW[:, v, m, ds(b, 1), :].broadcast_to([P, HG, KEYS]),
                            MK[:, :].unsqueeze(2).broadcast_to([P, HG, KEYS]), ALU.mult)
                ins.then_inc(s["kcur_r"], 1)

            def body(g, b, par, out=True, log=True, attn=True, nextk=None):
                if attn:
                    add_bo(g)
                    for k in range(2):
                        split(g * PIECES + (A_PIECES + k), (par + k) % 2, b * PIECES + ((A_PIECES + 3 * par + k) // 2))
                if out:
                    root3(g - 1)
                if attn:
                    split(g * PIECES + (A_PIECES + 2), par, b * PIECES + ((A_PIECES + 3 * par + 2) // 2))
                if log:
                    scatter(g - 2, par)
                if out:
                    low_rows(g - 1, 1 - par)
                if nextk is not None:
                    kcur(b + 1, nextk)

            pool.wait_ge(s["k_ready"], DC)
            kcur(0, 0)
            body(0, 0, 0, False, False, nextk=1)
            body(1, 0, 1, log=False)
            with pool.Fori(1, B - 1) as b:
                body(b * 2, b, 0, nextk=(b + 1) % 2)
                body(b * 2 + 1, b, 1)
            body(GROUPS - 2, B - 1, 0)
            body(GROUPS - 1, B - 1, 1)
            body(GROUPS, B, 0, attn=False)
            scatter(GROUPS - 1, 1)

            pool.memset(PAD, 0.0).then_inc(s["pad_r"], 1)
            pool.wait_ge(s["pad_r"], 1)
            pool.memset(PAD[:, D:D + 1], float(FAR)).then_inc(s["pad_r"], 1)
            pool.wait_ge(s["eb_r"], 1)

            def y_index(n, q, t):
                pool.wait_ge(RINS[q], 16 * (t + 1)).then_inc(s["pool_past"], 1)
                pool.tensor_tensor(IXF[:, q:q + 1], RIN[:, q, D + 1:ROW], EXB[:, ds(n, 1)], ALU.subtract)\
                    .then_inc(s["ixa"], 1)
                pool.wait_ge(s["ixa"], n + 1).then_inc(s["pool_past"], 1)
                pool.tensor_scalar(IXF[:, q:q + 1], IXF[:, q:q + 1], 0.0, float(NTOK), ALU.is_equal, ALU.mult)\
                    .then_inc(s["ixb"], 1)
                pool.wait_ge(s["ixb"], n + 1).then_inc(s["pool_past"], 1)
                pool.tensor_tensor(CIX[:, ds(n, 1)], RIN[:, q, D:D + 1], IXF[:, q:q + 1], ALU.subtract)\
                    .then_inc(s["cix_r"], 1)

            def y_scatter(n, q, t, first=False):
                if not first:
                    pool.wait_ge(YSC[q], 16 * t).then_inc(s["pool_past"], 1)
                pool.wait_ge(s["cix_r"], n + 1).then_inc(s["pool_past"], 1)
                pool.tensor_copy(NIX[:, q:q + 1], CIX[:, ds(n, 1)]).then_inc(s["nix_r"], 1)
                pool.wait_ge(s["cy_r"], n + 1).then_inc(s["pool_past"], 1)
                pool.wait_ge(s["nix_r"], n + 1).then_inc(s["pool_past"], 1)
                pool.indirect_dma_start(
                    y_rows, bass.IndirectOffsetOnAxis(ap=NIX[:, q:q + 1], axis=0), CY[:, q, :], None,
                    bounds_check=TOPK * NTOK - 1, oob_is_err=False).then_inc(YSC[q], 16)

            y_index(0, 0, 0)
            y_index(1, 1, 0)
            y_index(2, 0, 1)
            y_index(3, 1, 1)
            y_scatter(0, 0, 0, True)
            y_index(4, 0, 2)
            y_scatter(1, 1, 0, True)
            with pool.Fori(1, (NSLOT - 3) // 2) as t:
                y_index(t * 2 + 3, 1, t + 1)
                y_scatter(t * 2, 0, t)
                y_index(t * 2 + 4, 0, t + 2)
                y_scatter(t * 2 + 1, 1, t)
            for n in range(NSLOT - 3, NSLOT):
                y_scatter(n, n % 2, n // 2)

        @block.scalar
        def _(act):
            act.wait_ge(s["cst_in"], 16)
            act.activation(CST[:, C_GATE:C_GATE + D], CST[:, C_GATE:C_GATE + D], ACT.Tanh, scale=0.5)\
                .then_inc(s["gate_tanh"], 1)
            act.activation(SMALL[:, 0:1], CST[:, C_TD:C_TD + 1], ACT.Exp).then_inc(s["etf_exp"], 1)
            act.activation(SMALL[:, 1:2], CST[:, C_TF:C_TF + 1], ACT.Exp).then_inc(s["etf_exp"], 1)
            for m in range(DC):
                act.wait_ge(s["k_mm"], m + 1)
                act.wait_ge(s["small_ready"], 1)
                act.activation(KRAW[:, 0, m].rearrange("p b k -> p (b k)"), WK[m][:, 0:B * KEYS], ACT.Identity,
                               scale=0.25, bias=SMALL[:, 2 + m:3 + m]).then_inc(s["k_hi"], 1)

            def whi(n, q, h):
                act.wait_ge(STGI[q], 16 * (h + 1)).then_inc(s["act_past"], 1)
                act.activation(STG[:, q], STG[:, q], ACT.Copy, scale=WSC).then_inc(s["w_scaled"], 1)
                act.wait_ge(s["w_scaled"], n + 1).then_inc(s["act_past"], 1)
                act.activation(W16[:, ds(n, 1), 0, :].rearrange("p a w -> p (a w)"), STG[:, q], ACT.Copy)\
                    .then_inc(s["w_hi"], 1)

            def whis(first):
                with act.Fori(first, first + A_PIECES // 4) as h:
                    whi(h * 2, 0, h)
                    whi(h * 2 + 1, 1, h)

            whis(0)
            for p in range(2):
                for k in range(16):
                    act.wait_ge(s["a_t1"], 16 * p + k + 1)
                    if p:
                        act.wait_ge(s["a_kv"], 2 * p)
                    act.activation(XNT[:, :, k * P:(k + 1) * P],
                                   TRA[k % 2][:, 0:D].rearrange("p (c t) -> p c t", c=DC), ACT.Copy)\
                        .then_inc(s["a_xnt"], 1)
                for h in range(2):
                    for k in range(8):
                        act.wait_ge(s["a_t2"], 16 * p + 8 * h + k + 1)
                        act.wait_ge(s["a_sh"], 16 * (p + 1))
                        act.activation(XST[:, h, :, k * P:(k + 1) * P],
                                       TRA[k % 2][:, 0:D].rearrange("p (c t) -> p c t", c=DC), ACT.Copy)\
                            .then_inc(s["a_xst"], 1)
                    act.wait_ge(s["a_kv"], 2 * p + h + 1)
                    act.wait_ge(s["kv_bias_ready"], 1)
                    if p or h:
                        act.wait_ge(s["a_scan"], 2 * p + h)
                    act.activation(TW, KVA[0][:, :], ACT.Tanh, scale=0.5, bias=SMALL[:, 5:6])\
                        .then_inc(s["a_tanh"], 1)
                    act.wait_ge(s["a_tanh"], 2 * p + h + 1)
                    act.activation(TW, TW, ACT.Exp, scale=SMALL[:, 4:5], bias=SMALL[:, 4:5])\
                        .then_inc(s["a_exp"], 1)
                if p == 0:
                    whis(A_PIECES // 4)

            def norm_q(g, j, first=False):
                if j == 0:
                    if not first:
                        act.wait_ge(s["t_mm"], 2 * g).then_inc(s["act_past"], 1)
                    if not isinstance(g, int) or g >= 3:
                        act.wait_ge(s["lo_r"], g - 2).then_inc(s["act_past"], 1)
                        act.wait_ge(s["t3_mm"], 2 * (g - 2)).then_inc(s["act_past"], 1)
                act.activation(XQ[:, j, :], X[:, ds(g * GT + j, 1), :].rearrange("p a d -> p (a d)"), ACT.Identity,
                               scale=RSQ[:, 0, ds(g * GT + j, 1)], bias=RSQ[:, 1, ds(g * GT + j, 1)])\
                    .then_inc(s["xq_r"], 1)

            def evac_t(g):
                for r in range(2):
                    act.wait_ge(s["t_mm"], 2 * g + r + 1)
                    act.activation(XQT[:, :, 2 * r * P:2 * (r + 1) * P],
                                   WK[r][:, :].rearrange("p (j c t) -> p c j t", j=2, c=DC),
                                   ACT.Copy).then_inc(s["xqT_r"], 1)

            def evac_q(g, par):
                for m in range(DC):
                    act.wait_ge(s["q_mm"], 2 * g + m + 1)
                    act.activation(QH[:, par, m], WK[m][:, :], ACT.Identity, bias=CST[:, C_BQ + m:C_BQ + m + 1])\
                        .then_inc(s["qh_r"], 1)

            def evac_m(g):
                act.wait_ge(s["mt_mm"], g + 1)
                for h in range(2):
                    ins = act.activation(MT[:, h * 2 * P:(h + 1) * 2 * P], MTP[h], ACT.Copy)
                ins.then_inc(s["mT_r"], 1)

            def exps(g, m, c, first=False):
                rows = P if c < NCH - 1 else LAST
                act.wait_ge(s["sc_mm"], g * (2 * NCH) + (m * NCH + c + 1))
                if c == 0 and not first:
                    act.wait_ge(s["pv_mm"], 2 * g + m)
                act.activation(PB[0:rows, c, :], SC[(m * NCH + c) % 2][0:rows, :], ACT.Exp)\
                    .then_inc(s["exp_r"], 1)

            def norm_3(g):
                act.wait_ge(s["rs3_r"], g + 1)
                for j in range(GT):
                    act.activation(X3[:, j, :], X[:, ds(g * GT + j, 1), :].rearrange("p a d -> p (a d)"),
                                   ACT.Identity, scale=RS3[:, 0, j:j + 1], bias=RS3[:, 1, j:j + 1])\
                        .then_inc(s["xn3_r"], 1)

            def rows_hi(g, par, k):
                if not (isinstance(k, int) and k == 0):
                    act.wait_ge(SCT[par], k * (16 * TOPK * GT)).then_inc(s["act_past"], 1)
                act.wait_ge(s["xn3_r"], 4 * g + 4).then_inc(s["act_past"], 1)
                for j in range(GT):
                    ins = act.activation(RB[:, par, j, 0:D // 2].bitcast(F16), X3[:, j, :], ACT.Copy)
                ins.then_inc(s["hi_r"], 1)

            def evac_t3(g):
                for r in range(2):
                    act.wait_ge(s["t3_mm"], 2 * g + r + 1)
                    act.activation(X3T[:, :, 2 * r * P:2 * (r + 1) * P],
                                   WK[r][:, :].rearrange("p (j c t) -> p c j t", j=2, c=DC),
                                   ACT.Copy).then_inc(s["x3T_r"], 1)

            def pair_exp(g):
                act.wait_ge(s["rd_s"], g + 1)
                act.activation(RD[:, 1, :], RD[:, 0, :], ACT.Exp).then_inc(s["rd_e"], 1)

            def body(g, b, par, out=True, log=True, attn=True, nxt=True):
                first = isinstance(g, int) and g == 0
                if attn:
                    for c in range(NCH):
                        exps(g, 0, c, first)
                        if nxt and c < GT:
                            norm_q(g + 1, c)
                if log:
                    pair_exp(g - 2)
                if attn:
                    for k in range(2):
                        whi(g * PIECES + (A_PIECES + k), (par + k) % 2, b * PIECES + ((A_PIECES + 3 * par + k) // 2))
                if nxt:
                    evac_t(g + 1)
                if out:
                    norm_3(g - 1)
                    rows_hi(g - 1, 1 - par, b - 1 + par)
                if attn:
                    whi(g * PIECES + (A_PIECES + 2), par, b * PIECES + ((A_PIECES + 3 * par + 2) // 2))
                if nxt:
                    evac_q(g + 1, 1 - par)
                if attn:
                    for c in range(NCH):
                        exps(g, 1, c)
                if nxt:
                    evac_m(g + 1)
                if out:
                    evac_t3(g - 1)

            act.wait_ge(s["a_x1"], 16)
            act.wait_ge(s["rsq_r"], 4)
            for j in range(GT):
                norm_q(0, j, True)
            evac_t(0)
            evac_q(0, 0)
            evac_m(0)
            act.wait_ge(s["v_out"], 16 * B * DC)
            act.wait_ge(s["bex_ready"], 1)
            body(0, 0, 0, False, False)
            body(1, 0, 1, log=False)
            with act.Fori(1, B - 1) as b:
                body(b * 2, b, 0)
                body(b * 2 + 1, b, 1)
            body(GROUPS - 2, B - 1, 0)
            body(GROUPS - 1, B - 1, 1, nxt=False)
            body(GROUPS, B, 0, attn=False, nxt=False)
            pair_exp(GROUPS - 1)

            def c_tanh(n, q):
                act.wait_ge(s["cg_r"], n + 1)
                act.activation(CT[:, q], CG[:, q], ACT.Tanh, scale=ALPHA / 2).then_inc(s["ctanh_r"], 1)

            def c_gh(n, q):
                act.wait_ge(s["ctg_mm"], n + 1)
                act.activation(GH[:, q].rearrange("p c t -> p (c t)"), GTP[q][:, 0:E], ACT.Copy)\
                    .then_inc(s["cgh_r"], 1)

            def c_y(n, q, t, first=False):
                act.wait_ge(s["cd_mm"], n + 1)
                if not first:
                    act.wait_ge(YSC[q], 16 * t)
                act.activation(CY[:, q], YP[q][:, 0:D], ACT.Copy, scale=1.0 / YS).then_inc(s["cy_r"], 1)

            act.wait_ge(s["pad_r"], 2)
            c_tanh(0, 0)
            c_tanh(1, 1)
            c_gh(0, 0)
            c_tanh(2, 0)
            c_gh(1, 1)
            c_y(0, 0, 0, True)
            c_tanh(3, 1)
            c_gh(2, 0)
            c_y(1, 1, 0, True)
            with act.Fori(0, (NSLOT - 5) // 2) as t:
                c_tanh(t * 2 + 4, 0)
                c_gh(t * 2 + 3, 1)
                c_y(t * 2 + 2, 0, t + 1)
                c_tanh(t * 2 + 5, 1)
                c_gh(t * 2 + 4, 0)
                c_y(t * 2 + 3, 1, t + 1)
            c_tanh(NSLOT - 1, 0)
            c_gh(NSLOT - 2, 1)
            c_y(NSLOT - 3, 0, (NSLOT - 3) // 2)
            c_gh(NSLOT - 1, 0)
            c_y(NSLOT - 2, 1, (NSLOT - 3) // 2)
            c_y(NSLOT - 1, 0, (NSLOT - 1) // 2)

        @block.tensor
        def _(pe):
            pe.wait_ge(s["consts_ready"], 1)
            pe.wait_ge(s["cst_in"], 16)
            pe.wait_ge(s["kvc_in"], 16)
            for m in range(DC):
                for c in range(DC):
                    mm = pe.matmul(WK[m][:, 0:B * KEYS], KVC[:, Q_WK + c * D + m * P:Q_WK + c * D + (m + 1) * P],
                                   KVC[:, Q_CTX + c * B * KEYS:Q_CTX + (c + 1) * B * KEYS],
                                   start=(c == 0), stop=(c == DC - 1))
                mm.then_inc(s["k_mm"], 1)
            for kv in range(2):
                for hh in range(2):
                    for c in range(DC):
                        mm = pe.matmul(MXB[S * hh:S * hh + S, 0, kv:kv + 1],
                                       CST[:, C_WKV + c * 2 * S + kv * S:C_WKV + c * 2 * S + kv * S + S],
                                       CST[:, C_LNB + c:C_LNB + c + 1], start=(c == 0), stop=(c == DC - 1))
            mm.then_inc(s["kv_bias_mm"], 1)
            for b in range(B):
                v = [NUM, DEN][b % 2]
                if b >= 2:
                    pe.wait_ge(s["v_sb"], b - 1)
                for c in range(DC):
                    at = Q_CTX + c * B * KEYS + b * KEYS
                    mm = pe.matmul(v[0:KEYS, 0:D], KVC[:, at:at + KEYS], KVC[:, Q_WV + c * D:Q_WV + (c + 1) * D],
                                   start=(c == 0), stop=(c == DC - 1))
                mm.then_inc(s["v_mm"], 1)

            pe.wait_ge(s["kv_bias_ready"], 1)
            pe.wait_ge(s["v_sb"], B)
            pe.wait_ge(s["wkv_ready"], 1)
            pe.wait_ge(s["k_ready"], DC)
            pe.wait_ge(s["wsh_done"], 1)
            for p in range(2):
                for k in range(16):
                    pe.wait_ge(s["a_xn"], 16 * p + k + 1)
                    if k >= 2:
                        pe.wait_ge(s["a_xnt"], 16 * p + k - 1)
                    elif p:
                        pe.wait_ge(s["a_xst"], 16 * p)
                    for c in range(DC):
                        mm = pe.transpose(TRA[k % 2][:, c * P:(c + 1) * P], XN[:, k, c * P:(c + 1) * P], ID32[:, :])
                    mm.then_inc(s["a_t1"], 1)
                pe.wait_ge(s["a_xnt"], 16 * (p + 1))
                for n, k in enumerate(ORDER):
                    o = k // TPB * TPB + (k + SHIFT_TILES) % TPB
                    if n >= 2 or p:
                        pe.wait_ge(s["a_xs"], 16 * p + n - 1)
                    for c in range(DC):
                        mm = pe.matmul(SHA[n % 2][:, 0:D], XNT[:, c, o * P:(o + 1) * P], cst_w(C_WSH, D, c),
                                       start=(c == 0), stop=(c == DC - 1))
                    mm.then_inc(s["a_sh"], 1)
                for h in range(2):
                    for n, k in enumerate(HALF_TILES[h]):
                        pe.wait_ge(s["a_xn2"], 16 * p + 8 * h + n + 1)
                        if 8 * h + n >= 2:
                            pe.wait_ge(s["a_xst"], 16 * p + 8 * h + n - 1)
                        for c in range(DC):
                            mm = pe.transpose(TRA[n % 2][:, c * P:(c + 1) * P], XN[:, k, c * P:(c + 1) * P],
                                              ID32[:, :])
                        mm.then_inc(s["a_t2"], 1)
                    pe.wait_ge(s["a_xst"], 16 * p + 8 * (h + 1))
                    if p or h:
                        pe.wait_ge(s["a_wkv"], 2 * p + h)
                        pe.wait_ge(s["a_tanh"], 2 * p + h)
                    for kv in range(2):
                        for c in range(DC):
                            for bb in range(2):
                                mm = pe.matmul(KVA[kv][S * bb:S * bb + S, :],
                                               CST[:, C_WKV + c * 2 * S + kv * S:C_WKV + c * 2 * S + kv * S + S],
                                               XST[:, h, c, bb * GTOK:(bb + 1) * GTOK],
                                               start=(c == 0), stop=(c == DC - 1))
                    mm.then_inc(s["a_kv"], 1)
                for h in range(2):
                    pe.wait_ge(s["a_scan"], 2 * p + h + 1)
                    for r in range(4):
                        u = 8 * p + 4 * h + r
                        bb = r // 2
                        if u >= 2:
                            pe.wait_ge(s["a_x1"], u - 1)
                        for q in range(2):
                            t0 = (2 * (r % 2) + q) * P
                            mm = pe.matmul(OUA[r % 2][:, q * D:(q + 1) * D], ST[S * bb:S * bb + S, h, t0:t0 + P],
                                           CST[S * bb:S * bb + S, C_WOUT:C_WOUT + D], start=True, stop=True)
                        mm.then_inc(s["a_out"], 1)

            def turn(src, ready, g, mm_sem):
                for r in range(2):
                    pe.wait_ge(ready, 4 * g + 2 * (r + 1))
                    for j in range(2):
                        for c in range(DC):
                            at = (j * DC + c) * P
                            mm = pe.transpose(WK[r][:, at:at + P], src[:, 2 * r + j, c * P:(c + 1) * P], ID32[:, :])
                    mm.then_inc(mm_sem, 1)

            def s1_turn(g):
                if isinstance(g, int) and g == 1:
                    pe.wait_ge(s["ql_r"], 2)
                elif not (isinstance(g, int) and g == 0):
                    pe.wait_ge(s["x2_r"], 2 * (g - 1))
                turn(XQ, s["xq_r"], g, s["t_mm"])

            def s1_q(g):
                pe.wait_ge(s["xqT_r"], 2 * g + 2)
                for m in range(DC):
                    for c in range(DC):
                        mm = pe.matmul(WK[m][:, :], CST[:, C_WQ + c * D + m * P:C_WQ + c * D + (m + 1) * P],
                                       XQT[:, c, :], start=(c == 0), stop=(c == DC - 1))
                    mm.then_inc(s["q_mm"], 1)

            def s1_max(g, par, b, bp):
                for u in range(16):
                    j, m, half = u // 4, u // 2 % 2, u % 2
                    if u == 0:
                        pe.wait_ge(s["qh_r"], 2 * g + 2)
                        pe.wait_ge(s["kcur_r"], b + 1)
                    if not (isinstance(g, int) and g == 0 and u < 2):
                        pe.wait_ge(s["mx_r"], 16 * g + (u - 1))
                    pe.matmul(MXB[:, half, 0:GK // 2], QH[:, par, m, j * P:(j + 1) * P],
                              KCUR[:, ds(bp, 1), m, 0, 4 * half:4 * half + 4].rearrange("p a h k -> p (a h k)"),
                              start=True, stop=True).then_inc(s["mx_mm"], 1)
                    yield

            def s1_mt(g):
                pe.wait_ge(s["mh_r"], g + 1)
                for j in range(GT):
                    mm = pe.transpose(MTP[j // 2][:, j % 2 * P:(j % 2 + 1) * P], MH[:, j, :], ID16[:, :])
                mm.then_inc(s["mt_mm"], 1)

            def s2_scores(g, par, bp, m, c, units=iter(())):
                if m == 0 and c == 0:
                    pe.wait_ge(s["mT_r"], g + 1)
                    pe.wait_ge(s["ql_r"], 2 * g + 2)
                rows = P if c < NCH - 1 else LAST
                if not (isinstance(g, int) and g == 0 and m == 0 and c < 2):
                    pe.wait_ge(s["exp_r"], g * (2 * NCH) + (m * NCH + c - 1))
                o = SC[(m * NCH + c) % 2][0:rows, :]
                kk = KCUR[:, ds(bp, 1), m].rearrange("p a v h k -> p (a v) (h k)")
                kh, kl = kk[:, 0, c * P:c * P + rows], kk[:, 1, c * P:c * P + rows]
                ind = IND[:, m * GK + c * P:m * GK + c * P + rows]
                pe.matmul(o, ind, MT[:, :], start=True, stop=False)
                next(units, None)
                pe.matmul(o, kh, QL[:, par, m], start=False, stop=False)
                next(units, None)
                pe.matmul(o, kl, QH[:, par, m], start=False, stop=False)
                next(units, None)
                pe.matmul(o, kh, QH[:, par, m], start=False, stop=True).then_inc(s["sc_mm"], 1)
                next(units, None)

            def s2_pv(g, b, m, units=iter(())):
                pe.wait_ge(s["exp_r"], g * (2 * NCH) + (m + 1) * NCH)
                if m == 0:
                    pe.wait_ge(s["vcur_r"], b + 1)
                if not (isinstance(g, int) and g == 0 and m == 0):
                    pe.wait_ge(s["at_r"], 2 * g + m)
                for o, w in ((NUM, VCUR[:, m]), (DEN, MV)):
                    for v in range(2):
                        for j in range(4):
                            rows = P if j + v < NCH - 1 else LAST
                            mm = pe.matmul(o[32 * j:32 * j + 32, :],
                                           w[0:rows, j + v, v].rearrange("p a e -> p (a e)"),
                                           PB[0:rows, j + v, :], start=(v == 0), stop=(v == 1))
                        if (o, v) != (DEN, 1):
                            next(units, None)
                mm.then_inc(s["pv_mm"], 1)
                for _ in units:
                    pass

            def s2_out(g):
                pe.wait_ge(s["at_r"], 2 * g + 2)
                if isinstance(g, int) and g == 0:
                    pe.wait_ge(s["ql_r"], 4)
                else:
                    pe.wait_ge(s["x3T_r"], 2 * g)
                for j in range(GT):
                    for c in range(DC):
                        mm = pe.matmul(WK[j // 2][:, (j % 2) * D:(j % 2 + 1) * D], AT[:, c, j * P:(j + 1) * P],
                                       cst_w(C_WO, D, c), start=(c == 0), stop=(c == DC - 1))
                    if j % 2:
                        mm.then_inc(s["out_mm"], 1)

            def s3_turn(g, nxt):
                if nxt:
                    pe.wait_ge(s["ql_r"], 2 * g + 6)
                turn(X3, s["xn3_r"], g, s["t3_mm"])

            def s3_logits(g):
                pe.wait_ge(s["x3T_r"], 2 * g + 2)
                for j in range(GT):
                    for c in range(DC):
                        mm = pe.matmul(LGP[:, j * NEXP:(j + 1) * NEXP], X3T[:, c, j * P:(j + 1) * P],
                                       cst_w(C_WG, NEXP, c), start=(c == 0), stop=(c == DC - 1))
                mm.then_inc(s["lg_mm"], 1)

            def s3_prefix(g):
                pe.wait_ge(s["ms_r"], g + 1)
                ms = MS16[:, :, :].rearrange("p j e -> p (j e)")
                pe.matmul(UPP, UP16[:, :], ms, start=True, stop=True)
                pe.matmul(ONP, ON16[:, :], ms, start=True, stop=True).then_inc(s["px_mm"], 1)

            def body(g, b, par, bp, b1, bp1, out=True, log=True, attn=True, nxt=True):
                if attn:
                    for c in range(NCH):
                        s2_scores(g, par, bp, 0, c)
                if log:
                    if not nxt:
                        pe.wait_ge(s["run_s"], 5 * (g - 2))
                    s3_logits(g - 2)
                if out:
                    s2_out(g - 1)
                if nxt:
                    s1_turn(g + 1)
                if log:
                    s3_prefix(g - 2)
                if attn:
                    s2_pv(g, b, 0)
                if nxt:
                    s1_q(g + 1)
                if attn:
                    if log and nxt:
                        pe.wait_ge(s["run_s"], 5 * (g - 1))
                    units = s1_max(g + 1, 1 - par, b1, bp1) if nxt else iter(())
                    for c in range(NCH):
                        s2_scores(g, par, bp, 1, c, units if c >= 1 else iter(()))
                    s2_pv(g, b, 1, units)
                if nxt:
                    s1_mt(g + 1)
                if out:
                    s3_turn(g - 1, nxt)

            pe.wait_ge(s["a_x1"], 16)
            s1_turn(0)
            s1_q(0)
            for _ in s1_max(0, 0, 0, 0):
                pass
            s1_mt(0)
            body(0, 0, 0, 0, 0, 0, False, False)
            body(1, 0, 1, 0, 1, 1, log=False)
            with pe.Fori(1, B - 1) as b:
                body(b * 2, b, 0, b % 2, b, b % 2)
                body(b * 2 + 1, b, 1, b % 2, b + 1, (b + 1) % 2)
            body(GROUPS - 2, B - 1, 0, 1, B - 1, 1)
            body(GROUPS - 1, B - 1, 1, 1, None, None, nxt=False)
            body(GROUPS, None, 0, None, None, None, attn=False, nxt=False)
            pe.wait_ge(s["run_s"], 5 * (GROUPS - 1))
            s3_logits(GROUPS - 1)
            s3_prefix(GROUPS - 1)

            pe.wait_ge(s["c_tabe"], 19)
            pe.wait_ge(s["run_s"], 5 * GROUPS)
            pe.matmul(NUM[:, 0:P], ON16[:, :], DIAG, start=True, stop=True).then_inc(s["c_mm"], 1)
            pe.transpose(WA[0:1, 0:P], CW[:, 0, 0:1], ID32[:, :])
            pe.transpose(WA[0:1, P:2 * P], CW[:, 0, 1:2], ID32[:, :]).then_inc(s["c_mm"], 1)
            pe.transpose(WB[0:2 * NEXP, 0:P], CW[:, 8:10].rearrange("p a e -> p (a e)"), ID32[:, :])\
                .then_inc(s["c_mm"], 1)
            pe.wait_ge(s["c_cp"], 2)
            pe.wait_ge(s["w_split"], NPIECE)
            pe.wait_ge(s["bex_ready"], 1)

            def c_turn(n, q, t):
                pe.wait_ge(RINS[q], 16 * (t + 1))
                if not isinstance(n, int) or n >= 2:
                    pe.wait_ge(s["cxt_r"], n - 1)
                rows = RIN[:, q, 0:D].bitcast(F16)
                for v in range(4):
                    mm = pe.transpose(XTP[q][:, v * P:(v + 1) * P], rows[:, v * P:(v + 1) * P], ID16[:, :])
                mm.then_inc(s["ct_mm"], 1)

            def w_at(e, at, n):
                return w_flat[:, ds(e * WEX + at, n)]

            def expert(n):
                return pe.value_load(TAB[0:1, ds(n, 1)], min_val=0, max_val=NEXP - 1)

            def c_gu(n, q):
                e = expert(n)
                pe.wait_ge(s["cob_r"], n + 1)
                if not isinstance(n, int) or n >= 2:
                    pe.wait_ge(s["cu_r"], n - 1)
                    pe.wait_ge(s["cg_r"], n - 1)
                pe.matmul(GUP[q], OHB[0:2 * NEXP, q, 0], BEX[:, 0:F], start=True, stop=False)
                pe.wait_ge(s["cxt_r"], n + 1)
                for c in range(DC):
                    pe.matmul(GUP[q], XTS[:, q, c], w_at(e, c * 2 * PW + LOW, F), start=False, stop=False)
                    pe.matmul(GUP[q], XTS[:, q, c], w_at(e, c * 2 * PW, F), start=False, stop=False)
                for c in range(DC):
                    mm = pe.matmul(GUP[q], XTS[:, q, 2 + c], w_at(e, c * 2 * PW, F), start=False,
                                   stop=(c == DC - 1))
                mm.then_inc(s["cgu_mm"], 1)

            def c_tg(n, q):
                pe.wait_ge(s["cgd_r"], n + 1)
                if not isinstance(n, int) or n >= 2:
                    pe.wait_ge(s["cgl_r"], n - 1)
                for c in range(DC):
                    mm = pe.transpose(GTP[q][:, c * P:(c + 1) * P], CGD[:, q, c * P:(c + 1) * P], ID32[:, :])
                mm.then_inc(s["ctg_mm"], 1)

            def c_down(n, q):
                e = expert(n)
                pe.wait_ge(s["cod_r"], n + 1)
                if not isinstance(n, int) or n >= 2:
                    pe.wait_ge(s["cy_r"], n - 1)
                pe.matmul(YP[q][:, 0:D], OHB[0:2 * NEXP, q, 1], BEX[:, F:F + E], start=True, stop=False)
                pe.wait_ge(s["cgl_r"], n + 1)
                for c in range(DC):
                    pe.matmul(YP[q][:, 0:D], GH[:, q, c], w_at(e, W_DOWN + LOW + c * E, E), start=False, stop=False)
                    pe.matmul(YP[q][:, 0:D], GH[:, q, c], w_at(e, W_DOWN + c * E, E), start=False, stop=False)
                for c in range(DC):
                    mm = pe.matmul(YP[q][:, 0:D], GL[:, q, c], w_at(e, W_DOWN + c * E, E), start=False,
                                   stop=(c == DC - 1))
                mm.then_inc(s["cd_mm"], 1)

            c_turn(0, 0, 0)
            c_turn(1, 1, 0)
            c_gu(0, 0)
            c_turn(2, 0, 1)
            c_gu(1, 1)
            c_tg(0, 0)

            def steps(t):
                c_turn(t * 2 + 3, 1, t + 1)
                c_gu(t * 2 + 2, 0)
                c_tg(t * 2 + 1, 1)
                c_down(t * 2, 0)
                c_turn(t * 2 + 4, 0, t + 2)
                c_gu(t * 2 + 3, 1)
                c_tg(t * 2 + 2, 0)
                c_down(t * 2 + 1, 1)

            steps(0)
            with pe.Fori(1, (NSLOT - 3) // 2) as t:
                steps(t)
            c_gu(NSLOT - 1, 0)
            c_tg(NSLOT - 2, 1)
            c_down(NSLOT - 3, 0)
            c_tg(NSLOT - 1, 0)
            c_down(NSLOT - 2, 1)
            c_down(NSLOT - 1, 0)

        @block.vector
        def _(dve):
            dve.wait_ge(s["gate_tanh"], 1)
            gate = CST[:, C_GATE:C_GATE + D]
            for c in range(DC):
                w = cst_w(C_WSH, D, c)
                dve.scalar_tensor_tensor(out=w, in0=gate, scalar=1.0, in1=w, op0=ALU.add, op1=ALU.mult)\
                    .then_inc(s["wsh_ready"], 1)
            dve.wait_ge(s["wsh_ready"], 2)
            for c in range(DC):
                w = cst_w(C_WSH, D, c)
                dve.tensor_scalar(w, w, 0.5, None, ALU.mult)
            dve.tensor_scalar(gate, gate, -0.5, 0.5, ALU.mult, ALU.add).then_inc(s["wsh_done"], 1)
            dve.wait_ge(s["etf_exp"], 2)
            dve.tensor_scalar(SMALL[:, 2:4], CST[:, C_BK:C_BK + DC], 0.25, None, ALU.mult)
            dve.tensor_scalar(SMALL[:, 4:5], SMALL[:, 1:2], -0.5, None, ALU.mult).then_inc(s["small_ready"], 1)
            dve.wait_ge(s["small_ready"], 1)
            dve.wait_ge(s["kv_bias_mm"], 1)
            dve.tensor_scalar(SMALL[:, 5:6], MXB[:, 0, 0:1], 0.5, None, ALU.mult)
            dve.tensor_copy(SMALL[:, 6:7], MXB[:, 0, 1:2]).then_inc(s["kv_bias_ready"], 1)
            for c in range(DC):
                w = cst_w(C_WKV, 2 * S, c)
                ins = dve.tensor_scalar(w, w, CST[:, C_LNW + c:C_LNW + c + 1], None, ALU.mult)
            ins.then_inc(s["wkv_ready"], 1)
            for b in range(B):
                dve.wait_ge(s["v_mm"], b + 1)
                v = [NUM, DEN][b % 2]
                dve.tensor_tensor(VSB[:, b], v[0:KEYS, 0:D], KVC[0:KEYS, Q_BV:Q_BV + D], ALU.add)\
                    .then_inc(s["v_sb"], 1)
            for m in range(DC):
                dve.wait_ge(s["k_hi"], m + 1)
                if m:
                    dve.wait_ge(s["k_ready"], m)
                dve.tensor_scalar(KTMP, WK[m][:, 0:B * KEYS], 0.25, SMALL[:, 2 + m:3 + m], ALU.mult, ALU.add)\
                    .then_inc(s["k_tmp"], 1)
                dve.wait_ge(s["k_tmp"], m + 1)
                dve.tensor_tensor(KRAW[:, 1, m].rearrange("p b k -> p (b k)"), KTMP,
                                  KRAW[:, 0, m].rearrange("p b k -> p (b k)"), ALU.subtract).then_inc(s["k_ready"], 1)
            dve.wait_ge(s["bex_in"], 16)
            br = BRAW[0:2 * NEXP, 0:F + E]
            dve.tensor_scalar(br[:, 0:F], br[:, 0:F], GUS / ONE, None, ALU.mult)
            dve.tensor_scalar(br[:, F:F + E], br[:, F:F + E], YS / ONE, None, ALU.mult).then_inc(s["bex_s"], 1)
            dve.wait_ge(s["bex_s"], 1)
            dve.tensor_copy(BEX[:, :], br).then_inc(s["bex_s"], 1)
            dve.wait_ge(s["bex_s"], 2)
            dve.tensor_tensor(br, br, BEX[:, :], ALU.subtract).then_inc(s["bex_s"], 1)
            dve.wait_ge(s["bex_s"], 3)
            dve.wait_ge(s["consts_ready"], 1)
            mhi, mlo = SMALL[0:2 * NEXP, 8:9], SMALL[0:2 * NEXP, 9:10]
            dve.tensor_copy(mhi, MK[0:2 * NEXP, 0:1])
            dve.tensor_copy(mlo, MK[0:2 * NEXP, 1:2]).then_inc(s["bex_s"], 1)
            dve.wait_ge(s["bex_s"], 4)
            dve.tensor_scalar(br, br, mlo, None, ALU.mult).then_inc(s["bex_s"], 1)
            dve.wait_ge(s["bex_s"], 5)
            dve.scalar_tensor_tensor(out=BEX[:, :], in0=BEX[:, :], scalar=mhi, in1=br, op0=ALU.mult, op1=ALU.add)\
                .then_inc(s["bex_ready"], 1)
            dve.wait_ge(s["k_ready"], DC)

            def vcur(b):
                dve.wait_ge(s["v_in"], (b + 1) * (32 * DC))
                for m in range(DC):
                    for n in range(2):
                        rows, c0, c1 = (P, 0, NCH - 1) if n == 0 else (LAST, NCH - 1, NCH)
                        vf = VFLAT[0:rows, m, c0:c1, :]
                        nn = c1 - c0
                        ins = dve.tensor_tensor(
                            VCUR[0:rows, m, c0:c1].rearrange("p n v a e -> p n (v a) e"),
                            vf.unsqueeze(2).broadcast_to([rows, nn, 4, HD]),
                            MV[0:rows, c0:c1].rearrange("p n v a e -> p n (v a) e"), ALU.mult)
                ins.then_inc(s["vcur_r"], 1)

            for p in range(2):
                dve.wait_ge(s["x_in"], 32 * (p + 1))
                if p:
                    dve.wait_ge(s["a_rs2"], 2 * p)
                    dve.wait_ge(s["vaq"], p)
                for q in range(2):
                    for k in range(8 * q, 8 * q + 8):
                        ins = dve.bn_stats(STAT[:, k, :], X[:, 16 * p + k, :])
                    ins.then_inc(s["a_stat"], 1)
                for q in range(2):
                    dve.wait_ge(s["a_stat"], 2 * p + q + 1)
                    for k in range(8 * q, 8 * q + 8):
                        ins = dve.bn_aggr(MVA[:, k, :], STAT[:, k, :])
                    ins.then_inc(s["a_aggr"], 1)
                if p:
                    dve.wait_ge(s["a_t2"], 16 * p)
                for q in range(2):
                    dve.wait_ge(s["a_rs"], 2 * p + q + 1)
                    for k in range(8 * q, 8 * q + 8):
                        dve.tensor_scalar(XN[:, k, :], X[:, 16 * p + k, :], MVA[:, k, 0:1], RS[:, k:k + 1],
                                          ALU.subtract, ALU.mult).then_inc(s["a_xn"], 1)
                for h in range(2):
                    for n, k in enumerate(HALF_TILES[h]):
                        u = 16 * p + 8 * h + n
                        dve.wait_ge(s["a_sh"], u + 1)
                        dve.wait_ge(s["a_xg"], u + 1)
                        dve.tensor_tensor(XN[:, k, :], XN[:, k, :], SHA[n % 2][:, 0:D], ALU.add)\
                            .then_inc(s["a_xs"], 1)
                        if n:
                            dve.wait_ge(s["a_xs"], u)
                            dve.bn_stats(STAT[:, 8 * h + n - 1, :], XN[:, HALF_TILES[h][n - 1], :])
                    dve.wait_ge(s["a_xs"], 16 * p + 8 * h + 8)
                    dve.bn_stats(STAT[:, 8 * h + 7, :], XN[:, HALF_TILES[h][7], :]).then_inc(s["a_stat2"], 1)
                    dve.wait_ge(s["a_stat2"], 2 * p + h + 1)
                    for n in range(8 * h, 8 * h + 8):
                        ins = dve.bn_aggr(MVA[:, n, :], STAT[:, n, :])
                    ins.then_inc(s["a_aggr2"], 1)
                for h in range(2):
                    dve.wait_ge(s["a_rs2"], 2 * p + h + 1)
                    for n, k in enumerate(HALF_TILES[h]):
                        dve.tensor_scalar(XN[:, k, :], XN[:, k, :], MVA[:, 8 * h + n, 0:1],
                                          RS[:, 8 * h + n:8 * h + n + 1], ALU.subtract, ALU.mult)\
                            .then_inc(s["a_xn2"], 1)
                for h in range(2):
                    dve.wait_ge(s["a_exp"], 2 * p + h + 1)
                    dve.scalar_tensor_tensor(out=TW, in0=KVA[1][:, :], scalar=SMALL[:, 6:7], in1=TW,
                                             op0=ALU.add, op1=ALU.mult).then_inc(s["a_wkv"], 1)
                    dve.wait_ge(s["a_wkv"], 2 * p + h + 1)
                    if p:
                        dve.wait_ge(s["a_out"], 4 * (2 * p + h - 1))
                    if h:
                        dve.wait_ge(s["a_scan"], 2 * p + 1)
                    dve.tensor_tensor_scan(ST[:, h, :], SMALL[:, 0:1].broadcast_to([P, GTOK]), TW,
                                           ST[:, 0, GTOK - 1:GTOK] if h else 0.0, ALU.mult, ALU.add)\
                        .then_inc(s["a_scan"], 1)
                for h in range(2):
                    for r in range(4):
                        u = 8 * p + 4 * h + r
                        i = 16 * p + (r // 2) * TPB + 4 * h + 2 * (r % 2)
                        dve.wait_ge(s["a_out"], u + 1)
                        xt = X[:, i:i + 2, :].rearrange("p a d -> p (a d)")
                        ins = dve.tensor_tensor(xt, xt, OUA[r % 2][:, :], ALU.add).then_inc(s["a_x1"], 1)
                dve.wait_ge(s["a_x1"], 8 * (p + 1))
                for k in range(16):
                    ins = dve.bn_stats(STAT[:, k, :], X[:, 16 * p + k, :])
                ins.then_inc(s["stq"], 1)
                dve.wait_ge(s["stq"], p + 1)
                for k in range(16):
                    ins = dve.bn_aggr(MVQ[:, 16 * p + k, :], STAT[:, k, :])
                ins.then_inc(s["vaq"], 1)

            def s1_ql(g, par):
                for m in range(DC):
                    dve.wait_ge(s["qh_r"], 2 * g + m + 1)
                    dve.scalar_tensor_tensor(out=QL[:, par, m], in0=WK[m][:, :], scalar=CST[:, C_BQ + m:C_BQ + m + 1],
                                             in1=QH[:, par, m], op0=ALU.add, op1=ALU.subtract).then_inc(s["ql_r"], 1)

            def s1_max(g):
                for u in range(16):
                    j, m, half = u // 4, u // 2 % 2, u % 2
                    dve.wait_ge(s["mx_mm"], 16 * g + (u + 1))
                    dve.tensor_reduce(MX[:, j, m * HG + 4 * half:m * HG + 4 * half + 4],
                                      MXB[:, half, 0:GK // 2].rearrange("p (h k) -> p h k", k=KEYS),
                                      AX.X, ALU.max).then_inc(s["mx_r"], 1)

            def s1_mh(g):
                dve.wait_ge(s["mx_r"], 16 * g + 16)
                dve.tensor_scalar(MH[:, :, 0:HEADS], MX[:, :, :], -1.0, None, ALU.mult).then_inc(s["mh_s"], 1)
                dve.wait_ge(s["mh_s"], g + 1)
                dve.scalar_tensor_tensor(out=MH[:, :, HEADS:2 * HEADS], in0=MX[:, :, :], scalar=-1.0,
                                         in1=MH[:, :, 0:HEADS], op0=ALU.mult, op1=ALU.subtract)\
                    .then_inc(s["mh_r"], 1)

            def s2_attn(g, m):
                dve.wait_ge(s["pv_mm"], 2 * g + (m + 1))
                dve.reciprocal(AT[:, m], DEN[:, :]).then_inc(s["rec_s"], 1)
                dve.wait_ge(s["rec_s"], 2 * g + (m + 1))
                dve.tensor_tensor(AT[:, m], AT[:, m], NUM[:, :], ALU.mult).then_inc(s["at_r"], 1)

            def s2_x2(g):
                for r in range(2):
                    dve.wait_ge(s["out_mm"], 2 * g + (r + 1))
                    if r == 0:
                        dve.wait_ge(s["xb_r"], g + 1)
                    xt = X[:, ds(g * GT + 2 * r, 2), :].rearrange("p a d -> p (a d)")
                    dve.tensor_tensor(xt, xt, WK[r][:, :], ALU.add).then_inc(s["x2_r"], 1)

            def s3_stats(g):
                dve.wait_ge(s["x2_r"], 2 * g + 2).then_inc(s["dve_past"], 1)
                for j in range(GT):
                    ins = dve.bn_stats(STAT3[:, j, :], X[:, ds(g * GT + j, 1), :].rearrange("p a d -> p (a d)"))
                ins.then_inc(s["st3"], 1)
                dve.wait_ge(s["st3"], g + 1).then_inc(s["dve_past"], 1)
                if not (isinstance(g, int) and g == 0):
                    dve.wait_ge(s["rs3_r"], g).then_inc(s["dve_past"], 1)
                for j in range(GT):
                    ins = dve.bn_aggr(MVA3[:, j, :], STAT3[:, j, :])
                ins.then_inc(s["va3"], 1)

            def s3_logits(g, par, k):
                dve.wait_ge(s["lg_mm"], g + 1)
                dve.scalar_tensor_tensor(
                    out=LG[:, :, :], in0=LGP.rearrange("p (j e) -> p j e", j=GT), scalar=1.0 / XSC,
                    in1=CST[:, C_BG:C_BG + NEXP].unsqueeze(1).broadcast_to([P, GT, NEXP]),
                    op0=ALU.mult, op1=ALU.add).then_inc(s["lg_r"], 1)
                dve.wait_ge(s["lg_r"], g + 1).then_inc(s["dve_past"], 1)
                for j in range(GT):
                    ins = dve.max(M8[:, j, :], LG[:, j, :])
                ins.then_inc(s["top_r"], 1)
                dve.wait_ge(s["top_r"], g + 1)
                dve.tensor_tensor(RD[:, 0, :], M8[:, :, 1], M8[:, :, 0], ALU.subtract).then_inc(s["rd_s"], 1)
                for j in range(GT):
                    ins = dve.max_index(I8[:, j, :], M8[:, j, :], LG[:, j, :])
                ins.then_inc(s["ix_r"], 1)
                dve.wait_ge(s["ix_r"], g + 1)
                dve.tensor_copy(IF[:, :, :], I8[:, :, 0:TOPK]).then_inc(s["if_r"], 1)
                dve.wait_ge(s["if_r"], g + 1)
                for q in range(TOPK):
                    ins = dve.tensor_tensor(MS[:, q], IOTA[:, :].unsqueeze(1).broadcast_to([P, GT, NEXP]),
                                            IF[:, :, q:q + 1].broadcast_to([P, GT, NEXP]), ALU.is_equal)
                ins.then_inc(s["ms_s"], 1)
                dve.wait_ge(s["ms_s"], g + 1)
                dve.tensor_tensor(MS16[:, :, :], MS[:, 0], MS[:, 1], ALU.add).then_inc(s["ms_r"], 1)
                if not (isinstance(k, int) and k == 0):
                    dve.wait_ge(SCT[par], k * (16 * TOPK * GT))
                dve.tensor_copy(RB[:, par, :, D], TOKF[:, ds(g * GT, GT)])
                dve.tensor_copy(RB[:, par, :, D + 1], IF[:, :, 0])

            def s3_slots(g, par):
                dve.wait_ge(s["rd_e"], g + 1)
                dve.tensor_scalar(RD[:, 2, :], RD[:, 1, :], 1.0, None, ALU.add).then_inc(s["rd_r"], 1)
                dve.wait_ge(s["rd_r"], 2 * g + 1)
                dve.reciprocal(RW[:, 0, ds(g * GT, GT)], RD[:, 2, :]).then_inc(s["rd_r"], 1)
                dve.wait_ge(s["rd_r"], 2 * g + 2)
                dve.tensor_tensor(RW[:, 1, ds(g * GT, GT)], RD[:, 1, :], RW[:, 0, ds(g * GT, GT)], ALU.mult)
                dve.wait_ge(s["px_mm"], g + 1)
                for j in range(GT):
                    dve.tensor_tensor(RUN[:, j + 1, :], RUN[:, j, :], ONP[:, j * NEXP:(j + 1) * NEXP], ALU.add)\
                        .then_inc(s["run_s"], 1)
                    dve.wait_ge(s["run_s"], 5 * g + (j + 1))
                dve.tensor_tensor(LG[:, :, :], RUN[:, 0:GT, :], UPP.rearrange("p (j e) -> p j e", j=GT),
                                  ALU.add).then_inc(s["run_s"], 1)
                dve.wait_ge(s["run_s"], 5 * g + 5)
                dve.tensor_copy(RUN[:, 0, :], RUN[:, GT, :]).then_inc(s["pos_s"], 1)
                for q in range(TOPK):
                    ins = dve.tensor_tensor(SL[:, q], MS[:, q], LG[:, :, :], ALU.mult)
                ins.then_inc(s["sl_s"], 1)
                dve.wait_ge(s["sl_s"], g + 1)
                dve.tensor_reduce(SLF[:, :, :], SL[:, :, :, :], AX.X, ALU.add).then_inc(s["slf_s"], 1)
                dve.wait_ge(s["slf_s"], g + 1)
                dve.tensor_copy(SLOT[:, par], SLF[:, :, :]).then_inc(s["slot_r"], 1)

            def body(g, b, par, b1=None, out=True, log=True, attn=True, nxt=True):
                if log:
                    s3_logits(g - 2, par, b - 1)
                if out:
                    s2_x2(g - 1)
                    s3_stats(g - 1)
                if log:
                    s3_slots(g - 2, par)
                if attn:
                    s2_attn(g, 0)
                if nxt:
                    s1_ql(g + 1, 1 - par)
                    s1_max(g + 1)
                    s1_mh(g + 1)
                if b1 is not None:
                    dve.wait_ge(s["pv_mm"], 2 * g + 2)
                    vcur(b1)
                if attn:
                    s2_attn(g, 1)

            vcur(0)
            s1_ql(0, 0)
            s1_max(0)
            s1_mh(0)
            body(0, 0, 0, out=False, log=False)
            body(1, 0, 1, 1, log=False)
            with dve.Fori(1, B - 1) as b:
                body(b * 2, b, 0)
                body(b * 2 + 1, b, 1, b + 1)
            body(GROUPS - 2, B - 1, 0)
            body(GROUPS - 1, B - 1, 1, nxt=False)
            body(GROUPS, B, 0, attn=False, nxt=False)
            s3_logits(GROUPS - 1, 1, B - 1)
            s3_slots(GROUPS - 1, 1)

            dve.wait_ge(s["lo_r"], GROUPS)
            dve.wait_ge(s["pos_s"], GROUPS)
            dve.tensor_copy(RUNI, RUN[:, 0, :]).then_inc(s["c_tab"], 1)
            steps = [0]

            def link(ins):
                steps[0] += 1
                ins.then_inc(s["c_tabe"], 1)
                dve.wait_ge(s["c_tabe"], steps[0])

            cnt, nt, end, le, tmp = (CW[:, 1 + a] for a in range(5))
            link(dve.tensor_tensor(cnt, RUN[:, 0, :], ECAP[:, :], ALU.subtract))
            link(dve.tensor_scalar(CWI, cnt, float(P - 1), None, ALU.add))
            link(dve.tensor_scalar(CWI, CWI, 7, None, ALU.arith_shift_right))
            link(dve.tensor_copy(nt, CWI))
            link(dve.tensor_scalar(tmp, nt, 0.0, 1.0, ALU.mult, ALU.add))
            link(dve.tensor_tensor_scan(end, tmp, nt, 0.0, ALU.mult, ALU.add))
            pidx = CW[:, 7, 0:1]
            link(dve.tensor_copy(pidx, TOK[:, 0:1]))
            link(dve.tensor_scalar(le, end, pidx, None, ALU.is_le))
            link(dve.tensor_tensor(tmp, le, nt, ALU.mult))
            ei, done = CW[:, 6, 0:1], CW[:, 6, 1:2]
            link(dve.tensor_reduce(ei, le, AX.X, ALU.add))
            link(dve.tensor_reduce(done, tmp, AX.X, ALU.add))
            j_in = CW[:, 6, 2:3]
            link(dve.tensor_tensor(j_in, pidx, done, ALU.subtract))
            link(dve.tensor_scalar(j_in, j_in, float(P), None, ALU.mult))
            row = CW[:, 0, 1:2]
            link(dve.scalar_tensor_tensor(out=row, in0=ei, scalar=float(CAP), in1=j_in, op0=ALU.mult, op1=ALU.add))
            link(dve.tensor_scalar(row, row, float(NEXP * CAP), None, ALU.min))
            link(dve.tensor_scalar(CW[:, 0, 0:1], ei, float(NEXP - 1), None, ALU.min))
            link(dve.tensor_scalar(DIAG, ID16[:, :], CW[:, 0, 0:1], None, ALU.mult))
            for v in range(2):
                link(dve.tensor_scalar(CW[:, 8 + v], IOTA[:, :], CW[:, 0, 0:1], ONE, ALU.is_equal, ALU.mult))
            dve.wait_ge(s["c_mm"], 3)
            dve.tensor_copy(EXB, NUM[:, 0:P]).then_inc(s["eb_r"], 1)
            dve.tensor_copy(TAB[0:1, :], WA[0:1, 0:2 * P]).then_inc(s["c_cp"], 1)
            dve.tensor_copy(OHT[0:2 * NEXP], WB[0:2 * NEXP, 0:P]).then_inc(s["c_cp"], 1)
            dve.wait_ge(s["c_cp"], 2)

            def c_xt(n, q):
                dve.wait_ge(s["ct_mm"], n + 1)
                dve.tensor_copy(OHB[0:2 * NEXP, q, 0], OHT[0:2 * NEXP, ds(n, 1)].broadcast_to([2 * NEXP, P]))\
                    .then_inc(s["cob_r"], 1)
                dve.tensor_copy(XTS[:, q].rearrange("p v t -> p (v t)"), XTP[q]).then_inc(s["cxt_r"], 1)

            def c_gate(n, q):
                dve.wait_ge(s["cgu_mm"], n + 1)
                dve.tensor_scalar(CG[:, q], GUP[q][:, 0:E], 1.0 / GUS, LIMIT, ALU.mult, ALU.min)\
                    .then_inc(s["cg_r"], 1)
                dve.tensor_scalar(CU[:, q], GUP[q][:, E:F], LIMIT * GUS, -LIMIT * GUS, ALU.min, ALU.max)\
                    .then_inc(s["cu_r"], 1)

            def c_glu(n, q):
                dve.wait_ge(s["ctanh_r"], n + 1)
                dve.scalar_tensor_tensor(out=CT[:, q], in0=CT[:, q], scalar=1.0, in1=CG[:, q],
                                         op0=ALU.add, op1=ALU.mult).then_inc(s["ct1_r"], 1)
                dve.wait_ge(s["ct1_r"], n + 1)
                dve.wait_ge(s["cu_r"], n + 1)
                dve.scalar_tensor_tensor(out=CGD[:, q], in0=CU[:, q], scalar=GUS, in1=CT[:, q],
                                         op0=ALU.add, op1=ALU.mult).then_inc(s["cgd_r"], 1)

            def c_gl(n, q):
                dve.wait_ge(s["cgh_r"], n + 1)
                dve.tensor_copy(OHB[0:2 * NEXP, q, 1], OHT[0:2 * NEXP, ds(n, 1)].broadcast_to([2 * NEXP, P]))\
                    .then_inc(s["cod_r"], 1)
                dve.tensor_tensor(GL[:, q].rearrange("p c t -> p (c t)"), GTP[q][:, 0:E],
                                  GH[:, q].rearrange("p c t -> p (c t)"), ALU.subtract).then_inc(s["cgl_r"], 1)

            c_xt(0, 0)
            c_xt(1, 1)
            c_gate(0, 0)
            c_glu(0, 0)
            c_xt(2, 0)
            c_gate(1, 1)
            c_gl(0, 0)
            c_glu(1, 1)
            with dve.Fori(0, (NSLOT - 3) // 2) as t:
                c_xt(t * 2 + 3, 1)
                c_gate(t * 2 + 2, 0)
                c_gl(t * 2 + 1, 1)
                c_glu(t * 2 + 2, 0)
                c_xt(t * 2 + 4, 0)
                c_gate(t * 2 + 3, 1)
                c_gl(t * 2 + 2, 0)
                c_glu(t * 2 + 3, 1)
            c_gate(NSLOT - 1, 0)
            c_gl(NSLOT - 2, 1)
            c_glu(NSLOT - 1, 0)
            c_gl(NSLOT - 1, 0)

            for c in range(4):
                dve.wait_ge(YIN[c], 32)
                for i in range(8 * c, 8 * c + 8):
                    dve.scalar_tensor_tensor(out=X[:, i, :], in0=Y01[:, 0, i, :], scalar=RW[:, 0, i:i + 1],
                                             in1=X[:, i, :], op0=ALU.mult, op1=ALU.add).then_inc(s["f_s"], 1)
                for i in range(8 * c, 8 * c + 8):
                    dve.wait_ge(s["f_s"], i + 1)
                    dve.scalar_tensor_tensor(out=X[:, i, :], in0=Y01[:, 1, i, :], scalar=RW[:, 1, i:i + 1],
                                             in1=X[:, i, :], op0=ALU.mult, op1=ALU.add).then_inc(s["f_r"], 1)


def kernel(**inputs):
    import numpy as np
    import concourse.bacc as bacc
    from concourse.bass_utils import run_bass_kernel_spmd

    a = {k: np.asarray(v) for k, v in inputs.items()}

    def chunks(w):
        return w.reshape(DC, P, -1).transpose(1, 0, 2).reshape(P, -1)

    def rows(v):
        return np.broadcast_to(v[None, :], (P, v.shape[0]))

    def cols(v):
        return v.reshape(DC, P).T

    def both(v):
        return np.concatenate([v, v], 0)

    cst = np.concatenate([
        chunks(a["L0_attn_W_shift"].T), rows(a["L0_attn_shift_gate"]),
        chunks(np.concatenate([a["L0_attn_W_key"].T, a["L0_attn_W_value"].T], 1)),
        cols(a["L0_attn_ln_w"]), cols(a["L0_attn_ln_b"]),
        both(a["L0_attn_time_decay"][:, None]), both(a["L0_attn_time_first"][:, None]),
        both(a["L0_attn_W_output"].T),
        chunks(a["L0_xattn_wq"].T), chunks(a["L0_xattn_wo"].T),
        cols(a["L0_xattn_bq"]), cols(a["L0_xattn_bk"]), rows(a["L0_xattn_bo"]),
        chunks(a["L0_ffn_Wg"].T), rows(a["L0_ffn_bg"])], 1)
    ctx_t = a["ctx_1024"].reshape(B * KEYS, D).T
    kvc = np.concatenate([chunks(a["L0_xattn_wk"].T), chunks(a["L0_xattn_wv"].T), rows(a["L0_xattn_bv"]),
                          chunks(ctx_t)], 1)

    def apart(w):
        return np.concatenate([w[..., 0::2], w[..., 1::2]], -1)

    def by_part(w):
        return w.reshape(NEXP, DC, P, -1).transpose(0, 2, 1, 3).reshape(NEXP, P, -1)

    wexp = np.concatenate([by_part(apart(a["L0_ffn_Wgu"])), by_part(a["L0_ffn_Wd"])], 2)
    wexp = wexp.reshape(NEXP, P, PIECES, PW).transpose(0, 2, 1, 3).reshape(NPIECE, P, PW)
    bexp = np.concatenate([apart(a["L0_ffn_bgu"]), a["L0_ffn_bd"]], 1)
    bexp = np.concatenate([bexp, bexp], 0)
    arrays = {"x": a["x"].reshape(NTOK, D), "cst": cst, "kvc": kvc, "wexp": wexp, "bexp": bexp}
    arrays = {f"in_{n}": np.ascontiguousarray(v) for n, v in arrays.items()}
    nc = bacc.Bacc("TRN2", target_bir_lowering=False, num_devices=1)
    args = [nc.dram_tensor(n, v.shape, mybir.dt.from_np(v.dtype), kind="ExternalInput").ap()
            for n, v in arrays.items()]
    args.append(nc.dram_tensor("out_0", (NTOK, D), F32, kind="ExternalOutput").ap())
    build_decoder(nc, *args)
    r = run_bass_kernel_spmd(nc, [arrays], core_ids=[0])
    return np.asarray(r.results[0]["out_0"]).reshape(B, T, D)
```

```python
from contextlib import ExitStack

import concourse.bass as bass
from concourse import mybir

ALU = mybir.AluOpType
ACT = mybir.ActivationFunctionType
AX = mybir.AxisListType
F32 = mybir.dt.float32
F16 = mybir.dt.float16
I32 = mybir.dt.int32
U32 = mybir.dt.uint32
ds = bass.ds

P = 128
D = 256
DC = D // P
B, T, KEYS = 4, 1024, 77
NTOK = B * T
TILES = NTOK // P
TPB = T // P
SHIFT_TILES = TPB // 2
S = 64
HEADS, HD = 16, 16
HG = 8
GK = HG * KEYS
NCH = -(-GK // P)
LAST = GK - (NCH - 1) * P
GT = 4
GTOK = GT * P
GROUPS = TILES // GT
NEXP, TOPK, E = 16, 2, 256
F = 2 * E
CAP = NTOK + P
NSLOT = (TOPK * NTOK + NEXP * (P - 1)) // P
XS_ROWS = NEXP * CAP + P
ROW = D + 2
FAR = 1 << 20
EPS = 1e-5
XSC = 16.0
WSC = 16.0
GUS = XSC * WSC
ONE = 16.0
GDS = 2 * GUS
YS = GDS * WSC
ALPHA, LIMIT = 1.702, 7.0
YCH = 8
YT = TILES // YCH

_width = []


def _cols(n):
    _width.append(n)
    return sum(_width) - n


C_WSH = _cols(DC * D)
C_GATE = _cols(D)
C_WKV = _cols(DC * 2 * S)
C_LNW, C_LNB = _cols(DC), _cols(DC)
C_TD, C_TF = _cols(1), _cols(1)
C_WOUT = _cols(D)
C_WQ = _cols(DC * D)
C_WO = _cols(DC * D)
C_BQ, C_BK = _cols(DC), _cols(DC)
C_BO = _cols(D)
C_WG = _cols(DC * NEXP)
C_BG = _cols(NEXP)
C_ALL = sum(_width)
Q_WK, Q_WV, Q_BV, Q_CTX = 0, DC * D, 2 * DC * D, 2 * DC * D + D
Q_ALL = Q_CTX + DC * B * KEYS
PW = 512
PIECES = 3
NPIECE = NEXP * PIECES
A_PIECES = 2 * PIECES
assert A_PIECES + 2 * PIECES * (NTOK // 512 - 1) == NPIECE
A_ROOTS = 12
assert DC * F == 2 * PW and DC * E == PW
W_DOWN, LOW = 2 * 2 * PW, PW
WEX = 2 * PIECES * PW


def build_decoder(nc, x, cst, kvc, wexp, bexp, out):
    xs_rows = nc.dram_tensor("xs_rows", (XS_ROWS, ROW), F32, kind="Internal").ap()
    y_rows = nc.dram_tensor("y_rows", (TOPK * NTOK, D), F32, kind="Internal").ap()
    v_flat = nc.dram_tensor("v_flat", (B, HEADS // HG, GK, HD), F32, kind="Internal").ap()

    ctx = ExitStack()
    with ctx:
        def sb(name, shape, dt):
            return ctx.enter_context(nc.sbuf_tensor(name, shape, dt))

        def sem(name):
            return ctx.enter_context(nc.semaphore(name))

        X = sb("X", [P, TILES, D], F32)
        W16 = sb("W16", [P, NPIECE, 2, PW], F16)
        CST = sb("CST", [P, C_ALL], F32)
        KRAW = sb("KRAW", [P, 2, DC, B, KEYS], F16)
        KCUR = sb("KCUR", [P, 2, DC, 2, HG, KEYS], F16)
        VFLAT = sb("VFLAT", [P, DC, NCH, HD], F32)
        VCUR = sb("VCUR", [P, DC, NCH, 2, 2, HD], F32)
        MV = sb("MV", [P, NCH, 2, 2, HD], F32)
        MK = sb("MK", [P, HG], F16)
        IND = sb("IND", [2 * HEADS, HEADS * KEYS], F16)
        ID32 = sb("ID32", [P, P], F32)
        ID16 = sb("ID16", [P, P], F16)
        UP16 = sb("UP16", [P, P], F16)
        ON16 = sb("ON16", [P, P], F16)
        BEX = sb("BEX", [2 * NEXP, F + E], F16)
        TOK = sb("TOK", [P, TILES], I32)
        IOTA = sb("IOTA", [P, NEXP], F32)
        RUN = sb("RUN", [P, GT + 1, NEXP], F32)
        ECAP = sb("ECAP", [P, NEXP], F32)
        RW = sb("RW", [P, TOPK, TILES], F32)
        HALF = sb("HALF", [P, TPB], F32)
        SMALL = sb("SMALL", [P, 16], F32)
        STG = sb("STG", [P, 2, PW], F32)

        AR = sb("AR", [P, 9744], F32)

        def ar(at, n, dt=F32):
            v = AR[:, at:at + n]
            return v if dt == F32 else v.bitcast(dt)

        def tiles(v):
            return v.rearrange("p (k d) -> p k d", k=16)

        def turned(v):
            return v.rearrange("p (c t) -> p c t", c=DC)

        def halves(v):
            return v.rearrange("p (h c t) -> p h c t", h=2, c=DC)

        TW = ar(8192, GTOK)
        ST = ar(8704, 2 * GTOK).rearrange("p (h t) -> p h t", h=2)
        PB = ar(0, NCH * GTOK).rearrange("p (n t) -> p n t", n=NCH)
        XQ = ar(2560, GT * D).rearrange("p (k d) -> p k d", k=GT)
        XQT = ar(3584, DC * GTOK).rearrange("p (c t) -> p c t", c=DC)
        X3, X3T = XQ, XQT
        QH = ar(4608, DC * GTOK, F16).rearrange("p (b c t) -> p b c t", b=2, c=DC)
        QL = ar(5632, DC * GTOK, F16).rearrange("p (b c t) -> p b c t", b=2, c=DC)
        AT = ar(6656, DC * GTOK).rearrange("p (c t) -> p c t", c=DC)
        RB = ar(7680, 2 * GT * ROW).rearrange("p (b k w) -> p b k w", b=2, k=GT)
        RIN = ar(0, 2 * ROW).rearrange("p (b w) -> p b w", b=2)
        XTS = ar(516, 2 * D, F16).rearrange("p (b v t) -> p b v t", b=2, v=4)
        CG = ar(1028, 2 * E).rearrange("p (b e) -> p b e", b=2)
        CT = ar(1540, 2 * E).rearrange("p (b e) -> p b e", b=2)
        CU = ar(2052, 2 * E).rearrange("p (b e) -> p b e", b=2)
        CGD = ar(2564, 2 * E).rearrange("p (b e) -> p b e", b=2)
        GH = ar(3076, E, F16).rearrange("p (b c t) -> p b c t", b=2, c=DC)
        GL = ar(3332, E, F16).rearrange("p (b c t) -> p b c t", b=2, c=DC)
        CY = ar(3588, 2 * D).rearrange("p (b e) -> p b e", b=2)
        PAD = ar(7400, ROW)
        OHT = ar(4614, P, F16)[:, 0:P]
        TAB = ar(4742, 2 * P, I32)
        PAIR = ar(5472, 2 * P)
        QUAD = ar(5728, P // 2, I32)
        RUNI = ar(4998, NEXP, I32)
        CW = ar(5014, 10 * NEXP).rearrange("p (a e) -> p a e", e=NEXP)
        CWI = ar(5014 + 10 * NEXP, NEXP, I32)
        NIX = ar(5190, 2, I32)
        IXF = ar(5192, 2)
        CIX = ar(5194, NSLOT)
        DIAG = ar(5273, P // 2, F16)
        EXB = ar(5337, P)
        w_flat = W16[:, :, :, :].rearrange("p n v w -> p (n v w)")
        w_words = w_flat.bitcast(F32)
        Y01 = w_words[:, 0:TOPK * TILES * D].rearrange("p (k i d) -> p k i d", k=TOPK, i=TILES)

        def spare(e, n):
            return w_words[:, e * WEX // 2:(e + n) * WEX // 2]

        KVC = spare(NEXP - 2, 2)
        VSB = spare(6, 1)[0:KEYS, 0:B * D].rearrange("p (b e) -> p b e", b=B)
        KTMP = spare(6, 1)[:, B * D:B * D + B * KEYS]
        BRAW = spare(7, 1)
        SCR = spare(7, 1)[:, F + E:]
        w2 = w_words[:, 8 * WEX // 2:8 * WEX // 2 + 2 * 16 * D]
        stat = w_words[:, 13 * WEX // 2 + B * D:14 * WEX // 2]
        STAT = stat[:, 0:192].rearrange("p (b k w) -> p b k w", b=2, k=16)
        MVA = stat[:, 192:256].rearrange("p (b k w) -> p b k w", b=2, k=16)
        XN = [tiles(ar(0, 16 * D)), tiles(w2[:, 0:16 * D])]
        XNT = [turned(ar(4096, 16 * D)), turned(w2[:, 16 * D:])]
        XST = [halves(ar(4096, 16 * D)), halves(w2[:, 16 * D:])]

        RS = sb("RS", [P, 2, 2, 16], F32)
        MVQ = sb("MVQ", [P, TILES, 2], F32)
        RSQ = sb("RSQ", [P, 2, TILES], F32)
        STAT3 = sb("STAT3", [P, GT, 6], F32)
        MVA3 = sb("MVA3", [P, GT, 2], F32)
        RS3 = sb("RS3", [P, 2, GT], F32)
        MX = sb("MX", [P, GT, HEADS], F32)
        MH = sb("MH", [P, GT, 2 * HEADS], F16)
        MT = sb("MT", [2 * HEADS, GTOK], F16)
        LG = sb("LG", [P, GT, NEXP], F32)
        M8 = sb("M8", [P, GT, 8], F32)
        I8 = sb("I8", [P, GT, 8], U32)
        IF = sb("IF", [P, GT, TOPK], F32)
        MS = sb("MS", [P, TOPK, GT, NEXP], F32)
        MS16 = sb("MS16", [P, GT, NEXP], F16)
        TOKF = sb("TOKF", [P, TILES], F32)
        SLF = sb("SLF", [P, TOPK, GT], F32)
        SLOT = sb("SLOT", [P, 2, TOPK, GT], I32)
        RD = sb("RD", [P, 3, GT], F32)

        def bank(i, n=1):
            return ctx.enter_context(nc.psum_tensor(f"bank{i}", [P, n * 512], F32))

        SC = [bank(0), bank(1)]
        MXP = bank(2, 2)
        NUM, DEN = bank(4), bank(5)
        WA, WB = bank(6), bank(7)
        WK = [WA, WB]
        MXB = MXP[:, :].rearrange("p (b n) -> p b n", b=2)
        TRA, SHA, KVA, OUA = [SC[0], SC[1]], [MXB[:, 0], MXB[:, 1]], [NUM, DEN], [WA, WB]
        LGP, UPP, ONP = MXB[:, 0, 320:384], MXB[:, 0, 384:448], MXB[:, 1, 384:448]
        MTP = [MXB[0:2 * HEADS, h, 320:448].bitcast(F16) for h in range(2)]
        XTP = [SC[0][:, 0:D].bitcast(F16), SC[1][:, 0:D].bitcast(F16)]
        GUP, GTP, YP = [MXB[:, 0], MXB[:, 1]], [NUM, DEN], [WA, WB]

        def cst_w(c0, n, c):
            return CST[:, c0 + c * n:c0 + (c + 1) * n]

        names = []
        names += """cst_in kvc_in bex_in xin0 xin1 xin2 xin3 w_in0 w_in1 v_out v_in sct0 sct1 pads0 pads1 rin0 rin1
            ysc0 ysc1 y_in0 y_in1 y_in2 y_in3 y_in4 y_in5 y_in6 y_in7 out_done""".split()
        names += """consts1 consts_ready ind_ready small_ready gate_tanh etf_exp wsh_ready wsh_done wkv_ready
            kv_bias_ready k_mm k_hi k_tmp k_ready kcur_r v_mm v_sb vcur_r bex_s bex_ready w_scaled w_hi
            w_split""".split()
        names += """a_stat a_aggr a_rs a_nrm a_turn a_ev a_sh a_xg a_xs a_stat2 a_aggr2 a_rs2 a_kv a_tanh a_exp
            a_wkv a_scan a_out a_x1 stq vaq rsq_r root_s""".split()
        names += """xq_r t_mm xqT_r q_mm qh_r ql_r mx_mm mx_r mh_s mh_r mt_mm mT_r sc_mm exp_r pv_mm rec_s at_r
            xb_r out_mm x2_r""".split()
        names += """st3 va3 rs3_r xn3_r hi_r lo_r t3_mm x3T_r lg_mm lg_r top_r ix_r if_r ms_s ms_r px_mm rd_s rd_e
            rd_r run_s pos_s sl_s slf_s slot_r""".split()
        names += """c_tab c_tabe c_mm quad_s c_cp eb_r pad_r ct_mm cxt_r cgu_mm cg_r cu_r ctanh_r ct1_r cgd_r
            ctg_mm cgh_r cgl_r cd_mm cy_r ixa ixb cix_r nix_r f_s f_r""".split()
        names += """act_past pool_past dve_past""".split()
        s = {n: sem(n) for n in names}
        SCT = [s["sct0"], s["sct1"]]
        RINS = [s["rin0"], s["rin1"]]
        YSC = [s["ysc0"], s["ysc1"]]
        XIN = [s[f"xin{i}"] for i in range(4)]
        WIN = [s["w_in0"], s["w_in1"]]
        YIN = [s[f"y_in{i}"] for i in range(YCH)]

        block = ctx.enter_context(nc.Block())
        HALF_TILES = [[bb * TPB + SHIFT_TILES * h + j for bb in range(2) for j in range(SHIFT_TILES)]
                      for h in range(2)]
        ORDER = HALF_TILES[0] + HALF_TILES[1]
        x_t = x.rearrange("(i p) d -> p i d", p=P)
        out_t = out.rearrange("(i p) d -> p i d", p=P)

        def pads(eng, half):
            for e in range(half * NEXP // 2, (half + 1) * NEXP // 2):
                r = eng.value_load(RUNI[0:1, e:e + 1], min_val=0, max_val=XS_ROWS - P)
                eng.dma_start(xs_rows[ds(r, P), :], PAD).then_inc(s[f"pads{half}"], 16)

        @block.sync
        def _(sp):
            def xload(q):
                sp.dma_start(X[:, 8 * q:8 * q + 8, :], x_t[:, 8 * q:8 * q + 8, :]).then_inc(XIN[q], 16)

            xload(0)
            sp.dma_start(CST[:, :], cst).then_inc(s["cst_in"], 16)
            xload(1)
            xload(2)
            xload(3)
            sp.dma_start(KVC[:, 0:Q_ALL], kvc).then_inc(s["kvc_in"], 16)
            sp.dma_start(BRAW[0:2 * NEXP, 0:F + E], bexp).then_inc(s["bex_in"], 16)

            def wload(e, q, h):
                if not (isinstance(h, int) and h == 0):
                    sp.wait_ge(WIN[q], 16 * h)
                sp.dma_start(w_words[:, ds(e * (PIECES * PW), PIECES * PW)].rearrange("p (n w) -> p n w", w=PW),
                             wexp[ds(e * PIECES, PIECES)].rearrange("n p w -> p n w")).then_inc(WIN[q], 16)

            for h in range(3):
                wload(2 * h, 0, h)
                wload(2 * h + 1, 1, h)

            sp.wait_ge(s["v_sb"], B)
            for b in range(B):
                for m in range(DC):
                    sp.dma_start(v_flat[b, m].rearrange("(h k) e -> k h e", k=KEYS),
                                 VSB[:, b, m * P:(m + 1) * P].rearrange("p (h e) -> p h e", h=HG))\
                        .then_inc(s["v_out"], 16)
            sp.wait_ge(s["v_out"], 16 * B * DC)

            def vload(b, first=False):
                if not first:
                    sp.wait_ge(s["vcur_r"], b)
                for m in range(DC):
                    v = v_flat[ds(b, 1), m].rearrange("a n e -> (a n) e")
                    sp.dma_start(VFLAT[:, m, 0:NCH - 1, :],
                                 v[0:(NCH - 1) * P, :].rearrange("(n p) e -> p n e", p=P)).then_inc(s["v_in"], 16)
                    sp.dma_start(VFLAT[0:LAST, m, NCH - 1, :], v[(NCH - 1) * P:GK, :]).then_inc(s["v_in"], 16)

            vload(0, True)
            sp.wait_ge(s["a_kv"], 4)
            sp.wait_ge(s["vaq"], 2)
            sp.wait_ge(s["ind_ready"], 1)
            sp.wait_ge(s["bex_ready"], 1)
            with sp.Fori(3, NEXP // 2) as h:
                wload(h * 2, 0, h)
                wload(h * 2 + 1, 1, h)
            with sp.Fori(1, B) as b:
                vload(b)

            sp.wait_ge(s["c_tab"], 1)
            sp.wait_ge(s["pad_r"], 2)
            pads(sp, 0)
            sp.dma_start(xs_rows[NEXP * CAP:XS_ROWS, :], PAD).then_inc(s["pads0"], 16)
            sp.wait_ge(s["pads0"], 16 * (NEXP // 2 + 1))
            sp.wait_ge(s["pads1"], 16 * (NEXP // 2))
            for q in range(2):
                sp.wait_ge(SCT[q], 16 * TOPK * TILES // 2)
            sp.wait_ge(s["c_cp"], 2)

            def load(n, q, first=False):
                r = sp.value_load(TAB[0:1, ds(P + n, 1)], min_val=0, max_val=XS_ROWS - P)
                if not first:
                    sp.wait_ge(s["ct_mm"], n - 1)
                    sp.wait_ge(s["cix_r"], n - 1)
                sp.dma_start(RIN[:, q, :], xs_rows[ds(r, P), :]).then_inc(RINS[q], 16)

            load(0, 0, True)
            load(1, 1, True)
            load(2, 0)
            with sp.Fori(0, (NSLOT - 3) // 2) as t:
                load(t * 2 + 3, 1)
                load(t * 2 + 4, 0)

            for q in range(2):
                sp.wait_ge(YSC[q], 16 * ((NSLOT + 1 - q) // 2))
            y_t = y_rows.rearrange("(k i p) d -> p k i d", k=TOPK, p=P)
            for c in range(YCH):
                for k in range(TOPK):
                    sp.dma_start(Y01[:, k, YT * c:YT * (c + 1), :], y_t[:, k, YT * c:YT * (c + 1), :])\
                        .then_inc(YIN[c], 16)
            for c in range(YCH):
                sp.wait_ge(s["f_r"], YT * (c + 1))
                sp.dma_start(out_t[:, YT * c:YT * (c + 1), :], X[:, YT * c:YT * (c + 1), :])\
                    .then_inc(s["out_done"], 16)
            sp.wait_ge(s["out_done"], 16 * YCH)

        @block.gpsimd
        def _(pool):
            n1 = [0]

            def c1(ins):
                n1[0] += 1
                ins.then_inc(s["consts1"], 1)

            def sel(v, op, base, pattern, cm, fill=0.0):
                pool.wait_ge(s["consts1"], n1[0])
                c1(pool.affine_select(out=v, in_=v, compare_op=op, fill=fill, base=base, pattern=pattern,
                                      channel_multiplier=cm))

            c1(pool.memset(HALF[:, :], -0.5))
            c1(pool.memset(ID32[:, :], 0.0))
            sel(ID32[:, :], ALU.not_equal, 0, [[-1, P]], 1, 1.0)
            pool.wait_ge(s["consts1"], n1[0])
            c1(pool.tensor_copy(ID16[:, :], ID32[:, :]))
            assert n1[0] == 4

            def root(mv, rs, k, scale=1.0, alone=False):
                n = rs.shape[2]

                def step(i, ins):
                    ins.then_inc(s["root_s"], 1)
                    w = pool.wait_ge(s["root_s"], k * 3 + i)
                    if alone:
                        w.then_inc(s["pool_past"], 1)

                step(1, pool.tensor_scalar(rs[:, 0], mv[:, :, 1], EPS, 1.0 / (scale * scale), ALU.add, ALU.mult))
                step(2, pool.tensor_tensor(rs[:, 0], rs[:, 0], HALF[:, 0:n], ALU.pow))
                step(3, pool.tensor_tensor(rs[:, 1], rs[:, 0], mv[:, :, 0], ALU.mult))
                return pool.tensor_scalar(rs[:, 1], rs[:, 1], -1.0, 0.0, ALU.mult, ALU.add)

            c1(pool.memset(MK[:, :], 1.0))
            sel(MK[:, :], ALU.is_ge, 0, [[-HD, HG]], 1)
            sel(MK[:, :], ALU.is_ge, HD - 1, [[HD, HG]], -1)
            c1(pool.memset(MV[:, :, :, :, :].rearrange("p a b c d -> p (a b c d)"), 1.0))
            for v in range(2):
                pat = [[P - 2 * KEYS, NCH], [-KEYS, 2], [0, HD]]
                sel(MV[:, :, v], ALU.is_ge, 2 * KEYS * v, pat, 1)
                sel(MV[:, :, v], ALU.is_ge, (KEYS - 1) - 2 * KEYS * v, [[-a, n] for a, n in pat], -1)
            c1(pool.memset(ON16[:, :], 1.0))
            c1(pool.memset(UP16[:, :], 1.0))
            sel(UP16[:, :], ALU.is_gt, 0, [[1, P]], -1)
            c1(pool.iota(TOK[:, :], [[P, TILES]], base=0, channel_multiplier=1))
            pool.wait_ge(s["consts1"], n1[0])
            c1(pool.tensor_scalar(TOKF[:, :], TOK[:, :], 1.0, float(NTOK), ALU.mult, ALU.add))
            c1(pool.iota(SCR[:, 700:700 + NEXP].bitcast(I32), [[1, NEXP]], base=0, channel_multiplier=0))
            pool.wait_ge(s["consts1"], n1[0])
            c1(pool.tensor_copy(IOTA[:, :], SCR[:, 700:700 + NEXP].bitcast(I32)))
            pool.wait_ge(s["consts1"], n1[0])
            c1(pool.tensor_scalar(ECAP[:, :], IOTA[:, :], float(CAP), 0.0, ALU.mult, ALU.add))
            pool.wait_ge(s["consts1"], n1[0])
            pool.tensor_copy(RUN[:, 0, :], ECAP[:, :]).then_inc(s["consts_ready"], 1)

            for u in range(4):
                p, q = u // 2, u % 2
                pool.wait_ge(s["a_aggr"], u + 1)
                root(MVA[:, p, 8 * q:8 * q + 8], RS[:, p, :, 8 * q:8 * q + 8], u).then_inc(s["a_rs"], 1)

            def gate_half(p):
                pool.wait_ge(s["wsh_done"], 1)
                for k in ORDER:
                    pool.wait_ge(s["a_turn"], 16 * p + k + 1)
                    pool.tensor_tensor(XN[p][:, k, :], XN[p][:, k, :], CST[:, C_GATE:C_GATE + D], ALU.mult)\
                        .then_inc(s["a_xg"], 1)

            def roots_2(p):
                for h in range(2):
                    u = 2 * p + h
                    pool.wait_ge(s["a_aggr2"], u + 1)
                    root(MVA[:, p, 8 * h:8 * h + 8], RS[:, p, :, 8 * h:8 * h + 8], 4 + u).then_inc(s["a_rs2"], 1)

            gate_half(0)
            roots_2(0)
            gate_half(1)

            def split(n, q):
                pool.wait_ge(s["w_hi"], n + 1).then_inc(s["pool_past"], 1)
                w = W16[:, ds(n, 1), :, :].rearrange("p a v w -> p (a v) w")
                pool.tensor_tensor(w[:, 1], STG[:, q], w[:, 0], ALU.subtract).then_inc(s["w_split"], 1)

            roots_2(1)

            def kcur(b, bp):
                if not (isinstance(b, int) and b < 2):
                    pool.wait_ge(s["sc_mm"], (b - 1) * (4 * NCH))
                for m in range(DC):
                    for v in range(2):
                        ins = pool.tensor_tensor(
                            KCUR[:, ds(bp, 1), m, v].rearrange("p a h k -> p (a h) k"),
                            KRAW[:, v, m, ds(b, 1), :].broadcast_to([P, HG, KEYS]),
                            MK[:, :].unsqueeze(2).broadcast_to([P, HG, KEYS]), ALU.mult)
                ins.then_inc(s["kcur_r"], 1)

            ind2 = SCR[0:2 * HEADS, 0:HEADS * KEYS // 2].bitcast(F16)
            for v, base in ((IND[:, :], 0), (ind2, KEYS * HEADS)):
                c1(pool.memset(v, 1.0))
                sel(v, ALU.is_ge, base, [[1, HEADS * KEYS]], -KEYS)
                sel(v, ALU.is_ge, (KEYS - 1) - base, [[-1, HEADS * KEYS]], KEYS)
            pool.wait_ge(s["consts1"], n1[0])
            pool.tensor_tensor(IND[:, :], IND[:, :], ind2, ALU.add).then_inc(s["ind_ready"], 1)
            pool.wait_ge(s["k_ready"], DC)
            kcur(0, 0)
            for n in range(A_PIECES):
                split(n, n % 2)
            for u in range(4):
                pool.wait_ge(s["vaq"], u // 2 + 1)
                root(MVQ[:, 8 * u:8 * u + 8], RSQ[:, :, 8 * u:8 * u + 8], 8 + u).then_inc(s["rsq_r"], 1)

            def add_bo(g):
                pool.wait_ge(s["xq_r"], 4 * g + 4)
                for j in range(GT):
                    xt = X[:, ds(g * GT + j, 1), :].rearrange("p a d -> p (a d)")
                    ins = pool.tensor_tensor(xt, xt, CST[:, C_BO:C_BO + D], ALU.add)
                ins.then_inc(s["xb_r"], 1)

            def root3(g):
                pool.wait_ge(s["va3"], g + 1).then_inc(s["pool_past"], 1)
                root(MVA3, RS3, g + A_ROOTS, XSC, True).then_inc(s["rs3_r"], 1)

            def low_rows(g, par):
                pool.wait_ge(s["hi_r"], g + 1)
                for j in range(GT):
                    hl = RB[:, par, j, 0:D].bitcast(F16).rearrange("p (v d) -> p v d", v=2)
                    ins = pool.tensor_tensor(hl[:, 1], X3[:, j, :], hl[:, 0], ALU.subtract)
                ins.then_inc(s["lo_r"], 1)

            def scatter(g, par):
                pool.wait_ge(s["lo_r"], g + 1).then_inc(s["pool_past"], 1)
                pool.wait_ge(s["slot_r"], g + 1).then_inc(s["pool_past"], 1)
                for j in range(GT):
                    for k in range(TOPK):
                        pool.indirect_dma_start(
                            xs_rows, bass.IndirectOffsetOnAxis(ap=SLOT[:, par, k, j:j + 1], axis=0),
                            RB[:, par, j, :], None, bounds_check=XS_ROWS - 1, oob_is_err=True)\
                            .then_inc(SCT[par], 16)

            def body(g, b, par, out=True, log=True, attn=True, nxt=True, nextk=None):
                if attn:
                    add_bo(g)
                if attn and nxt:
                    for k in range(PIECES):
                        split(g * (2 * PIECES) + (A_PIECES + k), k % 2)
                if out:
                    root3(g - 1)
                if log:
                    scatter(g - 2, par)
                if attn and nxt:
                    for k in range(PIECES, 2 * PIECES):
                        split(g * (2 * PIECES) + (A_PIECES + k), k % 2)
                if out:
                    low_rows(g - 1, 1 - par)
                if nextk is not None:
                    kcur(b + 1, nextk)

            body(0, 0, 0, False, False, nextk=1)
            body(1, 0, 1, log=False)
            with pool.Fori(1, B - 1) as b:
                body(b * 2, b, 0, nextk=(b + 1) % 2)
                body(b * 2 + 1, b, 1)
            body(GROUPS - 2, B - 1, 0)
            body(GROUPS - 1, B - 1, 1, nxt=False)
            body(GROUPS, B, 0, attn=False)
            pool.memset(PAD, 0.0).then_inc(s["pad_r"], 1)
            pool.wait_ge(s["pad_r"], 1)
            pool.memset(PAD[:, D:D + 1], float(FAR)).then_inc(s["pad_r"], 1)
            scatter(GROUPS - 1, 1)

            pool.wait_ge(s["eb_r"], 1)

            def y_index(n, q, t):
                pool.wait_ge(RINS[q], 16 * (t + 1)).then_inc(s["pool_past"], 1)
                pool.tensor_tensor(IXF[:, q:q + 1], RIN[:, q, D + 1:ROW], EXB[:, ds(n, 1)], ALU.subtract)\
                    .then_inc(s["ixa"], 1)
                pool.wait_ge(s["ixa"], n + 1).then_inc(s["pool_past"], 1)
                pool.tensor_scalar(IXF[:, q:q + 1], IXF[:, q:q + 1], 0.0, float(NTOK), ALU.is_equal, ALU.mult)\
                    .then_inc(s["ixb"], 1)
                pool.wait_ge(s["ixb"], n + 1).then_inc(s["pool_past"], 1)
                pool.tensor_tensor(CIX[:, ds(n, 1)], RIN[:, q, D:D + 1], IXF[:, q:q + 1], ALU.subtract)\
                    .then_inc(s["cix_r"], 1)

            def y_scatter(n, q, t, first=False):
                if not first:
                    pool.wait_ge(YSC[q], 16 * t).then_inc(s["pool_past"], 1)
                pool.wait_ge(s["cix_r"], n + 1).then_inc(s["pool_past"], 1)
                pool.tensor_copy(NIX[:, q:q + 1], CIX[:, ds(n, 1)]).then_inc(s["nix_r"], 1)
                pool.wait_ge(s["cy_r"], n + 1).then_inc(s["pool_past"], 1)
                pool.wait_ge(s["nix_r"], n + 1).then_inc(s["pool_past"], 1)
                pool.indirect_dma_start(
                    y_rows, bass.IndirectOffsetOnAxis(ap=NIX[:, q:q + 1], axis=0), CY[:, q, :], None,
                    bounds_check=TOPK * NTOK - 1, oob_is_err=False).then_inc(YSC[q], 16)

            y_index(0, 0, 0)
            y_index(1, 1, 0)
            y_index(2, 0, 1)
            y_index(3, 1, 1)
            y_scatter(0, 0, 0, True)
            y_index(4, 0, 2)
            y_scatter(1, 1, 0, True)
            with pool.Fori(1, (NSLOT - 3) // 2) as t:
                y_index(t * 2 + 3, 1, t + 1)
                y_scatter(t * 2, 0, t)
                y_index(t * 2 + 4, 0, t + 2)
                y_scatter(t * 2 + 1, 1, t)
            for n in range(NSLOT - 3, NSLOT):
                y_scatter(n, n % 2, n // 2)

        @block.scalar
        def _(act):
            act.wait_ge(s["cst_in"], 16)
            act.activation(CST[:, C_GATE:C_GATE + D], CST[:, C_GATE:C_GATE + D], ACT.Tanh, scale=0.5)\
                .then_inc(s["gate_tanh"], 1)
            act.activation(SMALL[:, 0:1], CST[:, C_TD:C_TD + 1], ACT.Exp).then_inc(s["etf_exp"], 1)
            act.activation(SMALL[:, 1:2], CST[:, C_TF:C_TF + 1], ACT.Exp).then_inc(s["etf_exp"], 1)

            def whi(n, q, e_sem, loaded):
                act.wait_ge(e_sem, loaded).then_inc(s["act_past"], 1)
                if not (isinstance(n, int) and n < 2):
                    act.wait_ge(s["w_split"], n - 1).then_inc(s["act_past"], 1)
                act.activation(STG[:, q], w_words[:, ds(n * PW, PW)], ACT.Copy, scale=WSC).then_inc(s["w_scaled"], 1)
                act.wait_ge(s["w_scaled"], n + 1).then_inc(s["act_past"], 1)
                act.activation(W16[:, ds(n, 1), 0, :].rearrange("p a w -> p (a w)"), STG[:, q], ACT.Copy)\
                    .then_inc(s["w_hi"], 1)

            def norm_a(p, k, stage, n):
                src = X[:, 16 * p + k, :] if stage == 0 else XN[p][:, k, :]
                act.activation(XN[p][:, k, :], src, ACT.Identity, scale=RS[:, p, 0, n:n + 1],
                               bias=RS[:, p, 1, n:n + 1]).then_inc(s["a_nrm"], 1)

            def evac_a(u, dst):
                act.wait_ge(s["a_turn"], u + 1)
                act.activation(dst, TRA[u % 2][:, 0:D].rearrange("p (c t) -> p c t", c=DC), ACT.Copy)\
                    .then_inc(s["a_ev"], 1)

            AHEAD = 4

            def stage_1(p):
                for k in range(16 + AHEAD):
                    if k % 8 == 0 and k < 16:
                        act.wait_ge(s["a_rs"], 2 * p + k // 8 + 1)
                    if k < 16:
                        norm_a(p, k, 0, k)
                    if k >= AHEAD:
                        j = k - AHEAD
                        evac_a(16 * p + j, XNT[p][:, :, j * P:(j + 1) * P])

            def stage_2(p, h):
                act.wait_ge(s["a_rs2"], 2 * p + h + 1)
                act.wait_ge(s["a_sh"], 16 * (p + 1))
                for k in range(8 + AHEAD):
                    if k < 8:
                        norm_a(p, HALF_TILES[h][k], 1, 8 * h + k)
                    if k >= AHEAD:
                        j = k - AHEAD
                        evac_a(32 + 16 * p + 8 * h + j, XST[p][:, h, :, j * P:(j + 1) * P])

            def wkv_exp(w):
                act.wait_ge(s["a_kv"], w + 1)
                if w:
                    act.wait_ge(s["a_scan"], w)
                act.activation(TW, KVA[0][:, :], ACT.Tanh, scale=0.5, bias=SMALL[:, 5:6]).then_inc(s["a_tanh"], 1)
                act.wait_ge(s["a_tanh"], w + 1)
                act.activation(TW, TW, ACT.Exp, scale=SMALL[:, 4:5], bias=SMALL[:, 4:5]).then_inc(s["a_exp"], 1)

            stage_1(0)
            stage_1(1)
            for m in range(DC):
                act.wait_ge(s["k_mm"], m + 1)
                act.wait_ge(s["small_ready"], 1)
                act.activation(KRAW[:, 0, m].rearrange("p b k -> p (b k)"), WK[m][:, 0:B * KEYS], ACT.Identity,
                               scale=0.25, bias=SMALL[:, 2 + m:3 + m]).then_inc(s["k_hi"], 1)
            stage_2(0, 0)
            stage_2(0, 1)
            stage_2(1, 0)
            act.wait_ge(s["kv_bias_ready"], 1)
            wkv_exp(0)
            stage_2(1, 1)
            wkv_exp(1)
            wkv_exp(2)
            for n in range(A_PIECES):
                whi(n, n % 2, WIN[n // PIECES], 16)
            wkv_exp(3)

            def norm_q(g, j, first=False):
                if j == 0:
                    if not first:
                        act.wait_ge(s["t_mm"], 2 * g).then_inc(s["act_past"], 1)
                    if not isinstance(g, int) or g >= 3:
                        act.wait_ge(s["lo_r"], g - 2).then_inc(s["act_past"], 1)
                        act.wait_ge(s["t3_mm"], 2 * (g - 2)).then_inc(s["act_past"], 1)
                act.activation(XQ[:, j, :], X[:, ds(g * GT + j, 1), :].rearrange("p a d -> p (a d)"), ACT.Identity,
                               scale=RSQ[:, 0, ds(g * GT + j, 1)], bias=RSQ[:, 1, ds(g * GT + j, 1)])\
                    .then_inc(s["xq_r"], 1)

            def evac_t(g):
                for r in range(2):
                    act.wait_ge(s["t_mm"], 2 * g + r + 1)
                    act.activation(XQT[:, :, 2 * r * P:2 * (r + 1) * P],
                                   WK[r][:, :].rearrange("p (j c t) -> p c j t", j=2, c=DC),
                                   ACT.Copy).then_inc(s["xqT_r"], 1)

            def evac_q(g, par):
                for m in range(DC):
                    act.wait_ge(s["q_mm"], 2 * g + m + 1)
                    act.activation(QH[:, par, m], WK[m][:, :], ACT.Identity, bias=CST[:, C_BQ + m:C_BQ + m + 1])\
                        .then_inc(s["qh_r"], 1)

            def evac_m(g):
                act.wait_ge(s["mt_mm"], g + 1)
                for h in range(2):
                    ins = act.activation(MT[:, h * 2 * P:(h + 1) * 2 * P], MTP[h], ACT.Copy)
                ins.then_inc(s["mT_r"], 1)

            def exps(g, m, c, first=False):
                rows = P if c < NCH - 1 else LAST
                act.wait_ge(s["sc_mm"], g * (2 * NCH) + (m * NCH + c + 1))
                if c == 0 and not first:
                    act.wait_ge(s["pv_mm"], 2 * g + m)
                act.activation(PB[0:rows, c, :], SC[(m * NCH + c) % 2][0:rows, :], ACT.Exp)\
                    .then_inc(s["exp_r"], 1)

            def norm_3(g):
                act.wait_ge(s["rs3_r"], g + 1)
                for j in range(GT):
                    act.activation(X3[:, j, :], X[:, ds(g * GT + j, 1), :].rearrange("p a d -> p (a d)"),
                                   ACT.Identity, scale=RS3[:, 0, j:j + 1], bias=RS3[:, 1, j:j + 1])\
                        .then_inc(s["xn3_r"], 1)

            def rows_hi(g, par, k):
                if not (isinstance(k, int) and k == 0):
                    act.wait_ge(SCT[par], k * (16 * TOPK * GT)).then_inc(s["act_past"], 1)
                act.wait_ge(s["xn3_r"], 4 * g + 4).then_inc(s["act_past"], 1)
                for j in range(GT):
                    ins = act.activation(RB[:, par, j, 0:D // 2].bitcast(F16), X3[:, j, :], ACT.Copy)
                ins.then_inc(s["hi_r"], 1)

            def evac_t3(g):
                for r in range(2):
                    act.wait_ge(s["t3_mm"], 2 * g + r + 1)
                    act.activation(X3T[:, :, 2 * r * P:2 * (r + 1) * P],
                                   WK[r][:, :].rearrange("p (j c t) -> p c j t", j=2, c=DC),
                                   ACT.Copy).then_inc(s["x3T_r"], 1)

            def pair_exp(g):
                act.wait_ge(s["rd_s"], g + 1)
                act.activation(RD[:, 1, :], RD[:, 0, :], ACT.Exp).then_inc(s["rd_e"], 1)

            def body(g, b, par, out=True, log=True, attn=True, nxt=True):
                first = isinstance(g, int) and g == 0
                if attn:
                    for c in range(NCH):
                        exps(g, 0, c, first)
                        if nxt and c < GT:
                            norm_q(g + 1, c)
                if log:
                    pair_exp(g - 2)
                if attn and nxt:
                    for k in range(PIECES):
                        whi(g * (2 * PIECES) + (A_PIECES + k), k % 2, WIN[0], g * 16 + 32)
                if nxt:
                    evac_t(g + 1)
                if attn and not nxt:
                    for c in range(NCH):
                        exps(g, 1, c)
                if out:
                    norm_3(g - 1)
                    rows_hi(g - 1, 1 - par, b - 1 + par)
                if nxt:
                    evac_q(g + 1, 1 - par)
                if attn and nxt:
                    for c in range(NCH):
                        exps(g, 1, c)
                        if c >= NCH - PIECES:
                            k = c + 2 * PIECES - NCH
                            whi(g * (2 * PIECES) + (A_PIECES + k), k % 2, WIN[1], g * 16 + 32)
                if nxt:
                    evac_m(g + 1)
                if out:
                    evac_t3(g - 1)

            act.wait_ge(s["a_kv"], 2)
            act.wait_ge(s["rsq_r"], 2)
            for j in range(GT):
                norm_q(0, j, True)
            evac_t(0)
            evac_q(0, 0)
            evac_m(0)
            act.wait_ge(s["rsq_r"], 4)
            body(0, 0, 0, False, False)
            body(1, 0, 1, log=False)
            with act.Fori(1, B - 1) as b:
                body(b * 2, b, 0)
                body(b * 2 + 1, b, 1)
            body(GROUPS - 2, B - 1, 0)
            body(GROUPS - 1, B - 1, 1, nxt=False)
            body(GROUPS, B, 0, attn=False, nxt=False)
            pair_exp(GROUPS - 1)

            def c_tanh(n, q):
                act.wait_ge(s["cg_r"], n + 1)
                act.activation(CT[:, q], CG[:, q], ACT.Tanh, scale=ALPHA / 2).then_inc(s["ctanh_r"], 1)

            def c_gh(n, q):
                act.wait_ge(s["ctg_mm"], n + 1)
                act.activation(GH[:, q].rearrange("p c t -> p (c t)"), GTP[q][:, 0:E], ACT.Copy)\
                    .then_inc(s["cgh_r"], 1)

            def c_y(n, q, t, first=False):
                act.wait_ge(s["cd_mm"], n + 1)
                if not first:
                    act.wait_ge(YSC[q], 16 * t)
                act.activation(CY[:, q], YP[q][:, 0:D], ACT.Copy, scale=1.0 / YS).then_inc(s["cy_r"], 1)

            act.wait_ge(s["c_tab"], 1)
            act.wait_ge(s["pad_r"], 2)
            pads(act, 1)
            c_tanh(0, 0)
            c_tanh(1, 1)
            c_gh(0, 0)
            c_tanh(2, 0)
            c_gh(1, 1)
            c_y(0, 0, 0, True)
            c_tanh(3, 1)
            c_gh(2, 0)
            c_y(1, 1, 0, True)
            with act.Fori(0, (NSLOT - 5) // 2) as t:
                c_tanh(t * 2 + 4, 0)
                c_gh(t * 2 + 3, 1)
                c_y(t * 2 + 2, 0, t + 1)
                c_tanh(t * 2 + 5, 1)
                c_gh(t * 2 + 4, 0)
                c_y(t * 2 + 3, 1, t + 1)
            c_tanh(NSLOT - 1, 0)
            c_gh(NSLOT - 2, 1)
            c_y(NSLOT - 3, 0, (NSLOT - 3) // 2)
            c_gh(NSLOT - 1, 0)
            c_y(NSLOT - 2, 1, (NSLOT - 3) // 2)
            c_y(NSLOT - 1, 0, (NSLOT - 1) // 2)

        @block.tensor
        def _(pe):
            def turn_a(u, p, k):
                pe.wait_ge(s["a_nrm"], u + 1)
                if u >= 2:
                    pe.wait_ge(s["a_ev"], u - 1)
                for c in range(DC):
                    mm = pe.transpose(TRA[u % 2][:, c * P:(c + 1) * P], XN[p][:, k, c * P:(c + 1) * P], ID32[:, :])
                mm.then_inc(s["a_turn"], 1)

            def shift(p, turns):
                for n, k in enumerate(ORDER):
                    o = k // TPB * TPB + (k + SHIFT_TILES) % TPB
                    pe.wait_ge(s["a_ev"], 16 * p + (o + 1))
                    if n >= 2 or p:
                        pe.wait_ge(s["a_xs"], 16 * p + n - 1)
                    for c in range(DC):
                        mm = pe.matmul(SHA[n % 2][:, 0:D], XNT[p][:, c, o * P:(o + 1) * P], cst_w(C_WSH, D, c),
                                       start=(c == 0), stop=(c == DC - 1))
                    mm.then_inc(s["a_sh"], 1)
                    next(turns, None)

            def turns_1(p):
                for k in range(16):
                    yield turn_a(16 * p + k, p, k)

            def turns_2(p, hs):
                for h in hs:
                    for n, k in enumerate(HALF_TILES[h]):
                        yield turn_a(32 + 16 * p + 8 * h + n, p, k)

            def project(p, h, turns=iter(())):
                pe.wait_ge(s["a_ev"], 32 + 16 * p + 8 * (h + 1))
                w = 2 * p + h
                if w:
                    pe.wait_ge(s["a_wkv"], w)
                    pe.wait_ge(s["a_tanh"], w)
                for kv in range(2):
                    for c in range(DC):
                        for bb in range(2):
                            mm = pe.matmul(KVA[kv][S * bb:S * bb + S, :],
                                           CST[:, C_WKV + c * 2 * S + kv * S:C_WKV + c * 2 * S + kv * S + S],
                                           XST[p][:, h, c, bb * GTOK:(bb + 1) * GTOK],
                                           start=(c == 0), stop=(c == DC - 1))
                            if (kv, c, bb) != (1, DC - 1, 1):
                                next(turns, None)
                mm.then_inc(s["a_kv"], 1)
                next(turns, None)

            def output(p, h):
                pe.wait_ge(s["a_scan"], 2 * p + h + 1)
                for r in range(4):
                    u = 8 * p + 4 * h + r
                    bb = r // 2
                    if u >= 2:
                        pe.wait_ge(s["a_x1"], u - 1)
                    for q in range(2):
                        t0 = (2 * (r % 2) + q) * P
                        mm = pe.matmul(OUA[r % 2][:, q * D:(q + 1) * D], ST[S * bb:S * bb + S, h, t0:t0 + P],
                                       CST[S * bb:S * bb + S, C_WOUT:C_WOUT + D], start=True, stop=True)
                    mm.then_inc(s["a_out"], 1)

            pe.wait_ge(s["consts1"], 4)
            for _ in turns_1(0):
                pass
            pe.wait_ge(s["wsh_done"], 1)
            shift(0, turns_1(1))

            for kv in range(2):
                for hh in range(2):
                    for c in range(DC):
                        mm = pe.matmul(WA[S * hh:S * hh + S, 400 + kv:401 + kv],
                                       CST[:, C_WKV + c * 2 * S + kv * S:C_WKV + c * 2 * S + kv * S + S],
                                       CST[:, C_LNB + c:C_LNB + c + 1], start=(c == 0), stop=(c == DC - 1))
            pe.wait_ge(s["kvc_in"], 16)
            for m in range(DC):
                for c in range(DC):
                    mm = pe.matmul(WK[m][:, 0:B * KEYS], KVC[:, Q_WK + c * D + m * P:Q_WK + c * D + (m + 1) * P],
                                   KVC[:, Q_CTX + c * B * KEYS:Q_CTX + (c + 1) * B * KEYS],
                                   start=(c == 0), stop=(c == DC - 1))
                mm.then_inc(s["k_mm"], 1)
            for b in range(B):
                v = [NUM, DEN][b % 2]
                if b >= 2:
                    pe.wait_ge(s["v_sb"], b - 1)
                for c in range(DC):
                    at = Q_CTX + c * B * KEYS + b * KEYS
                    mm = pe.matmul(v[0:KEYS, 0:D], KVC[:, at:at + KEYS], KVC[:, Q_WV + c * D:Q_WV + (c + 1) * D],
                                   start=(c == 0), stop=(c == DC - 1))
                mm.then_inc(s["v_mm"], 1)

            shift(1, turns_2(0, (0, 1)))
            pe.wait_ge(s["kv_bias_ready"], 1)
            pe.wait_ge(s["v_sb"], B)
            pe.wait_ge(s["wkv_ready"], 1)
            pe.wait_ge(s["k_ready"], DC)
            project(0, 0, turns_2(1, (0,)))
            project(0, 1, turns_2(1, (1,)))
            output(0, 0)
            project(1, 0)
            output(0, 1)
            project(1, 1)
            output(1, 0)
            output(1, 1)

            def turn(src, ready, g, mm_sem):
                for r in range(2):
                    pe.wait_ge(ready, 4 * g + 2 * (r + 1))
                    for j in range(2):
                        for c in range(DC):
                            at = (j * DC + c) * P
                            mm = pe.transpose(WK[r][:, at:at + P], src[:, 2 * r + j, c * P:(c + 1) * P], ID32[:, :])
                    mm.then_inc(mm_sem, 1)

            def s1_turn(g):
                if isinstance(g, int) and g == 1:
                    pe.wait_ge(s["ql_r"], 2)
                elif not (isinstance(g, int) and g == 0):
                    pe.wait_ge(s["x2_r"], 2 * (g - 1))
                turn(XQ, s["xq_r"], g, s["t_mm"])

            def s1_q(g):
                pe.wait_ge(s["xqT_r"], 2 * g + 2)
                for m in range(DC):
                    for c in range(DC):
                        mm = pe.matmul(WK[m][:, :], CST[:, C_WQ + c * D + m * P:C_WQ + c * D + (m + 1) * P],
                                       XQT[:, c, :], start=(c == 0), stop=(c == DC - 1))
                    mm.then_inc(s["q_mm"], 1)

            def s1_max(g, par, b, bp):
                for u in range(16):
                    j, m, half = u // 4, u // 2 % 2, u % 2
                    if u == 0:
                        pe.wait_ge(s["qh_r"], 2 * g + 2)
                        pe.wait_ge(s["kcur_r"], b + 1)
                    if not (isinstance(g, int) and g == 0 and u < 2):
                        pe.wait_ge(s["mx_r"], 16 * g + (u - 1))
                    pe.matmul(MXB[:, half, 0:GK // 2], QH[:, par, m, j * P:(j + 1) * P],
                              KCUR[:, ds(bp, 1), m, 0, 4 * half:4 * half + 4].rearrange("p a h k -> p (a h k)"),
                              start=True, stop=True).then_inc(s["mx_mm"], 1)
                    yield

            def s1_mt(g):
                pe.wait_ge(s["mh_r"], g + 1)
                for j in range(GT):
                    mm = pe.transpose(MTP[j // 2][:, j % 2 * P:(j % 2 + 1) * P], MH[:, j, :], ID16[:, :])
                mm.then_inc(s["mt_mm"], 1)

            def s2_scores(g, par, bp, m, c, units=iter(())):
                if m == 0 and c == 0:
                    pe.wait_ge(s["mT_r"], g + 1)
                    pe.wait_ge(s["ql_r"], 2 * g + 2)
                rows = P if c < NCH - 1 else LAST
                if not (isinstance(g, int) and g == 0 and m == 0 and c < 2):
                    pe.wait_ge(s["exp_r"], g * (2 * NCH) + (m * NCH + c - 1))
                o = SC[(m * NCH + c) % 2][0:rows, :]
                kk = KCUR[:, ds(bp, 1), m].rearrange("p a v h k -> p (a v) (h k)")
                kh, kl = kk[:, 0, c * P:c * P + rows], kk[:, 1, c * P:c * P + rows]
                ind = IND[:, m * GK + c * P:m * GK + c * P + rows]
                pe.matmul(o, ind, MT[:, :], start=True, stop=False)
                next(units, None)
                pe.matmul(o, kh, QL[:, par, m], start=False, stop=False)
                next(units, None)
                pe.matmul(o, kl, QH[:, par, m], start=False, stop=False)
                next(units, None)
                pe.matmul(o, kh, QH[:, par, m], start=False, stop=True).then_inc(s["sc_mm"], 1)
                next(units, None)

            def s2_pv(g, b, m, units=iter(())):
                pe.wait_ge(s["exp_r"], g * (2 * NCH) + (m + 1) * NCH)
                if m == 0:
                    pe.wait_ge(s["vcur_r"], b + 1)
                if not (isinstance(g, int) and g == 0 and m == 0):
                    pe.wait_ge(s["at_r"], 2 * g + m)
                for o, w in ((NUM, VCUR[:, m]), (DEN, MV)):
                    for v in range(2):
                        for j in range(4):
                            rows = P if j + v < NCH - 1 else LAST
                            mm = pe.matmul(o[32 * j:32 * j + 32, :],
                                           w[0:rows, j + v, v].rearrange("p a e -> p (a e)"),
                                           PB[0:rows, j + v, :], start=(v == 0), stop=(v == 1))
                        if (o, v) != (DEN, 1):
                            next(units, None)
                mm.then_inc(s["pv_mm"], 1)
                for _ in units:
                    pass

            def s2_out(g):
                pe.wait_ge(s["at_r"], 2 * g + 2)
                if isinstance(g, int) and g == 0:
                    pe.wait_ge(s["ql_r"], 4)
                else:
                    pe.wait_ge(s["x3T_r"], 2 * g)
                for j in range(GT):
                    for c in range(DC):
                        mm = pe.matmul(WK[j // 2][:, (j % 2) * D:(j % 2 + 1) * D], AT[:, c, j * P:(j + 1) * P],
                                       cst_w(C_WO, D, c), start=(c == 0), stop=(c == DC - 1))
                    if j % 2:
                        mm.then_inc(s["out_mm"], 1)

            def s3_turn(g, nxt):
                if nxt:
                    pe.wait_ge(s["ql_r"], 2 * g + 6)
                turn(X3, s["xn3_r"], g, s["t3_mm"])

            def s3_logits(g):
                pe.wait_ge(s["x3T_r"], 2 * g + 2)
                for j in range(GT):
                    for c in range(DC):
                        mm = pe.matmul(LGP[:, j * NEXP:(j + 1) * NEXP], X3T[:, c, j * P:(j + 1) * P],
                                       cst_w(C_WG, NEXP, c), start=(c == 0), stop=(c == DC - 1))
                mm.then_inc(s["lg_mm"], 1)

            def s3_prefix(g):
                pe.wait_ge(s["ms_r"], g + 1)
                ms = MS16[:, :, :].rearrange("p j e -> p (j e)")
                pe.matmul(UPP, UP16[:, :], ms, start=True, stop=True)
                pe.matmul(ONP, ON16[:, :], ms, start=True, stop=True).then_inc(s["px_mm"], 1)

            def body(g, b, par, bp, b1, bp1, out=True, log=True, attn=True, nxt=True):
                if attn:
                    for c in range(NCH):
                        s2_scores(g, par, bp, 0, c)
                if log:
                    if not nxt:
                        pe.wait_ge(s["run_s"], 5 * (g - 2))
                    s3_logits(g - 2)
                if out:
                    s2_out(g - 1)
                if nxt:
                    s1_turn(g + 1)
                if log:
                    s3_prefix(g - 2)
                if attn:
                    s2_pv(g, b, 0)
                if nxt:
                    s1_q(g + 1)
                if attn:
                    if log and nxt:
                        pe.wait_ge(s["run_s"], 5 * (g - 1))
                    units = s1_max(g + 1, 1 - par, b1, bp1) if nxt else iter(())
                    for c in range(NCH):
                        s2_scores(g, par, bp, 1, c, units if c >= 1 else iter(()))
                    s2_pv(g, b, 1, units)
                if nxt:
                    s1_mt(g + 1)
                if out:
                    s3_turn(g - 1, nxt)

            pe.wait_ge(s["a_x1"], 16)
            pe.wait_ge(s["consts_ready"], 1)
            pe.wait_ge(s["ind_ready"], 1)
            s1_turn(0)
            s1_q(0)
            for _ in s1_max(0, 0, 0, 0):
                pass
            s1_mt(0)
            body(0, 0, 0, 0, 0, 0, False, False)
            body(1, 0, 1, 0, 1, 1, log=False)
            with pe.Fori(1, B - 1) as b:
                body(b * 2, b, 0, b % 2, b, b % 2)
                body(b * 2 + 1, b, 1, b % 2, b + 1, (b + 1) % 2)
            body(GROUPS - 2, B - 1, 0, 1, B - 1, 1)
            body(GROUPS - 1, B - 1, 1, 1, None, None, nxt=False)
            body(GROUPS, None, 0, None, None, None, attn=False, nxt=False)
            pe.wait_ge(s["run_s"], 5 * (GROUPS - 1))
            s3_logits(GROUPS - 1)
            s3_prefix(GROUPS - 1)

            pe.wait_ge(s["c_tabe"], 19)
            pe.wait_ge(s["run_s"], 5 * GROUPS)
            pe.matmul(NUM[:, 0:P], ON16[:, :], DIAG, start=True, stop=True).then_inc(s["c_mm"], 1)
            pe.transpose(WA[0:1, 0:P], CW[:, 0, 0:1], ID32[:, :])
            pe.transpose(WA[0:1, P:2 * P], CW[:, 0, 1:2], ID32[:, :]).then_inc(s["c_mm"], 1)
            pe.transpose(WB[0:2 * NEXP, 0:P], CW[:, 8:10].rearrange("p a e -> p (a e)"), ID32[:, :])\
                .then_inc(s["c_mm"], 1)
            pe.wait_ge(s["c_cp"], 2)
            pe.wait_ge(s["w_split"], NPIECE)
            pe.wait_ge(s["bex_ready"], 1)

            def c_turn(n, q, t):
                pe.wait_ge(RINS[q], 16 * (t + 1))
                if not isinstance(n, int) or n >= 2:
                    pe.wait_ge(s["cxt_r"], n - 1)
                rows = RIN[:, q, 0:D].bitcast(F16)
                for v in range(4):
                    mm = pe.transpose(XTP[q][:, v * P:(v + 1) * P], rows[:, v * P:(v + 1) * P], ID16[:, :])
                mm.then_inc(s["ct_mm"], 1)

            w_experts = w_flat.rearrange("p (e w) -> p e w", w=WEX)

            def w_at(e, at, n):
                return w_experts[:, ds(e, 1), at:at + n].rearrange("p a w -> p (a w)")

            def expert(n):
                return pe.value_load(TAB[0:1, ds(n, 1)], min_val=0, max_val=NEXP - 1)

            def selector(n):
                return OHT[0:2 * NEXP, ds(n, 1)].broadcast_to([2 * NEXP, P])

            def c_gu(n, q, e):
                if not isinstance(n, int) or n >= 2:
                    pe.wait_ge(s["cu_r"], n - 1)
                pe.wait_ge(s["cxt_r"], n + 1)
                pe.matmul(GUP[q], selector(n), BEX[:, 0:F], start=True, stop=False)
                for c in range(DC):
                    pe.matmul(GUP[q], XTS[:, q, c], w_at(e, c * 2 * PW + LOW, F), start=False, stop=False)
                    pe.matmul(GUP[q], XTS[:, q, c], w_at(e, c * 2 * PW, F), start=False, stop=False)
                for c in range(DC):
                    mm = pe.matmul(GUP[q], XTS[:, q, 2 + c], w_at(e, c * 2 * PW, F), start=False,
                                   stop=(c == DC - 1))
                mm.then_inc(s["cgu_mm"], 1)

            def c_tg(n, q):
                pe.wait_ge(s["cgd_r"], n + 1)
                if not isinstance(n, int) or n >= 2:
                    pe.wait_ge(s["cgl_r"], n - 1)
                for c in range(DC):
                    mm = pe.transpose(GTP[q][:, c * P:(c + 1) * P], CGD[:, q, c * P:(c + 1) * P], ID32[:, :])
                mm.then_inc(s["ctg_mm"], 1)

            def c_down(n, q, e):
                if not isinstance(n, int) or n >= 2:
                    pe.wait_ge(s["cy_r"], n - 1)
                pe.wait_ge(s["cgl_r"], n + 1)
                pe.matmul(YP[q][:, 0:D], selector(n), BEX[:, F:F + E], start=True, stop=False)
                for c in range(DC):
                    pe.matmul(YP[q][:, 0:D], GH[:, q, c], w_at(e, W_DOWN + LOW + c * E, E), start=False, stop=False)
                    pe.matmul(YP[q][:, 0:D], GH[:, q, c], w_at(e, W_DOWN + c * E, E), start=False, stop=False)
                for c in range(DC):
                    mm = pe.matmul(YP[q][:, 0:D], GL[:, q, c], w_at(e, W_DOWN + c * E, E), start=False,
                                   stop=(c == DC - 1))
                mm.then_inc(s["cd_mm"], 1)

            c_turn(0, 0, 0)
            c_turn(1, 1, 0)
            c_gu(0, 0, expert(0))
            c_turn(2, 0, 1)
            c_gu(1, 1, expert(1))
            c_tg(0, 0)

            c_turn(3, 1, 1)
            c_gu(2, 0, expert(2))

            def steps(t):
                four = pe.value_load(QUAD[0:1, ds(t, 1)], min_val=0, max_val=NEXP ** 4 - 1)
                c_tg(t * 2 + 1, 1)
                c_down(t * 2, 0, four % NEXP)
                c_turn(t * 2 + 4, 0, t + 2)
                c_gu(t * 2 + 3, 1, four // NEXP ** 2 % NEXP)
                c_tg(t * 2 + 2, 0)
                c_down(t * 2 + 1, 1, four // NEXP % NEXP)
                c_turn(t * 2 + 5, 1, t + 2)
                c_gu(t * 2 + 4, 0, four // NEXP ** 3)

            steps(0)
            with pe.Fori(1, (NSLOT - 5) // 2) as t:
                steps(t)
            c_tg(NSLOT - 4, 1)
            c_down(NSLOT - 5, 0, expert(NSLOT - 5))
            c_turn(NSLOT - 1, 0, (NSLOT - 1) // 2)
            c_gu(NSLOT - 2, 1, expert(NSLOT - 2))
            c_tg(NSLOT - 3, 0)
            c_down(NSLOT - 4, 1, expert(NSLOT - 4))
            c_gu(NSLOT - 1, 0, expert(NSLOT - 1))
            c_tg(NSLOT - 2, 1)
            c_down(NSLOT - 3, 0, expert(NSLOT - 3))
            c_tg(NSLOT - 1, 0)
            c_down(NSLOT - 2, 1, expert(NSLOT - 2))
            c_down(NSLOT - 1, 0, expert(NSLOT - 1))

        @block.vector
        def _(dve):
            def prepare():
                dve.wait_ge(s["small_ready"], 1)
                dve.wait_ge(s["k_hi"], 1)
                dve.tensor_scalar(SMALL[:, 5:6], WA[:, 400:401], 0.5, None, ALU.mult)
                dve.tensor_copy(SMALL[:, 6:7], WA[:, 401:402]).then_inc(s["kv_bias_ready"], 1)
                for c in range(DC):
                    w = cst_w(C_WKV, 2 * S, c)
                    ins = dve.tensor_scalar(w, w, CST[:, C_LNW + c:C_LNW + c + 1], None, ALU.mult)
                ins.then_inc(s["wkv_ready"], 1)
                for m in range(DC):
                    dve.wait_ge(s["k_hi"], m + 1)
                    if m:
                        dve.wait_ge(s["k_ready"], m)
                    dve.tensor_scalar(KTMP, WK[m][:, 0:B * KEYS], 0.25, SMALL[:, 2 + m:3 + m], ALU.mult, ALU.add)\
                        .then_inc(s["k_tmp"], 1)
                    dve.wait_ge(s["k_tmp"], m + 1)
                    dve.tensor_tensor(KRAW[:, 1, m].rearrange("p b k -> p (b k)"), KTMP,
                                      KRAW[:, 0, m].rearrange("p b k -> p (b k)"), ALU.subtract)\
                        .then_inc(s["k_ready"], 1)
                for b in range(B):
                    dve.wait_ge(s["v_mm"], b + 1)
                    v = [NUM, DEN][b % 2]
                    dve.tensor_tensor(VSB[:, b], v[0:KEYS, 0:D], KVC[0:KEYS, Q_BV:Q_BV + D], ALU.add)\
                        .then_inc(s["v_sb"], 1)

            def biases():
                dve.wait_ge(s["bex_in"], 16)
                br = BRAW[0:2 * NEXP, 0:F + E]
                dve.tensor_scalar(br[:, 0:F], br[:, 0:F], GUS / ONE, None, ALU.mult)
                dve.tensor_scalar(br[:, F:F + E], br[:, F:F + E], YS / ONE, None, ALU.mult).then_inc(s["bex_s"], 1)
                dve.wait_ge(s["bex_s"], 1)
                dve.tensor_copy(BEX[:, :], br).then_inc(s["bex_s"], 1)
                dve.wait_ge(s["bex_s"], 2)
                dve.tensor_tensor(br, br, BEX[:, :], ALU.subtract).then_inc(s["bex_s"], 1)
                dve.wait_ge(s["consts_ready"], 1)
                mhi, mlo = SMALL[0:2 * NEXP, 8:9], SMALL[0:2 * NEXP, 9:10]
                dve.tensor_copy(mhi, MK[0:2 * NEXP, 0:1])
                dve.tensor_copy(mlo, MK[0:2 * NEXP, 1:2]).then_inc(s["bex_s"], 1)
                dve.wait_ge(s["bex_s"], 4)
                dve.tensor_scalar(br, br, mlo, None, ALU.mult).then_inc(s["bex_s"], 1)
                dve.wait_ge(s["bex_s"], 5)
                dve.scalar_tensor_tensor(out=BEX[:, :], in0=BEX[:, :], scalar=mhi, in1=br, op0=ALU.mult,
                                         op1=ALU.add).then_inc(s["bex_ready"], 1)

            def vcur(b):
                dve.wait_ge(s["v_in"], (b + 1) * (32 * DC))
                for m in range(DC):
                    for n in range(2):
                        rows, c0, c1 = (P, 0, NCH - 1) if n == 0 else (LAST, NCH - 1, NCH)
                        vf = VFLAT[0:rows, m, c0:c1, :]
                        nn = c1 - c0
                        ins = dve.tensor_tensor(
                            VCUR[0:rows, m, c0:c1].rearrange("p n v a e -> p n (v a) e"),
                            vf.unsqueeze(2).broadcast_to([rows, nn, 4, HD]),
                            MV[0:rows, c0:c1].rearrange("p n v a e -> p n (v a) e"), ALU.mult)
                ins.then_inc(s["vcur_r"], 1)

            def stats_1(p):
                for q in range(2):
                    dve.wait_ge(XIN[2 * p + q], 16)
                    for k in range(8 * q, 8 * q + 8):
                        ins = dve.bn_stats(STAT[:, p, k, :], X[:, 16 * p + k, :])
                    ins.then_inc(s["a_stat"], 1)
                    dve.wait_ge(s["a_stat"], 2 * p + q + 1)
                    for k in range(8 * q, 8 * q + 8):
                        ins = dve.bn_aggr(MVA[:, p, k, :], STAT[:, p, k, :])
                    ins.then_inc(s["a_aggr"], 1)

            def shifted(p):
                dve.wait_ge(s["a_aggr"], 2 * p + 2)
                dve.wait_ge(s["a_rs"], 2 * p + 2)
                for h in range(2):
                    for n, k in enumerate(HALF_TILES[h]):
                        u = 16 * p + 8 * h + n
                        dve.wait_ge(s["a_sh"], u + 1)
                        dve.wait_ge(s["a_xg"], u + 1)
                        dve.tensor_tensor(XN[p][:, k, :], XN[p][:, k, :], SHA[n % 2][:, 0:D], ALU.add)\
                            .then_inc(s["a_xs"], 1)
                        if n:
                            dve.wait_ge(s["a_xs"], u)
                            dve.bn_stats(STAT[:, p, 8 * h + n - 1, :], XN[p][:, HALF_TILES[h][n - 1], :])
                    dve.wait_ge(s["a_xs"], 16 * p + 8 * h + 8)
                    dve.bn_stats(STAT[:, p, 8 * h + 7, :], XN[p][:, HALF_TILES[h][7], :]).then_inc(s["a_stat2"], 1)
                    dve.wait_ge(s["a_stat2"], 2 * p + h + 1)
                    for n in range(8 * h, 8 * h + 8):
                        ins = dve.bn_aggr(MVA[:, p, n, :], STAT[:, p, n, :])
                    ins.then_inc(s["a_aggr2"], 1)

            def recur(p, h):
                w = 2 * p + h
                dve.wait_ge(s["a_exp"], w + 1)
                dve.scalar_tensor_tensor(out=TW, in0=KVA[1][:, :], scalar=SMALL[:, 6:7], in1=TW,
                                         op0=ALU.add, op1=ALU.mult).then_inc(s["a_wkv"], 1)
                dve.wait_ge(s["a_wkv"], w + 1)
                if p:
                    dve.wait_ge(s["a_out"], 4 * (h + 1))
                if h:
                    dve.wait_ge(s["a_scan"], w)
                dve.tensor_tensor_scan(ST[:, h, :], SMALL[:, 0:1].broadcast_to([P, GTOK]), TW,
                                       ST[:, 0, GTOK - 1:GTOK] if h else 0.0, ALU.mult, ALU.add)\
                    .then_inc(s["a_scan"], 1)

            def add_1(p, h):
                for r in range(4):
                    u = 8 * p + 4 * h + r
                    i = 16 * p + (r // 2) * TPB + 4 * h + 2 * (r % 2)
                    dve.wait_ge(s["a_out"], u + 1)
                    xt = X[:, i:i + 2, :].rearrange("p a d -> p (a d)")
                    dve.tensor_tensor(xt, xt, OUA[r % 2][:, :], ALU.add).then_inc(s["a_x1"], 1)

            def stats_q(p):
                dve.wait_ge(s["a_x1"], 8 * (p + 1))
                dve.wait_ge(s["a_aggr2"], 2 * p + 2)
                for k in range(16):
                    ins = dve.bn_stats(STAT[:, p, k, :], X[:, 16 * p + k, :])
                ins.then_inc(s["stq"], 1)
                dve.wait_ge(s["stq"], p + 1)
                for k in range(16):
                    ins = dve.bn_aggr(MVQ[:, 16 * p + k, :], STAT[:, p, k, :])
                ins.then_inc(s["vaq"], 1)

            stats_1(0)
            dve.wait_ge(s["gate_tanh"], 1)
            gate = CST[:, C_GATE:C_GATE + D]
            for c in range(DC):
                w = cst_w(C_WSH, D, c)
                dve.scalar_tensor_tensor(out=w, in0=gate, scalar=1.0, in1=w, op0=ALU.add, op1=ALU.mult)\
                    .then_inc(s["wsh_ready"], 1)
            dve.wait_ge(s["wsh_ready"], 2)
            for c in range(DC):
                w = cst_w(C_WSH, D, c)
                dve.tensor_scalar(w, w, 0.5, None, ALU.mult)
            dve.tensor_scalar(gate, gate, -0.5, 0.5, ALU.mult, ALU.add).then_inc(s["wsh_done"], 1)
            dve.wait_ge(s["etf_exp"], 2)
            dve.tensor_scalar(SMALL[:, 2:4], CST[:, C_BK:C_BK + DC], 0.25, None, ALU.mult)
            dve.tensor_scalar(SMALL[:, 4:5], SMALL[:, 1:2], -0.5, None, ALU.mult).then_inc(s["small_ready"], 1)
            stats_1(1)
            shifted(0)
            prepare()
            biases()
            shifted(1)
            recur(0, 0)
            recur(0, 1)
            add_1(0, 0)
            recur(1, 0)
            add_1(0, 1)
            stats_q(0)
            recur(1, 1)
            add_1(1, 0)
            add_1(1, 1)
            stats_q(1)

            def s1_ql(g, par):
                for m in range(DC):
                    dve.wait_ge(s["qh_r"], 2 * g + m + 1)
                    dve.scalar_tensor_tensor(out=QL[:, par, m], in0=WK[m][:, :], scalar=CST[:, C_BQ + m:C_BQ + m + 1],
                                             in1=QH[:, par, m], op0=ALU.add, op1=ALU.subtract).then_inc(s["ql_r"], 1)

            def s1_max(g):
                for u in range(16):
                    j, m, half = u // 4, u // 2 % 2, u % 2
                    dve.wait_ge(s["mx_mm"], 16 * g + (u + 1))
                    dve.tensor_reduce(MX[:, j, m * HG + 4 * half:m * HG + 4 * half + 4],
                                      MXB[:, half, 0:GK // 2].rearrange("p (h k) -> p h k", k=KEYS),
                                      AX.X, ALU.max).then_inc(s["mx_r"], 1)

            def s1_mh(g):
                dve.wait_ge(s["mx_r"], 16 * g + 16)
                dve.tensor_scalar(MH[:, :, 0:HEADS], MX[:, :, :], -1.0, None, ALU.mult).then_inc(s["mh_s"], 1)
                dve.wait_ge(s["mh_s"], g + 1)
                dve.scalar_tensor_tensor(out=MH[:, :, HEADS:2 * HEADS], in0=MX[:, :, :], scalar=-1.0,
                                         in1=MH[:, :, 0:HEADS], op0=ALU.mult, op1=ALU.subtract)\
                    .then_inc(s["mh_r"], 1)

            def s2_attn(g, m):
                dve.wait_ge(s["pv_mm"], 2 * g + (m + 1))
                dve.reciprocal(AT[:, m], DEN[:, :]).then_inc(s["rec_s"], 1)
                dve.wait_ge(s["rec_s"], 2 * g + (m + 1))
                dve.tensor_tensor(AT[:, m], AT[:, m], NUM[:, :], ALU.mult).then_inc(s["at_r"], 1)

            def s2_x2(g):
                for r in range(2):
                    dve.wait_ge(s["out_mm"], 2 * g + (r + 1))
                    if r == 0:
                        dve.wait_ge(s["xb_r"], g + 1)
                    xt = X[:, ds(g * GT + 2 * r, 2), :].rearrange("p a d -> p (a d)")
                    dve.tensor_tensor(xt, xt, WK[r][:, :], ALU.add).then_inc(s["x2_r"], 1)

            def s3_stats(g):
                dve.wait_ge(s["x2_r"], 2 * g + 2).then_inc(s["dve_past"], 1)
                for j in range(GT):
                    ins = dve.bn_stats(STAT3[:, j, :], X[:, ds(g * GT + j, 1), :].rearrange("p a d -> p (a d)"))
                ins.then_inc(s["st3"], 1)
                dve.wait_ge(s["st3"], g + 1).then_inc(s["dve_past"], 1)
                if not (isinstance(g, int) and g == 0):
                    dve.wait_ge(s["rs3_r"], g).then_inc(s["dve_past"], 1)
                for j in range(GT):
                    ins = dve.bn_aggr(MVA3[:, j, :], STAT3[:, j, :])
                ins.then_inc(s["va3"], 1)

            def s3_logits(g, par, k):
                dve.wait_ge(s["lg_mm"], g + 1)
                dve.scalar_tensor_tensor(
                    out=LG[:, :, :], in0=LGP.rearrange("p (j e) -> p j e", j=GT), scalar=1.0 / XSC,
                    in1=CST[:, C_BG:C_BG + NEXP].unsqueeze(1).broadcast_to([P, GT, NEXP]),
                    op0=ALU.mult, op1=ALU.add).then_inc(s["lg_r"], 1)
                dve.wait_ge(s["lg_r"], g + 1).then_inc(s["dve_past"], 1)
                for j in range(GT):
                    ins = dve.max(M8[:, j, :], LG[:, j, :])
                ins.then_inc(s["top_r"], 1)
                dve.wait_ge(s["top_r"], g + 1)
                dve.tensor_tensor(RD[:, 0, :], M8[:, :, 1], M8[:, :, 0], ALU.subtract).then_inc(s["rd_s"], 1)
                for j in range(GT):
                    ins = dve.max_index(I8[:, j, :], M8[:, j, :], LG[:, j, :])
                ins.then_inc(s["ix_r"], 1)
                dve.wait_ge(s["ix_r"], g + 1)
                dve.tensor_copy(IF[:, :, :], I8[:, :, 0:TOPK]).then_inc(s["if_r"], 1)
                dve.wait_ge(s["if_r"], g + 1)
                for q in range(TOPK):
                    ins = dve.tensor_tensor(MS[:, q], IOTA[:, :].unsqueeze(1).broadcast_to([P, GT, NEXP]),
                                            IF[:, :, q:q + 1].broadcast_to([P, GT, NEXP]), ALU.is_equal)
                ins.then_inc(s["ms_s"], 1)
                dve.wait_ge(s["ms_s"], g + 1)
                dve.tensor_tensor(MS16[:, :, :], MS[:, 0], MS[:, 1], ALU.add).then_inc(s["ms_r"], 1)
                if not (isinstance(k, int) and k == 0):
                    dve.wait_ge(SCT[par], k * (16 * TOPK * GT))
                dve.tensor_copy(RB[:, par, :, D], TOKF[:, ds(g * GT, GT)])
                dve.tensor_copy(RB[:, par, :, D + 1], IF[:, :, 0])

            def s3_slots(g, par):
                dve.wait_ge(s["rd_e"], g + 1)
                dve.tensor_scalar(RD[:, 2, :], RD[:, 1, :], 1.0, None, ALU.add).then_inc(s["rd_r"], 1)
                dve.wait_ge(s["rd_r"], 2 * g + 1)
                dve.reciprocal(RW[:, 0, ds(g * GT, GT)], RD[:, 2, :]).then_inc(s["rd_r"], 1)
                dve.wait_ge(s["rd_r"], 2 * g + 2)
                dve.tensor_tensor(RW[:, 1, ds(g * GT, GT)], RD[:, 1, :], RW[:, 0, ds(g * GT, GT)], ALU.mult)
                dve.wait_ge(s["px_mm"], g + 1)
                for j in range(GT):
                    dve.tensor_tensor(RUN[:, j + 1, :], RUN[:, j, :], ONP[:, j * NEXP:(j + 1) * NEXP], ALU.add)\
                        .then_inc(s["run_s"], 1)
                    dve.wait_ge(s["run_s"], 5 * g + (j + 1))
                dve.tensor_tensor(LG[:, :, :], RUN[:, 0:GT, :], UPP.rearrange("p (j e) -> p j e", j=GT),
                                  ALU.add).then_inc(s["run_s"], 1)
                dve.wait_ge(s["run_s"], 5 * g + 5)
                dve.tensor_copy(RUN[:, 0, :], RUN[:, GT, :]).then_inc(s["pos_s"], 1)
                for q in range(TOPK):
                    ins = dve.tensor_tensor(MS[:, q], MS[:, q], LG[:, :, :], ALU.mult)
                ins.then_inc(s["sl_s"], 1)
                dve.wait_ge(s["sl_s"], g + 1)
                dve.tensor_reduce(SLF[:, :, :], MS[:, :, :, :], AX.X, ALU.add).then_inc(s["slf_s"], 1)
                dve.wait_ge(s["slf_s"], g + 1)
                dve.tensor_copy(SLOT[:, par], SLF[:, :, :]).then_inc(s["slot_r"], 1)

            def body(g, b, par, b1=None, out=True, log=True, attn=True, nxt=True):
                if log:
                    s3_logits(g - 2, par, b - 1)
                if out:
                    s2_x2(g - 1)
                    s3_stats(g - 1)
                if log:
                    s3_slots(g - 2, par)
                if attn:
                    s2_attn(g, 0)
                if nxt:
                    s1_ql(g + 1, 1 - par)
                    s1_max(g + 1)
                    s1_mh(g + 1)
                if b1 is not None:
                    dve.wait_ge(s["pv_mm"], 2 * g + 2)
                    vcur(b1)
                if attn:
                    s2_attn(g, 1)

            vcur(0)
            s1_ql(0, 0)
            s1_max(0)
            s1_mh(0)
            body(0, 0, 0, out=False, log=False)
            body(1, 0, 1, 1, log=False)
            with dve.Fori(1, B - 1) as b:
                body(b * 2, b, 0)
                body(b * 2 + 1, b, 1, b + 1)
            body(GROUPS - 2, B - 1, 0)
            body(GROUPS - 1, B - 1, 1, nxt=False)
            body(GROUPS, B, 0, attn=False, nxt=False)
            s3_logits(GROUPS - 1, 1, B - 1)
            s3_slots(GROUPS - 1, 1)

            dve.wait_ge(s["lo_r"], GROUPS)
            dve.wait_ge(s["pos_s"], GROUPS)
            dve.tensor_copy(RUNI, RUN[:, 0, :]).then_inc(s["c_tab"], 1)
            steps = [0]

            def link(ins):
                steps[0] += 1
                ins.then_inc(s["c_tabe"], 1)
                dve.wait_ge(s["c_tabe"], steps[0])

            cnt, nt, end, le, tmp = (CW[:, 1 + a] for a in range(5))
            link(dve.tensor_tensor(cnt, RUN[:, 0, :], ECAP[:, :], ALU.subtract))
            link(dve.tensor_scalar(CWI, cnt, float(P - 1), None, ALU.add))
            link(dve.tensor_scalar(CWI, CWI, 7, None, ALU.arith_shift_right))
            link(dve.tensor_copy(nt, CWI))
            link(dve.tensor_scalar(tmp, nt, 0.0, 1.0, ALU.mult, ALU.add))
            link(dve.tensor_tensor_scan(end, tmp, nt, 0.0, ALU.mult, ALU.add))
            pidx = CW[:, 7, 0:1]
            link(dve.tensor_copy(pidx, TOK[:, 0:1]))
            link(dve.tensor_scalar(le, end, pidx, None, ALU.is_le))
            link(dve.tensor_tensor(tmp, le, nt, ALU.mult))
            ei, done = CW[:, 6, 0:1], CW[:, 6, 1:2]
            link(dve.tensor_reduce(ei, le, AX.X, ALU.add))
            link(dve.tensor_reduce(done, tmp, AX.X, ALU.add))
            j_in = CW[:, 6, 2:3]
            link(dve.tensor_tensor(j_in, pidx, done, ALU.subtract))
            link(dve.tensor_scalar(j_in, j_in, float(P), None, ALU.mult))
            row = CW[:, 0, 1:2]
            link(dve.scalar_tensor_tensor(out=row, in0=ei, scalar=float(CAP), in1=j_in, op0=ALU.mult, op1=ALU.add))
            link(dve.tensor_scalar(row, row, float(NEXP * CAP), None, ALU.min))
            link(dve.tensor_scalar(CW[:, 0, 0:1], ei, float(NEXP - 1), None, ALU.min))
            link(dve.tensor_scalar(DIAG, ID16[:, :], CW[:, 0, 0:1], None, ALU.mult))
            for v in range(2):
                link(dve.tensor_scalar(CW[:, 8 + v], IOTA[:, :], CW[:, 0, 0:1], ONE, ALU.is_equal, ALU.mult))
            dve.wait_ge(s["c_mm"], 3)
            dve.tensor_copy(EXB, NUM[:, 0:P]).then_inc(s["eb_r"], 1)
            dve.tensor_copy(TAB[0:1, :], WA[0:1, 0:2 * P])
            dve.tensor_copy(PAIR[0:1, 0:P], WA[0:1, 0:P]).then_inc(s["quad_s"], 1)
            dve.wait_ge(s["quad_s"], 1)
            odd = PAIR[0:1, 0:P].rearrange("p (t v) -> p t v", v=2)
            dve.scalar_tensor_tensor(out=PAIR[0:1, P:P + P // 2], in0=odd[:, :, 1], scalar=float(NEXP),
                                     in1=odd[:, :, 0], op0=ALU.mult, op1=ALU.add)
            dve.scalar_tensor_tensor(out=PAIR[0:1, P + P // 2:2 * P - 1], in0=odd[:, 1:, 0], scalar=float(NEXP),
                                     in1=odd[:, 0:P // 2 - 1, 1], op0=ALU.mult, op1=ALU.add)\
                .then_inc(s["quad_s"], 1)
            dve.wait_ge(s["quad_s"], 2)
            dve.scalar_tensor_tensor(out=QUAD[0:1, 0:P // 2 - 2], in0=PAIR[0:1, P + P // 2 + 1:2 * P - 1],
                                     scalar=float(NEXP ** 2), in1=PAIR[0:1, P:P + P // 2 - 2],
                                     op0=ALU.mult, op1=ALU.add).then_inc(s["c_cp"], 1)
            dve.tensor_copy(OHT[0:2 * NEXP], WB[0:2 * NEXP, 0:P]).then_inc(s["c_cp"], 1)
            dve.wait_ge(s["c_cp"], 2)

            def c_xt(n, q):
                dve.wait_ge(s["ct_mm"], n + 1)
                dve.tensor_copy(XTS[:, q].rearrange("p v t -> p (v t)"), XTP[q]).then_inc(s["cxt_r"], 1)

            def c_gate(n, q):
                dve.wait_ge(s["cgu_mm"], n + 1)
                dve.tensor_scalar(CG[:, q], GUP[q][:, 0:E], 1.0 / GUS, LIMIT, ALU.mult, ALU.min)\
                    .then_inc(s["cg_r"], 1)
                dve.tensor_scalar(CU[:, q], GUP[q][:, E:F], LIMIT * GUS, -LIMIT * GUS, ALU.min, ALU.max)\
                    .then_inc(s["cu_r"], 1)

            def c_glu(n, q):
                dve.wait_ge(s["ctanh_r"], n + 1)
                dve.scalar_tensor_tensor(out=CT[:, q], in0=CT[:, q], scalar=1.0, in1=CG[:, q],
                                         op0=ALU.add, op1=ALU.mult).then_inc(s["ct1_r"], 1)
                dve.wait_ge(s["ct1_r"], n + 1)
                dve.wait_ge(s["cu_r"], n + 1)
                dve.scalar_tensor_tensor(out=CGD[:, q], in0=CU[:, q], scalar=GUS, in1=CT[:, q],
                                         op0=ALU.add, op1=ALU.mult).then_inc(s["cgd_r"], 1)

            def c_gl(n, q):
                dve.wait_ge(s["cgh_r"], n + 1)
                dve.tensor_tensor(GL[:, q].rearrange("p c t -> p (c t)"), GTP[q][:, 0:E],
                                  GH[:, q].rearrange("p c t -> p (c t)"), ALU.subtract).then_inc(s["cgl_r"], 1)

            c_xt(0, 0)
            c_xt(1, 1)
            c_gate(0, 0)
            c_glu(0, 0)
            c_xt(2, 0)
            c_gate(1, 1)
            c_gl(0, 0)
            c_glu(1, 1)
            with dve.Fori(0, (NSLOT - 3) // 2) as t:
                c_xt(t * 2 + 3, 1)
                c_gate(t * 2 + 2, 0)
                c_gl(t * 2 + 1, 1)
                c_glu(t * 2 + 2, 0)
                c_xt(t * 2 + 4, 0)
                c_gate(t * 2 + 3, 1)
                c_gl(t * 2 + 2, 0)
                c_glu(t * 2 + 3, 1)
            c_gate(NSLOT - 1, 0)
            c_gl(NSLOT - 2, 1)
            c_glu(NSLOT - 1, 0)
            c_gl(NSLOT - 1, 0)

            for c in range(YCH):
                dve.wait_ge(YIN[c], 32)
                for i in range(YT * c, YT * (c + 1)):
                    dve.scalar_tensor_tensor(out=X[:, i, :], in0=Y01[:, 0, i, :], scalar=RW[:, 0, i:i + 1],
                                             in1=X[:, i, :], op0=ALU.mult, op1=ALU.add).then_inc(s["f_s"], 1)
                for i in range(YT * c, YT * (c + 1)):
                    dve.wait_ge(s["f_s"], i + 1)
                    dve.scalar_tensor_tensor(out=X[:, i, :], in0=Y01[:, 1, i, :], scalar=RW[:, 1, i:i + 1],
                                             in1=X[:, i, :], op0=ALU.mult, op1=ALU.add).then_inc(s["f_r"], 1)


def kernel(**inputs):
    import numpy as np
    import concourse.bacc as bacc
    from concourse.bass_utils import run_bass_kernel_spmd

    a = {k: np.asarray(v) for k, v in inputs.items()}

    def chunks(w):
        return w.reshape(DC, P, -1).transpose(1, 0, 2).reshape(P, -1)

    def rows(v):
        return np.broadcast_to(v[None, :], (P, v.shape[0]))

    def cols(v):
        return v.reshape(DC, P).T

    def both(v):
        return np.concatenate([v, v], 0)

    cst = np.concatenate([
        chunks(a["L0_attn_W_shift"].T), rows(a["L0_attn_shift_gate"]),
        chunks(np.concatenate([a["L0_attn_W_key"].T, a["L0_attn_W_value"].T], 1)),
        cols(a["L0_attn_ln_w"]), cols(a["L0_attn_ln_b"]),
        both(a["L0_attn_time_decay"][:, None]), both(a["L0_attn_time_first"][:, None]),
        both(a["L0_attn_W_output"].T),
        chunks(a["L0_xattn_wq"].T), chunks(a["L0_xattn_wo"].T),
        cols(a["L0_xattn_bq"]), cols(a["L0_xattn_bk"]), rows(a["L0_xattn_bo"]),
        chunks(a["L0_ffn_Wg"].T), rows(a["L0_ffn_bg"])], 1)
    ctx_t = a["ctx_1024"].reshape(B * KEYS, D).T
    kvc = np.concatenate([chunks(a["L0_xattn_wk"].T), chunks(a["L0_xattn_wv"].T), rows(a["L0_xattn_bv"]),
                          chunks(ctx_t)], 1)

    def apart(w):
        return np.concatenate([w[..., 0::2], w[..., 1::2]], -1)

    def by_part(w):
        return w.reshape(NEXP, DC, P, -1).transpose(0, 2, 1, 3).reshape(NEXP, P, -1)

    wexp = np.concatenate([by_part(apart(a["L0_ffn_Wgu"])), by_part(a["L0_ffn_Wd"])], 2)
    wexp = wexp.reshape(NEXP, P, PIECES, PW).transpose(0, 2, 1, 3).reshape(NPIECE, P, PW)
    bexp = np.concatenate([apart(a["L0_ffn_bgu"]), a["L0_ffn_bd"]], 1)
    bexp = np.concatenate([bexp, bexp], 0)
    arrays = {"x": a["x"].reshape(NTOK, D), "cst": cst, "kvc": kvc, "wexp": wexp, "bexp": bexp}
    arrays = {f"in_{n}": np.ascontiguousarray(v) for n, v in arrays.items()}
    nc = bacc.Bacc("TRN2", target_bir_lowering=False, num_devices=1)
    args = [nc.dram_tensor(n, v.shape, mybir.dt.from_np(v.dtype), kind="ExternalInput").ap()
            for n, v in arrays.items()]
    args.append(nc.dram_tensor("out_0", (NTOK, D), F32, kind="ExternalOutput").ap())
    build_decoder(nc, *args)
    r = run_bass_kernel_spmd(nc, [arrays], core_ids=[0])
    return np.asarray(r.results[0]["out_0"]).reshape(B, T, D)
```
